# Optimizing a Trainium2 kernel written in Bass

```python
import numpy as np
import jax
import jax.numpy as jnp

def _softmax(x, axis=-1):
    return jax.nn.softmax(x, axis=axis)

def _gelu(x):
    return jax.nn.gelu(x, approximate=True)

def _silu(x):
    return jax.nn.silu(x)

def _sigmoid(x):
    return jax.nn.sigmoid(x)

def _layernorm(x, axis=-1, eps=1e-05):
    m = jnp.mean(x, axis=axis, keepdims=True)
    v = jnp.var(x, axis=axis, keepdims=True)
    return (x - m) / jnp.sqrt(v + eps)

def _scatter_add(tgt, idx, src, axis=0):
    return tgt.at[idx].add(src)

def _segment_sum(src, seg, n):
    return jax.ops.segment_sum(src, seg, n)
kernel_name = 'mk_prb_d2_jaxref_r4_fbbee7'

def setup_inputs(seed: int=0):
    np.random.seed(seed)
    _w = jnp.asarray

    def _L0_attn_setup():
        import jax, jax.numpy as jnp
        import numpy as np
        from jax import lax
        B, T, D, H, K = (8, 512, 256, 16, 64)
        LAYER_ID, N_LAYERS = (6, 12)
        key = jax.random.key(seed)
        ks = jax.random.split(key, 12)
        r01 = LAYER_ID / max(N_LAYERS - 1, 1)
        r10 = 1.0 - LAYER_ID / N_LAYERS
        ddd = (np.arange(D) / D).astype(np.float32)
        conv_w = np.zeros((D, 1, 3), np.float32)
        conv_w[:, 0, 0] = 0.5
        conv_w[:, 0, 2] = 0.5
        decay_speed = (-6.0 + 5.0 * (np.arange(D) / (D - 1)) ** (0.7 + 1.3 * r01)).astype(np.float32)
        u = lambda k, s: jax.random.uniform(k, s, jnp.float32, -0.01, 0.01)
        n = lambda k, s: jax.random.normal(k, s, jnp.float32) / np.sqrt(D)
        return {'x': jax.random.normal(ks[0], (B, T, D), jnp.float32), 'conv_w': jnp.asarray(conv_w), 'maa_x': jnp.asarray(1.0 - ddd ** r10), 'maa_w': jnp.asarray(1.0 - ddd ** r10), 'maa_k': jnp.asarray(1.0 - ddd ** r10), 'maa_v': jnp.asarray(1.0 - (ddd ** r10 + 0.3 * r01)), 'maa_r': jnp.asarray(1.0 - ddd ** (0.5 * r10)), 'maa_g': jnp.asarray(1.0 - ddd ** (0.5 * r10)), 'maa_w1': u(ks[1], (D, 32 * 5)), 'maa_w2': u(ks[2], (5, 32, D)), 'time_decay': jnp.asarray(decay_speed), 'decay_w1': u(ks[3], (D, 64)), 'decay_w2': u(ks[4], (64, D)), 'Wr': n(ks[5], (D, D)), 'Wk': n(ks[6], (D, D)), 'Wv': n(ks[7], (D, D)), 'Wg': n(ks[8], (D, D)), 'Wo': n(ks[9], (D, D)), 'ln_w': jnp.ones((D,), jnp.float32), 'ln_b': jnp.zeros((D,), jnp.float32), 'gate_w': u(ks[10], (D, D)), 'gate_b': 3.0 * jnp.ones((D,), jnp.float32)}
    _L0_attn_in = _L0_attn_setup()

    def _L0_ffn_setup():
        import jax, jax.numpy as jnp
        import numpy as np
        TOP_K = 2
        key = jax.random.key(seed)
        ks = jax.random.split(key, 5)
        B, S, D, H, E = (2, 512, 256, 704, 8)
        x = jax.random.normal(ks[0], (B, S, D), dtype=jnp.float32)
        Wg = jax.random.normal(ks[1], (E, D), dtype=jnp.float32) * 0.02
        W1 = jax.random.normal(ks[2], (E, H, D), dtype=jnp.float32) * 0.02
        W2 = jax.random.normal(ks[3], (E, H, D), dtype=jnp.float32) * 0.02
        W3 = jax.random.normal(ks[4], (E, D, H), dtype=jnp.float32) * 0.02
        return {'x': x, 'Wg': Wg, 'W1': W1, 'W2': W2, 'W3': W3}
    _L0_ffn_in = _L0_ffn_setup()

    def _L1_attn_setup():
        import jax, jax.numpy as jnp
        import numpy as np
        D = 256
        H = 16
        KVH = 4
        HD = D // H
        LAT = 64
        WIN = 64
        B, S = (1, 512)
        BASE_G, BASE_L = (1000000.0, 10000.0)
        EPS = 1e-06

        def rmsnorm(x, w):
            return x * jax.lax.rsqrt(jnp.mean(x * x, axis=-1, keepdims=True) + EPS) * w

        def qk_norm(x):
            return x * jax.lax.rsqrt(jnp.mean(x * x, axis=-1, keepdims=True) + EPS)

        def rope(x, base):
            s, hd = (x.shape[-2], x.shape[-1])
            inv_freq = 1.0 / base ** (jnp.arange(0, hd, 2, dtype=jnp.float32) / hd)
            freqs = jnp.arange(s, dtype=jnp.float32)[:, None] * inv_freq[None, :]
            cos, sin = (jnp.cos(freqs), jnp.sin(freqs))
            xe, xo = (x[..., ::2], x[..., 1::2])
            out = jnp.stack([xe * cos - xo * sin, xe * sin + xo * cos], axis=-1)
            return out.reshape(x.shape)

        def split_heads(x, n_heads):
            b, s, _ = x.shape
            return x.reshape(b, s, n_heads, HD).transpose(0, 2, 1, 3)

        def repeat_kv(x):
            return jnp.repeat(x, H // KVH, axis=1)

        def sdpa(q, k, v, mask):
            scores = jnp.einsum('bhqd,bhkd->bhqk', q, k) / np.sqrt(HD).astype(np.float32)
            scores = jnp.where(mask, scores, jnp.float32(-1e+30))
            probs = jax.nn.softmax(scores, axis=-1)
            return jnp.einsum('bhqk,bhkd->bhqd', probs, v)

        def merge_heads(x):
            b, h, s, hd = x.shape
            return x.transpose(0, 2, 1, 3).reshape(b, s, h * hd)

        def global_latent_attn(x, wq, w_kv_down, w_k_up, w_v_up, wo):
            q = split_heads(x @ wq, H)
            latent = x @ w_kv_down
            k = split_heads(latent @ w_k_up, KVH)
            v = split_heads(latent @ w_v_up, KVH)
            q, k = (rope(q, BASE_G), rope(k, BASE_G))
            q, k = (qk_norm(q), qk_norm(k))
            k, v = (repeat_kv(k), repeat_kv(v))
            i = jnp.arange(x.shape[1])
            causal = i[:, None] >= i[None, :]
            return merge_heads(sdpa(q, k, v, causal)) @ wo

        def local_gqa_attn(x, wq, wk, wv, wo):
            q = split_heads(x @ wq, H)
            k = split_heads(x @ wk, KVH)
            v = split_heads(x @ wv, KVH)
            q, k = (rope(q, BASE_L), rope(k, BASE_L))
            q, k = (qk_norm(q), qk_norm(k))
            k, v = (repeat_kv(k), repeat_kv(v))
            i = jnp.arange(x.shape[1])
            diff = i[:, None] - i[None, :]
            mask = (diff >= 0) & (diff < WIN)
            return merge_heads(sdpa(q, k, v, mask)) @ wo
        key = jax.random.key(seed)
        ks = jax.random.split(key, 12)
        std = 0.02
        return {'hidden': jax.random.normal(ks[0], (B, S, D), dtype=jnp.float32), 'norm1_w': jnp.ones((D,), jnp.float32), 'norm2_w': jnp.ones((D,), jnp.float32), 'g_wq': jax.random.normal(ks[1], (D, H * HD), jnp.float32) * std, 'g_kv_down': jax.random.normal(ks[2], (D, LAT), jnp.float32) * std, 'g_k_up': jax.random.normal(ks[3], (LAT, KVH * HD), jnp.float32) * std, 'g_v_up': jax.random.normal(ks[4], (LAT, KVH * HD), jnp.float32) * std, 'g_wo': jax.random.normal(ks[5], (D, D), jnp.float32) * std, 'l_wq': jax.random.normal(ks[6], (D, H * HD), jnp.float32) * std, 'l_wk': jax.random.normal(ks[7], (D, KVH * HD), jnp.float32) * std, 'l_wv': jax.random.normal(ks[8], (D, KVH * HD), jnp.float32) * std, 'l_wo': jax.random.normal(ks[9], (D, D), jnp.float32) * std}
    _L1_attn_in = _L1_attn_setup()

    def _L1_ffn_setup():
        import jax, jax.numpy as jnp
        import numpy as np
        E = 16
        G = 4
        EPG = E // G
        K = 4
        TOPK_GROUP = 2
        PER_GROUP_K = K // TOPK_GROUP

        def _route(xf, router_w, correction_bias):
            S = xf.shape[0]
            logits = xf @ router_w.T
            scores = jax.nn.sigmoid(logits)
            sb = scores + correction_bias
            grp_top = jax.lax.top_k(sb.reshape(S, G, EPG), PER_GROUP_K)[0]
            group_scores = grp_top.sum(axis=-1)
            _, group_idx = jax.lax.top_k(group_scores, TOPK_GROUP)
            group_mask = jnp.zeros((S, G), sb.dtype).at[jnp.arange(S)[:, None], group_idx].set(1.0)
            score_mask = jnp.broadcast_to(group_mask[:, :, None], (S, G, EPG)).reshape(S, E)
            masked = jnp.where(score_mask > 0, sb, -jnp.inf)
            _, topk_idx = jax.lax.top_k(masked, K)
            w = jnp.take_along_axis(scores, topk_idx, axis=1)
            w = w / (w.sum(axis=-1, keepdims=True) + 1e-20)
            return (topk_idx, w, scores)
        key = jax.random.key(seed)
        ks = jax.random.split(key, 9)
        B, T, C, H, HS = (2, 256, 256, 64, 512)
        std = 0.02
        return {'x': jax.random.normal(ks[0], (B, T, C), jnp.float32), 'router_w': jax.random.normal(ks[1], (E, C), jnp.float32) * std, 'correction_bias': jnp.zeros((E,), jnp.float32), 'gate_w': jax.random.normal(ks[2], (E, C, H), jnp.float32) * std, 'up_w': jax.random.normal(ks[3], (E, C, H), jnp.float32) * std, 'down_w': jax.random.normal(ks[4], (E, H, C), jnp.float32) * std, 'shared_gate_w': jax.random.normal(ks[5], (HS, C), jnp.float32) * std, 'shared_up_w': jax.random.normal(ks[6], (HS, C), jnp.float32) * std, 'shared_down_w': jax.random.normal(ks[7], (C, HS), jnp.float32) * std}
    _L1_ffn_in = _L1_ffn_setup()
    _d = {'L0_attn_x': _L0_attn_in['x'], 'L0_attn_conv_w': _L0_attn_in['conv_w'], 'L0_attn_maa_x': _L0_attn_in['maa_x'], 'L0_attn_maa_w': _L0_attn_in['maa_w'], 'L0_attn_maa_k': _L0_attn_in['maa_k'], 'L0_attn_maa_v': _L0_attn_in['maa_v'], 'L0_attn_maa_r': _L0_attn_in['maa_r'], 'L0_attn_maa_g': _L0_attn_in['maa_g'], 'L0_attn_maa_w1': _L0_attn_in['maa_w1'], 'L0_attn_maa_w2': _L0_attn_in['maa_w2'], 'L0_attn_time_decay': _L0_attn_in['time_decay'], 'L0_attn_decay_w1': _L0_attn_in['decay_w1'], 'L0_attn_decay_w2': _L0_attn_in['decay_w2'], 'L0_attn_Wr': _L0_attn_in['Wr'], 'L0_attn_Wk': _L0_attn_in['Wk'], 'L0_attn_Wv': _L0_attn_in['Wv'], 'L0_attn_Wg': _L0_attn_in['Wg'], 'L0_attn_Wo': _L0_attn_in['Wo'], 'L0_attn_ln_w': _L0_attn_in['ln_w'], 'L0_attn_ln_b': _L0_attn_in['ln_b'], 'L0_attn_gate_w': _L0_attn_in['gate_w'], 'L0_attn_gate_b': _L0_attn_in['gate_b'], 'L0_ffn_Wg': _L0_ffn_in['Wg'], 'L0_ffn_W1': _L0_ffn_in['W1'], 'L0_ffn_W2': _L0_ffn_in['W2'], 'L0_ffn_W3': _L0_ffn_in['W3'], 'L1_attn_norm1_w': _L1_attn_in['norm1_w'], 'L1_attn_norm2_w': _L1_attn_in['norm2_w'], 'L1_attn_g_wq': _L1_attn_in['g_wq'], 'L1_attn_g_kv_down': _L1_attn_in['g_kv_down'], 'L1_attn_g_k_up': _L1_attn_in['g_k_up'], 'L1_attn_g_v_up': _L1_attn_in['g_v_up'], 'L1_attn_g_wo': _L1_attn_in['g_wo'], 'L1_attn_l_wq': _L1_attn_in['l_wq'], 'L1_attn_l_wk': _L1_attn_in['l_wk'], 'L1_attn_l_wv': _L1_attn_in['l_wv'], 'L1_attn_l_wo': _L1_attn_in['l_wo'], 'L1_ffn_router_w': _L1_ffn_in['router_w'], 'L1_ffn_correction_bias': _L1_ffn_in['correction_bias'], 'L1_ffn_gate_w': _L1_ffn_in['gate_w'], 'L1_ffn_up_w': _L1_ffn_in['up_w'], 'L1_ffn_down_w': _L1_ffn_in['down_w'], 'L1_ffn_shared_gate_w': _L1_ffn_in['shared_gate_w'], 'L1_ffn_shared_up_w': _L1_ffn_in['shared_up_w'], 'L1_ffn_shared_down_w': _L1_ffn_in['shared_down_w']}
    _x0 = _d['L0_attn_x']
    _d['L0_attn_x'] = jax.random.normal(jax.random.fold_in(jax.random.key(seed), 1), (8, 512, 256), dtype=_x0.dtype)
    del _x0
    return _d

def reference(L0_attn_x, L0_attn_conv_w, L0_attn_maa_x, L0_attn_maa_w, L0_attn_maa_k, L0_attn_maa_v, L0_attn_maa_r, L0_attn_maa_g, L0_attn_maa_w1, L0_attn_maa_w2, L0_attn_time_decay, L0_attn_decay_w1, L0_attn_decay_w2, L0_attn_Wr, L0_attn_Wk, L0_attn_Wv, L0_attn_Wg, L0_attn_Wo, L0_attn_ln_w, L0_attn_ln_b, L0_attn_gate_w, L0_attn_gate_b, L0_ffn_Wg, L0_ffn_W1, L0_ffn_W2, L0_ffn_W3, L1_attn_norm1_w, L1_attn_norm2_w, L1_attn_g_wq, L1_attn_g_kv_down, L1_attn_g_k_up, L1_attn_g_v_up, L1_attn_g_wo, L1_attn_l_wq, L1_attn_l_wk, L1_attn_l_wv, L1_attn_l_wo, L1_ffn_router_w, L1_ffn_correction_bias, L1_ffn_gate_w, L1_ffn_up_w, L1_ffn_down_w, L1_ffn_shared_gate_w, L1_ffn_shared_up_w, L1_ffn_shared_down_w):

    def _L0_attn_ref(x, conv_w, maa_x, maa_w, maa_k, maa_v, maa_r, maa_g, maa_w1, maa_w2, time_decay, decay_w1, decay_w2, Wr, Wk, Wv, Wg, Wo, ln_w, ln_b, gate_w, gate_b):
        import jax, jax.numpy as jnp
        import numpy as np
        from jax import lax
        B, T, D, H, K = (8, 512, 256, 16, 64)
        LAYER_ID, N_LAYERS = (6, 12)
        B, T, D = x.shape
        H = 16
        K = D // H
        xc = lax.conv_general_dilated(x.transpose(0, 2, 1), conv_w, window_strides=(1,), padding=((1, 1),), feature_group_count=D, dimension_numbers=('NCH', 'OIH', 'NCH')).transpose(0, 2, 1)
        dx = xc - x
        xxx = x + dx * maa_x
        t5 = jnp.tanh(xxx @ maa_w1).reshape(B, T, 5, 32)
        m = jnp.einsum('btfc,fcd->fbtd', t5, maa_w2)
        xw = x + dx * (maa_w + m[0])
        xk = x + dx * (maa_k + m[1])
        xv = x + dx * (maa_v + m[2])
        xr = x + dx * (maa_r + m[3])
        xg = x + dx * (maa_g + m[4])
        r = xr @ Wr
        k = xk @ Wk
        v = xv @ Wv
        g = jax.nn.silu(xg @ Wg)
        w = time_decay + jnp.tanh(xw @ decay_w1) @ decay_w2
        w_log = -jnp.exp(w)
        to_h = lambda a: a.reshape(B, T, H, K).transpose(1, 0, 2, 3)
        r_h, k_h, v_h, wd = (to_h(r), to_h(k), to_h(v), to_h(w_log))
        S0 = jnp.zeros((B, H, K, K), x.dtype)

        def fwd_step(S, inp):
            rt, kt, vt, wt = inp
            S = jnp.exp(wt)[..., None] * S + kt[..., None] * vt[..., None, :]
            return (S, jnp.einsum('bhk,bhkv->bhv', rt, S))
        _, y_f = lax.scan(fwd_step, S0, (r_h, k_h, v_h, wd))

        def bwd_step(S, inp):
            rt, kt, vt, wt = inp
            y = jnp.einsum('bhk,bhkv->bhv', rt, S)
            S = jnp.exp(wt)[..., None] * (S + kt[..., None] * vt[..., None, :])
            return (S, y)
        _, y_b = lax.scan(bwd_step, S0, (r_h, k_h, v_h, wd), reverse=True)
        y = (y_f + y_b).transpose(1, 0, 2, 3).reshape(B, T, D)
        y = y * jax.nn.sigmoid(dx @ gate_w + gate_b)
        eps = 1e-05 * 8.0 ** 2
        yg = y.reshape(B, T, H, K)
        mu = yg.mean(-1, keepdims=True)
        var = yg.var(-1, keepdims=True)
        yn = ((yg - mu) / jnp.sqrt(var + eps)).reshape(B, T, D) * ln_w + ln_b
        return yn * g @ Wo

    def _L0_ffn_ref(x, Wg, W1, W2, W3):
        import jax, jax.numpy as jnp
        import numpy as np
        TOP_K = 2
        B, S, D = x.shape
        E = Wg.shape[0]
        xt = x.reshape(B * S, D)
        scores = xt @ Wg.T
        topk_scores, topk_idx = jax.lax.top_k(scores, TOP_K)
        gate = jax.nn.silu(jnp.einsum('td,ehd->teh', xt, W1))
        up = jnp.einsum('td,ehd->teh', xt, W2)
        y = jnp.einsum('teh,edh->ted', gate * up, W3)
        onehot = jax.nn.one_hot(topk_idx, E, dtype=x.dtype)
        w = jnp.einsum('tke,tk->te', onehot, topk_scores)
        out = jnp.einsum('te,ted->td', w, y)
        return out.reshape(B, S, D)

    def _L1_attn_ref(hidden, norm1_w, norm2_w, g_wq, g_kv_down, g_k_up, g_v_up, g_wo, l_wq, l_wk, l_wv, l_wo):
        import jax, jax.numpy as jnp
        import numpy as np
        D = 256
        H = 16
        KVH = 4
        HD = D // H
        LAT = 64
        WIN = 64
        B, S = (1, 512)
        BASE_G, BASE_L = (1000000.0, 10000.0)
        EPS = 1e-06

        def rmsnorm(x, w):
            return x * jax.lax.rsqrt(jnp.mean(x * x, axis=-1, keepdims=True) + EPS) * w

        def qk_norm(x):
            return x * jax.lax.rsqrt(jnp.mean(x * x, axis=-1, keepdims=True) + EPS)

        def rope(x, base):
            s, hd = (x.shape[-2], x.shape[-1])
            inv_freq = 1.0 / base ** (jnp.arange(0, hd, 2, dtype=jnp.float32) / hd)
            freqs = jnp.arange(s, dtype=jnp.float32)[:, None] * inv_freq[None, :]
            cos, sin = (jnp.cos(freqs), jnp.sin(freqs))
            xe, xo = (x[..., ::2], x[..., 1::2])
            out = jnp.stack([xe * cos - xo * sin, xe * sin + xo * cos], axis=-1)
            return out.reshape(x.shape)

        def split_heads(x, n_heads):
            b, s, _ = x.shape
            return x.reshape(b, s, n_heads, HD).transpose(0, 2, 1, 3)

        def repeat_kv(x):
            return jnp.repeat(x, H // KVH, axis=1)

        def sdpa(q, k, v, mask):
            scores = jnp.einsum('bhqd,bhkd->bhqk', q, k) / np.sqrt(HD).astype(np.float32)
            scores = jnp.where(mask, scores, jnp.float32(-1e+30))
            probs = jax.nn.softmax(scores, axis=-1)
            return jnp.einsum('bhqk,bhkd->bhqd', probs, v)

        def merge_heads(x):
            b, h, s, hd = x.shape
            return x.transpose(0, 2, 1, 3).reshape(b, s, h * hd)

        def global_latent_attn(x, wq, w_kv_down, w_k_up, w_v_up, wo):
            q = split_heads(x @ wq, H)
            latent = x @ w_kv_down
            k = split_heads(latent @ w_k_up, KVH)
            v = split_heads(latent @ w_v_up, KVH)
            q, k = (rope(q, BASE_G), rope(k, BASE_G))
            q, k = (qk_norm(q), qk_norm(k))
            k, v = (repeat_kv(k), repeat_kv(v))
            i = jnp.arange(x.shape[1])
            causal = i[:, None] >= i[None, :]
            return merge_heads(sdpa(q, k, v, causal)) @ wo

        def local_gqa_attn(x, wq, wk, wv, wo):
            q = split_heads(x @ wq, H)
            k = split_heads(x @ wk, KVH)
            v = split_heads(x @ wv, KVH)
            q, k = (rope(q, BASE_L), rope(k, BASE_L))
            q, k = (qk_norm(q), qk_norm(k))
            k, v = (repeat_kv(k), repeat_kv(v))
            i = jnp.arange(x.shape[1])
            diff = i[:, None] - i[None, :]
            mask = (diff >= 0) & (diff < WIN)
            return merge_heads(sdpa(q, k, v, mask)) @ wo
        x = hidden
        x = x + global_latent_attn(rmsnorm(x, norm1_w), g_wq, g_kv_down, g_k_up, g_v_up, g_wo)
        x = x + local_gqa_attn(rmsnorm(x, norm2_w), l_wq, l_wk, l_wv, l_wo)
        return x

    def _L1_ffn_ref(x, router_w, correction_bias, gate_w, up_w, down_w, shared_gate_w, shared_up_w, shared_down_w):
        import jax, jax.numpy as jnp
        import numpy as np
        E = 16
        G = 4
        EPG = E // G
        K = 4
        TOPK_GROUP = 2
        PER_GROUP_K = K // TOPK_GROUP

        def _route(xf, router_w, correction_bias):
            S = xf.shape[0]
            logits = xf @ router_w.T
            scores = jax.nn.sigmoid(logits)
            sb = scores + correction_bias
            grp_top = jax.lax.top_k(sb.reshape(S, G, EPG), PER_GROUP_K)[0]
            group_scores = grp_top.sum(axis=-1)
            _, group_idx = jax.lax.top_k(group_scores, TOPK_GROUP)
            group_mask = jnp.zeros((S, G), sb.dtype).at[jnp.arange(S)[:, None], group_idx].set(1.0)
            score_mask = jnp.broadcast_to(group_mask[:, :, None], (S, G, EPG)).reshape(S, E)
            masked = jnp.where(score_mask > 0, sb, -jnp.inf)
            _, topk_idx = jax.lax.top_k(masked, K)
            w = jnp.take_along_axis(scores, topk_idx, axis=1)
            w = w / (w.sum(axis=-1, keepdims=True) + 1e-20)
            return (topk_idx, w, scores)
        B, T, C = x.shape
        S = B * T
        xf = x.reshape(S, C)
        sg = xf @ shared_gate_w.T
        su = xf @ shared_up_w.T
        shared_out = jax.nn.silu(sg) * su @ shared_down_w.T
        topk_idx, w, _scores = _route(xf, router_w, correction_bias)
        combine = jnp.zeros((S, E), xf.dtype).at[jnp.arange(S)[:, None], topk_idx].add(w)
        g = jnp.einsum('sc,ech->esh', xf, gate_w)
        u = jnp.einsum('sc,ech->esh', xf, up_w)
        h = jax.nn.silu(g) * u
        hw = h * combine.T[:, :, None]
        routed = jnp.einsum('esh,ehc->sc', hw, down_w)
        return (shared_out + routed).reshape(B, T, C)
    x = L0_attn_x
    xn = _layernorm(x, axis=-1)
    x = x + _L0_attn_ref(xn, L0_attn_conv_w, L0_attn_maa_x, L0_attn_maa_w, L0_attn_maa_k, L0_attn_maa_v, L0_attn_maa_r, L0_attn_maa_g, L0_attn_maa_w1, L0_attn_maa_w2, L0_attn_time_decay, L0_attn_decay_w1, L0_attn_decay_w2, L0_attn_Wr, L0_attn_Wk, L0_attn_Wv, L0_attn_Wg, L0_attn_Wo, L0_attn_ln_w, L0_attn_ln_b, L0_attn_gate_w, L0_attn_gate_b) + _L0_ffn_ref(xn, L0_ffn_Wg, L0_ffn_W1, L0_ffn_W2, L0_ffn_W3)
    xn = _layernorm(x, axis=-1)
    x = x + _L1_attn_ref(xn, L1_attn_norm1_w, L1_attn_norm2_w, L1_attn_g_wq, L1_attn_g_kv_down, L1_attn_g_k_up, L1_attn_g_v_up, L1_attn_g_wo, L1_attn_l_wq, L1_attn_l_wk, L1_attn_l_wv, L1_attn_l_wo) + _L1_ffn_ref(xn, L1_ffn_router_w, L1_ffn_correction_bias, L1_ffn_gate_w, L1_ffn_up_w, L1_ffn_down_w, L1_ffn_shared_gate_w, L1_ffn_shared_up_w, L1_ffn_shared_down_w)
    return x

_drawn_inputs = setup_inputs


def setup_inputs(seed=0):
    import zlib

    import numpy as np

    out = dict(_drawn_inputs(seed))
    spreads = {'L0_attn_ln_w': (1.0, 0.2),
     'L0_attn_ln_b': (0.0, 0.1),
     'L0_attn_gate_b': (3.0, 0.6),
     'L1_attn_norm1_w': (1.0, 0.6),
     'L1_attn_norm2_w': (1.0, 0.6),
     'L1_ffn_correction_bias': (0.0, 0.8)}
    factors = {'L0_attn_maa_x': 8.0,
     'L0_attn_maa_w': 8.0,
     'L0_attn_maa_w1': 8.0,
     'L0_attn_maa_w2': 8.0,
     'L0_attn_decay_w1': 8.0,
     'L0_attn_decay_w2': 8.0,
     'L0_attn_gate_w': 8.0,
     'L0_ffn_Wg': 3.943,
     'L0_ffn_W1': 3.502,
     'L0_ffn_W2': 3.461,
     'L0_ffn_W3': 3.475,
     'L1_attn_g_wq': 8.0,
     'L1_attn_g_kv_down': 8.0,
     'L1_attn_g_k_up': 8.0,
     'L1_attn_g_v_up': 8.0,
     'L1_attn_g_wo': 8.0,
     'L1_attn_l_wq': 7.283,
     'L1_attn_l_wk': 7.278,
     'L1_attn_l_wv': 5.189,
     'L1_attn_l_wo': 5.225,
     'L1_ffn_router_w': 8.0,
     'L1_ffn_gate_w': 8.0,
     'L1_ffn_up_w': 8.0,
     'L1_ffn_down_w': 8.0,
     'L1_ffn_shared_gate_w': 5.049,
     'L1_ffn_shared_up_w': 4.99,
     'L1_ffn_shared_down_w': 5.001}
    for name, (base, spread) in spreads.items():
        noise = np.random.default_rng([zlib.crc32(name.encode()), seed]).standard_normal(out[name].shape)
        drawn = base * np.exp(spread * noise) if base else spread * noise
        out[name] = jnp.asarray(drawn.astype(out[name].dtype))
    for name, factor in factors.items():
        out[name] = (out[name] * factor).astype(out[name].dtype)
    return out
```

```python
from contextlib import ExitStack

import concourse.bass as bass
from concourse import mybir

F32 = mybir.dt.float32
BF16 = mybir.dt.bfloat16
ALU = mybir.AluOpType
ACT = mybir.ActivationFunctionType
AX = mybir.AxisListType.X

P = 128
NB, T, D = 8, 512, 256
C2 = D // P
TT = T // P
H, K = 16, 16
E0, H0 = 8, 704
HT0 = (H0 + P - 1) // P
E1, H1, HS = 16, 64, 512
MT1 = (E1 * H1 + HS) // P
RT1 = E1 * H1 // P
KVH = 4
G4 = 4
LAT = 64


class Steps:

    def __init__(self, engine, semaphore, per_round):
        self.engine, self.semaphore, self.per_round, self.done = engine, semaphore, per_round, 0
        self.base = 0

    def round(self, number):
        self.base, self.done = number * self.per_round, 0

    def add(self, instruction):
        instruction.then_inc(self.semaphore, 1)
        self.done += 1

    def settle(self):
        self.engine.wait_ge(self.semaphore, self.base + self.done)

    def end(self):
        assert self.done == self.per_round, (self.semaphore, self.done)


def at(number, per_round, n):
    return number * per_round + max(n, 0)


def build(nc, a, out):
    ctx = ExitStack()
    with ctx:
        scratch = {n: nc.dram_tensor("scratch_" + n, shape, F32, kind="Internal").ap() for n, shape in
                   (("rkw", [3, NB * D, T]), ("v", [NB * D, T]), ("gate", [NB * D, T]), ("g", [NB * D, T]),
                    ("y", [NB * D, T]), ("ffn", [P, NB * TT, D]))}
        keep = {"ident": ctx.enter_context(nc.sbuf_tensor("ident", [P, P], F32))}
        with ExitStack() as first:
            keep["xnT"] = first.enter_context(nc.sbuf_tensor("xnT", [P, C2, NB * T], F32))
            keep["w0"] = first.enter_context(nc.sbuf_tensor("route0", [P, NB * TT, E0], F32))
            project(nc, a, scratch, keep)
            scan_and_experts(nc, a, scratch, keep)
        layer_one(nc, a, scratch, keep, out)


def project(nc, a, scratch, keep):
    with ExitStack() as ctx:
        def sb(name, shape, dt=F32):
            return ctx.enter_context(nc.sbuf_tensor("b1_" + name, shape, dt))

        def sem(name):
            return ctx.enter_context(nc.semaphore("b1_" + name))

        bank = [ctx.enter_context(nc.psum_tensor(f"b1_bank{n}", [P, 512], F32)) for n in range(8)]
        xnT, ident = keep["xnT"], keep["ident"]
        x_tok = sb("x_tok", [P, 2, TT, D])
        xn_tok = sb("xn_tok", [P, 2, TT, D])
        stats = sb("stats", [P, 2, TT, 6])
        mv = sb("mv", [P, 2, TT, 2])
        std = sb("std", [P, 2, TT])
        rstd = sb("rstd", [P, 2, TT])
        eps = sb("eps", [P, 1])
        holds_wait = sb("holds_wait", [P, 1])
        pool_wait = sb("pool_wait", [P, 5])
        dx = sb("dx", [P, C2, NB * T])
        xxx = sb("xxx", [P, 2, C2, T])
        t5 = sb("t5", [P, 2, NB * T])
        vecs = sb("vecs", [P, 10, C2])
        td = sb("time_decay", [P, C2])
        maa_w1 = sb("maa_w1", [P, C2, 160])
        mix_w = sb("mix_w", [P, 5, D])
        proj_w = sb("proj_w", [P, 5, C2, D])
        dec_w1 = sb("dec_w1", [P, C2, P])
        dec_w2 = sb("dec_w2", [P, D])
        tmp = sb("tmp", [P, 2, C2, T])
        xf = sb("xf", [P, 2, C2, T])
        tw = sb("tw", [P, T])
        ew = sb("ew", [P, 2, T])
        stage = sb("stage", [P, 6, C2, T])

        weights_in, zeroed = sem("weights_in"), sem("zeroed")
        x_in = [sem(f"x_in{u}") for u in range(2)]
        vec_ready, var_ready, std_ready = sem("vec_ready"), sem("var_ready"), sem("std_ready")
        xn_made = [sem(f"xn_made{u}") for u in range(2)]
        xT_ps = sem("xT_ps")
        xT_out = [sem(f"xT_out{u}") for u in range(2)]
        xxx_made = [sem(f"xxx_made{u}") for u in range(2)]
        t5_ps = sem("t5_ps")
        t5_out = [sem(f"t5_out{u}") for u in range(2)]
        own1 = sem("dve_own1")
        m_ps, m_used, xf_made = sem("m_ps"), sem("m_used"), sem("xf_made")
        unit_ps, unit_out, act_own = sem("unit_ps"), sem("unit_out"), sem("act_own")
        staged = [sem(f"staged{n}") for n in range(6)]

        WEIGHT_LOADS = 16
        UNITS = [("gate", 0), ("gate", 1), ("tw", 0), ("k", 0), ("k", 1), ("v", 0), ("v", 1), ("r", 0), ("r", 1),
                 ("decay", 0), ("decay", 1), ("g", 0), ("g", 1)]
        NU = len(UNITS)
        UB = 5
        SLOT = {"gate": 0, "k": 1, "v": 2, "r": 3, "decay": 4, "g": 5}
        USED = [3, 5, 7, 9, 13]

        block = ctx.enter_context(nc.Block())

        @block.sync
        def _(sp):
            for dst, src in ((ident[:], a["c_ident"]), (vecs[:], a["c_vecs"]), (maa_w1[:], a["maa_w1"]),
                             (proj_w[:, 0], a["gate_w"]), (proj_w[:, 1], a["Wk"]), (proj_w[:, 2], a["Wv"]),
                             (proj_w[:, 3], a["Wr"]), (proj_w[:, 4], a["Wg"]), (td[:], a["time_decay"])):
                sp.dma_start(dst, src).then_inc(weights_in, 16)
            sp.wait_ge(zeroed, 4)
            for f in range(4):
                sp.dma_start(mix_w[32 * f:32 * f + 32, f, :], a["maa_w2"][f]).then_inc(weights_in, 16)
            sp.dma_start(mix_w[0:32, 4, :], a["maa_w2"][4]).then_inc(weights_in, 16)
            sp.dma_start(dec_w1[:, :, 0:64], a["decay_w1"]).then_inc(weights_in, 16)
            sp.dma_start(dec_w2[0:64, :], a["decay_w2"]).then_inc(weights_in, 16)
            with sp.Fori(0, NB // 2) as i:
                for u in range(2):
                    sp.wait_ge(xn_made[u], TT * i)
                    sp.dma_start(x_tok[:, u], a["x"][2 * i + u]).then_inc(x_in[u], 16)
            outs = [(0, scratch["gate"], 2), (1, scratch["rkw"][1], 5), (2, scratch["v"], 7),
                    (3, scratch["rkw"][0], 9), (4, scratch["rkw"][2], 11), (5, scratch["g"], 13)]
            with sp.Fori(0, NB) as b:
                for n, dram, units in outs:
                    sp.wait_ge(unit_out, b * NU + units)
                    dst = dram.rearrange("(b c p) t -> b p c t", c=C2, p=P)[b]
                    sp.dma_start(dst, stage[:, n]).then_inc(staged[n], 16)
            for n in range(6):
                sp.wait_ge(staged[n], 16 * NB)

        @block.gpsimd
        def _(pool):
            pool.memset(mix_w[:], 0.0).then_inc(zeroed, 1)
            pool.memset(dec_w1[:], 0.0).then_inc(zeroed, 1)
            pool.memset(dec_w2[:], 0.0).then_inc(zeroed, 1)
            pool.memset(t5[:, 1, :], 0.0).then_inc(zeroed, 1)
            pool.memset(eps[:], 1e-5).then_inc(zeroed, 1)
            with pool.Fori(0, NB) as b:
                for f in range(5):
                    pool.wait_ge(m_used, b * 10 + 2 * f + 2)
                    pool.wait_ge(unit_ps, at(b, NU, USED[f - 2] if f >= 2 else 0))
                    pool.tensor_tensor(pool_wait[:, f:f + 1], eps[:], eps[:], ALU.add)
                    for c in range(C2):
                        pool.tensor_tensor(xf[:, f % 2, c], tmp[:, f % 2, c], xnT[:, c, bass.ds(b * T, T)],
                                           ALU.add).then_inc(xf_made, 1)

        @block.vector
        def _(dve):
            own = Steps(dve, own1, 32)
            dve.wait_ge(weights_in, 16 * WEIGHT_LOADS)
            dve.tensor_scalar(vecs[:, 1, :], vecs[:, 1, :], -1.0, None, ALU.add).then_inc(vec_ready, 1)
            dve.tensor_scalar(vecs[:, 9, :], vecs[:, 9, :], 0.5, None, ALU.mult).then_inc(vec_ready, 1)
            dve.wait_ge(vec_ready, 2)
            with dve.Fori(0, NB // 2) as i:
                own.round(i)
                for u in range(2):
                    dve.wait_ge(x_in[u], 16 * i + 16)
                    for t in range(TT):
                        own.add(dve.bn_stats(stats[:, u, t], x_tok[:, u, t]))
                    own.settle()
                    own.add(dve.memset(holds_wait[:, 0:1], 0.0))
                    for t in range(TT):
                        ins = dve.bn_aggr(mv[:, u, t], stats[:, u, t])
                        if t < TT - 1:
                            own.add(ins)
                    ins.then_inc(var_ready, 1)
                for u in range(2):
                    dve.wait_ge(std_ready, 2 * i + u + 1)
                    dve.wait_ge(xT_out[u], 2 * i)
                    own.add(dve.reciprocal(rstd[:, u], std[:, u]))
                    own.settle()
                    for t in range(TT):
                        ins = dve.tensor_scalar(xn_tok[:, u, t], x_tok[:, u, t], mv[:, u, t, 0:1],
                                                rstd[:, u, t:t + 1], ALU.subtract, ALU.mult)
                        ins.then_inc(xn_made[u], 1)
                for u in range(2):
                    dve.wait_ge(xT_out[u], 2 * i + 2)
                    x = [xnT[:, c, bass.ds((2 * i + u) * T, T)] for c in range(C2)]
                    x_head = [xnT[:, c, bass.ds((2 * i + u) * T, T - 1)] for c in range(C2)]
                    x_tail = [xnT[:, c, bass.ds((2 * i + u) * T + 1, T - 1)] for c in range(C2)]
                    d = [dx[:, c, bass.ds((2 * i + u) * T, T)] for c in range(C2)]
                    d_head = [dx[:, c, bass.ds((2 * i + u) * T, T - 1)] for c in range(C2)]
                    d_tail = [dx[:, c, bass.ds((2 * i + u) * T + 1, T - 1)] for c in range(C2)]
                    for c in range(C2):
                        own.add(dve.tensor_scalar(d[c], x[c], vecs[:, 1, c:c + 1], None, ALU.mult))
                    own.settle()
                    for c in range(C2):
                        own.add(dve.scalar_tensor_tensor(d_tail[c], x_head[c], vecs[:, 0, c:c + 1], d_tail[c],
                                                         ALU.mult, ALU.add))
                    own.settle()
                    for c in range(C2):
                        own.add(dve.scalar_tensor_tensor(d_head[c], x_tail[c], vecs[:, 2, c:c + 1], d_head[c],
                                                         ALU.mult, ALU.add))
                    own.settle()
                    dve.wait_ge(t5_out[u], 2 * i)
                    for c in range(C2):
                        ins = dve.scalar_tensor_tensor(xxx[:, u, c], d[c], vecs[:, 3, c:c + 1], x[c],
                                                       ALU.mult, ALU.add)
                        if c == 0:
                            own.add(ins)
                    ins.then_inc(xxx_made[u], 1)
                own.end()
            with dve.Fori(0, NB) as b:
                for f in range(5):
                    for c in range(C2):
                        dve.wait_ge(m_ps, b * 10 + 2 * f + c + 1)
                        dve.wait_ge(xf_made, at(b, 10, 2 * (f - 2) + c + 1))
                        dve.scalar_tensor_tensor(tmp[:, f % 2, c], bank[(2 * f + c) % 2][:], vecs[:, 4 + f, c:c + 1],
                                                 dx[:, c, bass.ds(b * T, T)], ALU.add, ALU.mult).then_inc(m_used, 1)

        @block.scalar
        def _(act):
            act.wait_ge(zeroed, 5)
            with act.Fori(0, NB // 2) as i:
                for u in range(2):
                    act.wait_ge(var_ready, 2 * i + u + 1)
                    act.activation(std[:, u], mv[:, u, :, 1], ACT.Sqrt, bias=eps[:]).then_inc(std_ready, 1)
                for u in range(2):
                    for c in range(C2):
                        act.wait_ge(xT_ps, 4 * i + 2 * u + c + 1)
                        act.activation(xnT[:, c, bass.ds((2 * i + u) * T, T)], bank[2 * u + c][:], ACT.Copy)\
                           .then_inc(xT_out[u], 1)
                for u in range(2):
                    act.wait_ge(t5_ps, 2 * i + u + 1)
                    act.activation(t5[:, 0, bass.ds((2 * i + u) * T, T)], bank[4 + 2 * u][:], ACT.Tanh)\
                       .then_inc(t5_out[u], 1)
                    act.activation(t5[0:32, 1, bass.ds((2 * i + u) * T, T)], bank[5 + 2 * u][0:32, :], ACT.Tanh)\
                       .then_inc(t5_out[u], 1)
            act.wait_ge(vec_ready, 2)
            with act.Fori(0, NB) as b:
                for n, (what, c) in enumerate(UNITS):
                    act.wait_ge(unit_ps, b * NU + n + 1)
                    ps = bank[2 + n % UB][:]
                    if what in SLOT and c == 0:
                        act.wait_ge(staged[SLOT[what]], 16 * b)
                    if what == "gate":
                        ins = act.activation(stage[:, 0, c], ps, ACT.Tanh, bias=vecs[:, 9, c:c + 1], scale=0.5)
                    elif what == "tw":
                        ins = act.activation(tw[:], ps, ACT.Tanh)
                    elif what == "decay":
                        act.activation(ew[:, c], ps, ACT.Exp, bias=td[:, c:c + 1]).then_inc(act_own, 1)
                        act.wait_ge(act_own, 2 * b + c + 1)
                        ins = act.activation(stage[:, 4, c], ew[:, c], ACT.Exp, scale=-1.0)
                    elif what == "g":
                        ins = act.activation(stage[:, 5, c], ps, ACT.Silu)
                    else:
                        ins = act.activation(stage[:, SLOT[what], c], ps, ACT.Copy)
                    ins.then_inc(unit_out, 1)

        @block.tensor
        def _(pe):
            pe.wait_ge(weights_in, 16 * WEIGHT_LOADS)
            pe.wait_ge(zeroed, 5)
            with pe.Fori(0, NB // 2) as i:
                for u in range(2):
                    pe.wait_ge(xT_out[u], 2 * i)
                    for c in range(C2):
                        for t in range(TT):
                            if c == 0:
                                pe.wait_ge(xn_made[u], TT * i + t + 1)
                            ins = pe.transpose(bank[2 * u + c][:, t * P:(t + 1) * P],
                                               xn_tok[:, u, t, c * P:(c + 1) * P], ident[:])
                        ins.then_inc(xT_ps, 1)
                for u in range(2):
                    pe.wait_ge(xxx_made[u], i + 1)
                    pe.wait_ge(t5_out[u], 2 * i)
                    for n, (lo, hi) in enumerate(((0, P), (P, 160))):
                        for c in range(C2):
                            ins = pe.matmul(bank[4 + 2 * u + n][0:hi - lo, :], maa_w1[:, c, lo:hi], xxx[:, u, c],
                                            start=c == 0, stop=c == C2 - 1)
                    ins.then_inc(t5_ps, 1)
            for u in range(2):
                pe.wait_ge(xT_out[u], 2 * (NB // 2))
                pe.wait_ge(t5_out[u], 2 * (NB // 2))

            with pe.Fori(0, NB) as b:
                def mix(f):
                    for c in range(C2):
                        pe.wait_ge(m_used, at(b, 10, 2 * f + c - 1))
                        pe.matmul(bank[(2 * f + c) % 2][:], mix_w[:, f, c * P:(c + 1) * P],
                                  t5[:, f // 4, bass.ds(b * T, T)], start=True, stop=True).then_inc(m_ps, 1)

                def unit(n):
                    what, o = UNITS[n]
                    pe.wait_ge(unit_out, at(b, NU, n - UB + 1))
                    cols = slice(o * P, (o + 1) * P)
                    ps = bank[2 + n % UB][:]
                    if what == "gate":
                        for c in range(C2):
                            ins = pe.matmul(ps, proj_w[:, 0, c, cols], dx[:, c, bass.ds(b * T, T)],
                                            start=c == 0, stop=c == C2 - 1)
                    elif what == "tw":
                        pe.wait_ge(xf_made, b * 10 + 2)
                        for c in range(C2):
                            ins = pe.matmul(ps, dec_w1[:, c, :], xf[:, 0, c], start=c == 0, stop=c == C2 - 1)
                    elif what == "decay":
                        pe.wait_ge(unit_out, b * NU + 3)
                        ins = pe.matmul(ps, dec_w2[:, cols], tw[:], start=True, stop=True)
                    else:
                        f = {"k": 1, "v": 2, "r": 3, "g": 4}[what]
                        pe.wait_ge(xf_made, b * 10 + 2 * f + 2)
                        for c in range(C2):
                            ins = pe.matmul(ps, proj_w[:, f, c, cols], xf[:, f % 2, c],
                                            start=c == 0, stop=c == C2 - 1)
                    ins.then_inc(unit_ps, 1)

                mix(0)
                mix(1)
                unit(0)
                unit(1)
                unit(2)
                mix(2)
                unit(3)
                unit(4)
                mix(3)
                unit(5)
                unit(6)
                mix(4)
                for n in range(7, NU):
                    unit(n)


def scan_and_experts(nc, a, scratch, keep):
    with ExitStack() as ctx:
        def sb(name, shape, dt=F32):
            return ctx.enter_context(nc.sbuf_tensor("b2_" + name, shape, dt))

        def sem(name):
            return ctx.enter_context(nc.semaphore("b2_" + name))

        bank = [ctx.enter_context(nc.psum_tensor(f"b2_bank{n}", [P, 512], F32)) for n in range(8)]
        xnT, w0 = keep["xnT"], keep["w0"]
        VH, VQ = 8, 4
        KR = K // 4
        NCH = 4 * VH // VQ
        assert NCH == NB and 2 * KR == E0
        ffn = sb("ffn", [P, NB * TT, D])
        w_up = sb("w_up", [P, 2, C2, H0])
        w_down = sb("w_down", [P, HT0, D])
        hid = sb("hid", [P, 2, HT0, T])
        silu = sb("silu", [P, 2, T])
        rkw = sb("rkw", [P, 2, 3, T])
        v = sb("v", [P, VH, T])
        y = sb("y", [P, VH, T])
        kv = sb("kv", [P, 2, VQ, T])
        fwd = sb("fwd", [P, VQ, T])
        bwd = sb("bwd", [P, VQ, T])

        route_w = sb("route_w", [P, C2, E0])
        before = sb("before", [P, E0 * E0])
        sc = sb("sc", [P, NB * TT, E0])
        rank = sb("rank", [P, NB * TT, E0])
        more = kv[:, 0].rearrange("p q t -> p (q t)")
        same = kv[:, 1].rearrange("p q t -> p (q t)")

        up_in, down_in = sem("up_in"), sem("down_in")
        route_in, route_ps, route_own = sem("route_in"), sem("route_ps"), sem("route_own")
        v_in, y_stored, ffn_stored = sem("v_in"), sem("y_stored"), sem("ffn_stored")
        rkw_in = [sem(f"rkw_in{n}") for n in range(2)]
        cleared = sem("cleared")
        kv_made, summed, y_done = sem("kv_made"), sem("summed"), sem("y_done")
        scanned = [sem(f"scanned{n}") for n in range(2)]
        y_added = [sem(f"y_added{n}") for n in range(2)]
        up_ps, silu_made, hid_made, down_ps, combined = (sem(n) for n in
                                                         ("up_ps", "silu_made", "hid_made", "down_ps", "combined"))
        NHID = NB * HT0
        NY = NB * TT
        rows = [P] * (HT0 - 1) + [H0 - P * (HT0 - 1)]
        view = "(p k) t -> p k t"
        rkw_rows = scratch["rkw"].rearrange("n (p k) t -> k p n t", k=K)
        v_rows = scratch["v"].rearrange(view, k=K)
        y_rows = scratch["y"].rearrange(view, k=K)

        block = ctx.enter_context(nc.Block())

        @block.sync
        def _(sp):
            sp.dma_start(route_w[:], a["ffn_Wg"]).then_inc(route_in, 16)
            sp.dma_start(before[:], a["c_before8"]).then_inc(route_in, 16)
            for half in range(2):
                if half:
                    sp.wait_ge(kv_made, KR * NCH)
                sp.dma_start(v[:], v_rows[:, half * VH:(half + 1) * VH, :]).then_inc(v_in, 16)
                with sp.Fori(0, KR) as i:
                    rnd = half * KR + i
                    sp.wait_ge(up_ps, rnd * NHID)
                    sp.dma_start(w_up[:], a["ffn_up"][rnd]).then_inc(up_in, 16)
                    sp.wait_ge(down_ps, rnd * NY)
                    sp.dma_start(w_down[:, 0:HT0 - 1], a["ffn_down"][rnd, 0:P * (HT0 - 1)]
                                 .rearrange("(m p) n -> p m n", p=P)).then_inc(down_in, 16)
                    sp.dma_start(w_down[0:rows[-1], HT0 - 1], a["ffn_down"][rnd, P * (HT0 - 1):H0])\
                      .then_inc(down_in, 16)

        @block.gpsimd
        def _(pool):
            pool.memset(bwd[:], 0.0).then_inc(cleared, 1)
            for half in range(2):
                if half:
                    pool.wait_ge(y_stored, 16)
                pool.memset(y[:], 0.0).then_inc(cleared, 1)
                if not half:
                    pool.memset(ffn[:], 0.0).then_inc(cleared, 1)
                pool.wait_ge(v_in, 16 * half + 16)
                if not half:
                    pool.wait_ge(route_own, 7)
                with pool.Fori(0, KR) as i:
                    rnd = half * KR + i
                    for s in range(4):
                        pool.wait_ge(y_added[s % 2], 4 * rnd + 2 * (s // 2))
                        pool.dma_start(rkw[:, s % 2], rkw_rows[4 * i + s]).then_inc(rkw_in[s % 2], 16)
                        pool.wait_ge(rkw_in[s % 2], 32 * rnd + 16 * (s // 2) + 16)
                        for q in range(VH // VQ):
                            n = 2 * s + q
                            pool.wait_ge(scanned[n % 2], VQ * NCH * rnd + 2 * VQ * (n // 2))
                            key = rkw[:, s % 2, 1, :].rearrange("p (o t) -> p o t", o=1).broadcast_to([P, VQ, T])
                            pool.tensor_tensor(kv[:, n % 2], key, v[:, q * VQ:(q + 1) * VQ, :], ALU.mult)\
                                .then_inc(kv_made, 1)

        @block.vector
        def _(dve):
            dve.wait_ge(route_in, 32)
            dve.wait_ge(route_ps, 1)
            n_rows = NB * TT
            own = Steps(dve, route_own, 7)
            own.add(dve.tensor_copy(sc[:], bank[7][:, 0:n_rows * E0].rearrange("p (t e) -> p t e", e=E0)))
            own.settle()
            others = sc[:].rearrange("p t (o e) -> p t o e", o=1).broadcast_to([P, n_rows, E0, E0])
            itself = sc[:].rearrange("p t (e o) -> p t e o", o=1).broadcast_to([P, n_rows, E0, E0])
            square = "p (t e j) -> p t e j"
            own.add(dve.tensor_tensor(more.rearrange(square, e=E0, j=E0), others, itself, ALU.is_gt))
            own.add(dve.tensor_tensor(same.rearrange(square, e=E0, j=E0), others, itself, ALU.is_equal))
            own.settle()
            same_rows = same.rearrange("p (t n) -> p t n", n=E0 * E0)
            own.add(dve.tensor_tensor(same_rows, same_rows, before[:].rearrange("p (o n) -> p o n", o=1)
                                      .broadcast_to([P, n_rows, E0 * E0]), ALU.mult))
            own.settle()
            own.add(dve.tensor_tensor(more, more, same, ALU.add))
            own.settle()
            own.add(dve.reduce_sum(rank[:], more.rearrange("p (n j) -> p n j", j=E0), AX))
            own.settle()
            own.add(dve.scalar_tensor_tensor(w0[:], rank[:], 2.0, sc[:], ALU.is_lt, ALU.mult))
            own.settle()
            dve.wait_ge(cleared, 3)
            for half in range(2):
                dve.wait_ge(cleared, 3 + half)
                with dve.Fori(0, KR) as i:
                    rnd = half * KR + i

                    def hidden(tb, m):
                        n = tb * HT0 + m
                        dve.wait_ge(silu_made, rnd * NHID + n + 1)
                        dve.wait_ge(down_ps, at(rnd, NY, (tb - 1) * TT))
                        r = rows[m]
                        dve.tensor_tensor(hid[0:r, tb % 2, m, :], silu[0:r, n % 2, :], bank[3 + n % 3][0:r, :],
                                          ALU.mult).then_inc(hid_made, 1)

                    def scan(n, step):
                        s, q = n // 2, n % 2
                        k_row = rkw[:, s % 2]
                        if step < VQ:
                            if step == 0:
                                dve.wait_ge(kv_made, rnd * NCH + n + 1)
                                if q:
                                    dve.wait_ge(y_added[s % 2], 4 * rnd + 2 * (s // 2) + 1)
                                elif s:
                                    dve.wait_ge(y_added[(s - 1) % 2], 4 * rnd + 2 * ((s - 1) // 2) + 2)
                                else:
                                    dve.wait_ge(y_added[1], 4 * rnd)
                            dve.tensor_tensor_scan(fwd[:, step, :], k_row[:, 2, :], kv[:, n % 2, step, :], 0.0,
                                                   ALU.mult, ALU.add).then_inc(scanned[n % 2], 1)
                            dve.tensor_tensor_scan(bwd[:, step, T - 2::-1], kv[:, n % 2, step, T - 1:0:-1],
                                                   k_row[:, 2, T - 1:0:-1], 0.0, ALU.add, ALU.mult)\
                               .then_inc(scanned[n % 2], 1)
                        elif step == VQ:
                            dve.wait_ge(scanned[n % 2], VQ * NCH * rnd + 2 * VQ * (n // 2) + 2 * VQ)
                            dve.tensor_tensor(fwd[:], fwd[:], bwd[:], ALU.add).then_inc(summed, 1)
                            dve.wait_ge(summed, 2 * (rnd * NCH + n) + 1)
                            rr = k_row[:, 0, :].rearrange("p (o t) -> p o t", o=1).broadcast_to([P, VQ, T])
                            dve.tensor_tensor(fwd[:], fwd[:], rr, ALU.mult).then_inc(summed, 1)
                        else:
                            dve.wait_ge(summed, 2 * (rnd * NCH + n) + 2)
                            part = y[:, q * VQ:(q + 1) * VQ, :]
                            dve.tensor_tensor(part, part, fwd[:], ALU.add).then_inc(y_added[s % 2], 1)

                    def combine(tb):
                        for t in range(TT):
                            n = tb * TT + t
                            dve.wait_ge(down_ps, rnd * NY + n + 1)
                            dve.wait_ge(combined, rnd * NY)
                            row = ffn[:, n, :]
                            dve.scalar_tensor_tensor(row, bank[6 + n % 2][:, 0:D], w0[:, n, bass.ds(rnd, 1)], row,
                                                     ALU.mult, ALU.add).then_inc(combined, 1)

                    for tb in range(NB):
                        for m in range(HT0):
                            hidden(tb, m)
                            scan(tb, m)
                        if tb:
                            combine(tb - 1)
                    combine(NB - 1)
                for slot in range(2):
                    dve.wait_ge(y_added[slot], (half + 1) * KR * 4)
                dve.nop().then_inc(y_done, 1)

        @block.scalar
        def _(act):
            for half in range(2):
                with act.Fori(0, KR) as i:
                    rnd = half * KR + i
                    for n in range(NHID):
                        r = rows[n % HT0]
                        act.wait_ge(up_ps, rnd * NHID + n + 1)
                        act.wait_ge(hid_made, at(rnd, NHID, n - 1))
                        act.activation(silu[0:r, n % 2, :], bank[n % 3][0:r, :], ACT.Silu).then_inc(silu_made, 1)
                act.wait_ge(y_done, half + 1)
                act.dma_start(y_rows[:, half * VH:(half + 1) * VH, :], y[:]).then_inc(y_stored, 16)
            act.wait_ge(combined, E0 * NY)
            act.dma_start(scratch["ffn"], ffn[:]).then_inc(ffn_stored, 16)
            act.wait_ge(ffn_stored, 16)
            act.wait_ge(y_stored, 32)

        @block.tensor
        def _(pe):
            pe.wait_ge(route_in, 32)
            for t in range(NB * TT):
                for c in range(C2):
                    ins = pe.matmul(bank[7][:, t * E0:(t + 1) * E0], xnT[:, c, t * P:(t + 1) * P],
                                    route_w[:, c], start=c == 0, stop=c == C2 - 1)
            ins.then_inc(route_ps, 1)
            pe.wait_ge(route_own, 1)
            with pe.Fori(0, E0) as e:
                def up(tb):
                    for m in range(HT0):
                        n = tb * HT0 + m
                        r = rows[m]
                        pe.wait_ge(hid_made, at(e, NHID, n - 2))
                        for j in range(2):
                            for c in range(C2):
                                ins = pe.matmul(bank[3 * j + n % 3][0:r, :], w_up[:, j, c, m * P:m * P + r],
                                                xnT[:, c, tb * T:(tb + 1) * T], start=c == 0, stop=c == C2 - 1)
                        ins.then_inc(up_ps, 1)

                def down(tb):
                    pe.wait_ge(hid_made, e * NHID + (tb + 1) * HT0)
                    for t in range(TT):
                        n = tb * TT + t
                        pe.wait_ge(combined, at(e, NY, n - 1))
                        for m in range(HT0):
                            r = rows[m]
                            ins = pe.matmul(bank[6 + n % 2][:, 0:D], hid[0:r, tb % 2, m, t * P:(t + 1) * P],
                                            w_down[0:r, m, :], start=m == 0, stop=m == HT0 - 1)
                        ins.then_inc(down_ps, 1)

                pe.wait_ge(up_in, 16 * e + 16)
                for tb in range(NB):
                    up(tb)
                    if tb == 1:
                        pe.wait_ge(down_in, 32 * e + 32)
                    if tb:
                        down(tb - 1)
                down(NB - 1)


def layer_one(nc, a, scratch, keep, out):
    with ExitStack() as ctx:
        def sb(name, shape, dt=F32):
            return ctx.enter_context(nc.sbuf_tensor("b3_" + name, shape, dt))

        def sem(name):
            return ctx.enter_context(nc.semaphore("b3_" + name))

        bank = [ctx.enter_context(nc.psum_tensor(f"b3_bank{n}", [P, 512], F32)) for n in range(8)]
        ident = keep["ident"]
        NH = H * TT
        QK, QKV = 320, 384
        identb = sb("identb", [P, P], BF16)
        causal = sb("causal", [P, P], BF16)
        window = sb("window", [P, P + 64], BF16)
        rope = sb("rope", [P, 2, 2, TT, QK])
        slot_of = sb("slot_of", [P, 8])
        eps = sb("eps", [P, 3])
        sel = sb("sel", [48, RT1, P], BF16)
        before16 = sb("before16", [P, E1 * E1])
        before4 = sb("before4", [P, G4 * G4])
        bias_r = sb("bias_r", [P, E1])
        ln_wb = sb("ln_wb", [P, 2, C2])
        norm_w = sb("norm_w", [P, 2, C2])
        wo0 = sb("rwkv_wo", [P, C2, D])
        wq = [sb(f"wq{n}", [P, C2, QKV if n else D]) for n in range(2)]
        wd = sb("wd", [P, C2, LAT])
        kv_up = sb("kv_up", [LAT, P])
        wo = [sb(f"attn_wo{n}", [P, C2, D]) for n in range(2)]
        route_w = sb("route_w", [P, C2, E1])
        up_w = sb("up_w", [P, 2, C2, MT1 * P])
        down_w = sb("down_w", [P, MT1, D])
        y_in_sb = sb("y", [P, C2, T])
        gate = sb("gate", [P, C2, T])
        g = sb("g", [P, C2, T])
        x_tok = sb("x_tok", [P, TT, D])
        f_tok = sb("f_tok", [P, TT, D])
        w1 = sb("w1", [P, TT * QK])
        w2 = sb("w2", [P, TT * QK])
        qk = sb("qk", [P, TT, QKV])
        small = sb("small", [P, 5, TT * 20])
        yl = sb("yl", [P, C2, T])
        x1 = sb("x1", [P, TT, D])
        stats = sb("stats", [P, TT, 6])
        mv = sb("mv", [P, TT, 2])
        std = sb("std", [P, TT])
        rstd = sb("rstd", [P, TT])
        xn = sb("xn", [P, TT, D])
        holds_wait = sb("holds_wait", [P, 3])
        xT = sb("xT", [P, C2, T])
        arena = sb("arena", [P, 2 * 8 * T])
        silu = sb("silu", [P, 2, T])
        prod = sb("prod", [P, 2, T])
        sq = sb("sq", [P, D])
        ss = sb("ss", [P, 2, TT])
        rms_std = sb("rms_std", [P, TT])
        rs = sb("rs", [P, TT])
        lat = sb("lat", [LAT, T])
        qkv = sb("qkv", [P, TT, QKV])
        qT = sb("qT", [P, C2, T])
        kT = sb("kT", [P, T])
        v1 = sb("v1", [P, TT, KVH, 32])
        oT = sb("oT", [P, 2, T])
        o_tok = sb("o_tok", [P, TT, D])
        den = sb("den", [P, 4, NH // 4])
        onT = sb("onT", [P, C2, T])
        xb = sb("xb", [P, TT, D])
        fin = sb("fin", [P, TT, D])
        sc = sb("sc", [P, TT, E1])
        sbias = sb("sbias", [P, TT, E1])
        rk = sb("rk", [P, 4, TT * E1])
        cbp = sb("cbp", [P, TT, 3, E1], BF16)
        crest = sb("crest", [P, TT, E1])
        cbT = sb("cbT", [48, T], BF16)

        hid = arena[:, 0:MT1 * T].rearrange("p (m t) -> p m t", t=T)
        kz = arena[:, 0:8 * T].rearrange("p (m t) -> p m t", t=T)
        prob = arena[:, 8 * T:16 * T].rearrange("p (s h t) -> p s h t", s=2, t=T)
        yt = w1[:, 0:TT * D].rearrange("p (n d) -> p n d", d=K)
        ysq = w2[:, 0:TT * D].rearrange("p (n d) -> p n d", d=K)
        ya = qk[:, :, :].rearrange("p t n -> p (t n)")[:, 0:C2 * T].rearrange("p (c t) -> p c t", t=T)
        rope_a = w1[:, :]
        rope_b = w2[:, :]
        more = w1[:, 0:TT * E1 * E1].rearrange("p (t e j) -> p t e j", t=TT, j=E1)
        same = w2[:, 0:TT * E1 * E1].rearrange("p (t e j) -> p t e j", t=TT, j=E1)

        names = ("weights_in", "setup", "ones_made", "y_in", "gate_in", "g_in", "x_in", "f_in", "ya_made", "yT_ps", "yt_out",
                 "gn_var", "gn_std", "yn_made", "ynT_ps", "yl_made", "ag_made", "wo_ps", "xr_made", "x1_made",
                 "ln_var", "ln_std", "xn_made", "xT_ps", "xT_out", "route_ps", "sc_out", "cb_made", "cbT_ps",
                 "cbT_out", "up_ps", "silu_made", "prod_made", "cb_ps", "hid_made", "fy_ps", "fy_used",
                 "ss_made", "rms_made", "rs_made", "lat_ps", "lat_out", "qkv_ps", "qkv_out", "qn_sum", "qn_std",
                 "qk_made", "v_made", "qkT_ps", "qkT_out", "kz_made", "score_ps", "exp_out", "pv_ps", "oT_out",
                 "ot_ps", "o_made", "onT_ps", "onT_out", "ao_ps", "xb_made", "acc_made", "fin_made", "stored")
        s = {n: sem(n) for n in names}
        own_sem, aown_sem = sem("dve_own"), sem("act_own")

        ORDER = list(range(RT1, MT1)) + list(range(RT1))
        groups = []
        for layer in range(2):
            for j in range(4):
                for i in range(TT):
                    width = T - P * i if layer == 0 else min(P + 64, T - P * i)
                    per = max(1, 512 // width)
                    per = 4 if per >= 4 else 2 if per >= 2 else 1
                    for g0 in range(0, KVH, per):
                        groups.append((layer, j, i, list(range(g0, g0 + per)), P * i, width))
        NG = len(groups)

        def groups_until(layer, j, i):
            return sum(1 for x in groups if x[:3] <= (layer, j, i))

        block = ctx.enter_context(nc.Block())

        loads = [(identb[:], "c_identb"), (causal[:], "c_causal"), (window[:], "c_window"), (rope[:], "c_rope"),
                 (slot_of[:], "c_slot"), (eps[:], "c_eps"), (sel[:], "c_sel"), (before16[:], "c_before16"),
                 (before4[:], "c_before4"), (bias_r[:], "bias_r"), (ln_wb[:], "ln_wb"), (norm_w[:], "norm_w"),
                 (wo0[:], "Wo"), (wq[0][:], "g_wq"), (wq[1][:], "l_wqkv"), (wd[:], "g_kv_down"),
                 (kv_up[:], "g_kv_up"), (wo[0][:], "g_wo"), (wo[1][:], "l_wo"), (route_w[:], "router_w"),
                 (up_w[:], "ffn1_up"), (down_w[:], "ffn1_down")]
        SETUP = 3 * C2

        @block.sync
        def _(sp):
            for dst, name in loads:
                sp.dma_start(dst, a[name]).then_inc(s["weights_in"], 16)
            chan = "(b c p) t -> b p c t"
            with sp.Fori(0, NB) as b:
                sp.wait_ge(s["ya_made"], 2 * b)
                sp.dma_start(y_in_sb[:], scratch["y"].rearrange(chan, c=C2, p=P)[b]).then_inc(s["y_in"], 16)
                sp.dma_start(gate[:], scratch["gate"].rearrange(chan, c=C2, p=P)[b]).then_inc(s["gate_in"], 16)
                sp.wait_ge(s["ag_made"], 2 * b)
                sp.dma_start(g[:], scratch["g"].rearrange(chan, c=C2, p=P)[b]).then_inc(s["g_in"], 16)
                sp.wait_ge(s["x1_made"], 2 * b)
                sp.dma_start(x_tok[:], a["x"][b]).then_inc(s["x_in"], 16)
                sp.dma_start(f_tok[:], scratch["ffn"][:, bass.ds(b * TT, TT), :]).then_inc(s["f_in"], 16)
                sp.wait_ge(s["fin_made"], 2 * b + 2)
                sp.dma_start(out[b], fin[:]).then_inc(s["stored"], 16)
            sp.wait_ge(s["stored"], 16 * NB)

        @block.gpsimd
        def _(pool):
            pool.wait_ge(s["weights_in"], 16 * len(loads))
            pool.memset(v1[:], 1.0).then_inc(s["ones_made"], 1)
            pool.wait_ge(s["ones_made"], 1)
            with pool.Fori(0, NB) as b:
                pool.wait_ge(s["x_in"], 16 * b + 16)
                pool.wait_ge(s["f_in"], 16 * b + 16)
                pool.tensor_tensor(x_tok[:], x_tok[:], f_tok[:], ALU.add).then_inc(s["xr_made"], 1)
                pool.wait_ge(s["g_in"], 16 * b + 16)
                for c in range(C2):
                    pool.wait_ge(s["yl_made"], 2 * b + c + 1)
                    pool.tensor_tensor(yl[:, c], yl[:, c], g[:, c], ALU.mult).then_inc(s["ag_made"], 1)
                for layer in range(2):
                    pool.wait_ge(s["qkv_out"], 8 * b + 4 * layer + 4)
                    pool.wait_ge(s["pv_ps"], 32 * b + 16 * layer)
                    pool.tensor_tensor(holds_wait[:, 1 + layer:2 + layer], eps[:, 0:1], eps[:, 0:1], ALU.add)
                    pool.tensor_copy(v1[:, :, :, 0:K],
                                     qkv[:, :, QK:QKV].rearrange("p t (g d) -> p t g d", d=K))\
                        .then_inc(s["v_made"], 1)
                    if layer == 0:
                        pool.wait_ge(s["xb_made"], 2 * b + 2)
                        pool.wait_ge(s["fy_used"], 2 * b + 2)
                        pool.tensor_tensor(x1[:], x1[:], xb[:], ALU.add).then_inc(s["acc_made"], 1)

        @block.vector
        def _(dve):
            dve.wait_ge(s["weights_in"], 16 * len(loads))
            for c in range(C2):
                for w, layer in ((wq[0], 0), (wd, 0), (wq[1], 1)):
                    dve.tensor_scalar(w[:, c], w[:, c], norm_w[:, layer, c:c + 1], None, ALU.mult)\
                       .then_inc(s["setup"], 1)
            own = Steps(dve, own_sem, 100)
            with dve.Fori(0, NB) as b:
                own.round(b)
                dve.wait_ge(s["y_in"], 16 * b + 16)
                dve.wait_ge(s["gate_in"], 16 * b + 16)
                dve.wait_ge(s["qkT_ps"], 6 * b)
                own.settle()
                for c in range(C2):
                    dve.scalar_tensor_tensor(ya[:, c], gate[:, c], 1.0, y_in_sb[:, c], ALU.add, ALU.mult)\
                       .then_inc(s["ya_made"], 1)
                dve.wait_ge(s["yt_out"], 2 * b + 2)
                mean, var, gstd, grstd = (small[:, n, 0:NH] for n in range(4))
                own.add(dve.reduce_sum(mean, yt, AX))
                own.settle()
                own.add(dve.tensor_scalar(mean, mean, 1.0 / K, None, ALU.mult))
                own.settle()
                each = "p (n o) -> p n o"
                own.add(dve.tensor_tensor(yt, yt, mean.rearrange(each, o=1).broadcast_to([P, NH, K]), ALU.subtract))
                own.settle()
                own.add(dve.tensor_tensor(ysq, yt, yt, ALU.mult))
                own.settle()
                dve.reduce_sum(var, ysq, AX).then_inc(s["gn_var"], 1)
                dve.wait_ge(s["gn_std"], b + 1)
                own.add(dve.reciprocal(grstd, gstd))
                own.settle()
                dve.tensor_tensor(yt, yt, grstd.rearrange(each, o=1).broadcast_to([P, NH, K]), ALU.mult)\
                   .then_inc(s["yn_made"], 1)
                dve.wait_ge(s["xr_made"], b + 1)
                for h in range(2):
                    dve.wait_ge(s["wo_ps"], 4 * b + 2 * h + 2)
                    dve.tensor_tensor(x1[:, 2 * h:2 * h + 2], bank[4 + h][:].rearrange("p (t n) -> p t n", n=D),
                                      x_tok[:, 2 * h:2 * h + 2], ALU.add).then_inc(s["x1_made"], 1)
                dve.wait_ge(s["x1_made"], 2 * b + 2)
                for t in range(TT):
                    own.add(dve.bn_stats(stats[:, t], x1[:, t]))
                own.settle()
                own.add(dve.memset(holds_wait[:, 0:1], 0.0))
                for t in range(TT):
                    ins = dve.bn_aggr(mv[:, t], stats[:, t])
                    if t < TT - 1:
                        own.add(ins)
                ins.then_inc(s["ln_var"], 1)
                dve.wait_ge(s["ln_std"], b + 1)
                own.add(dve.reciprocal(rstd[:], std[:]))
                own.settle()
                for t in range(TT):
                    dve.tensor_scalar(xn[:, t], x1[:, t], mv[:, t, 0:1], rstd[:, t:t + 1], ALU.subtract, ALU.mult)\
                       .then_inc(s["xn_made"], 1)

                def rank_in(dst, scores, n, table, op_rows):
                    oth = scores.rearrange("p m (o e) -> p m o e", o=1).broadcast_to([P, op_rows, n, n])
                    its = scores.rearrange("p m (e o) -> p m e o", o=1).broadcast_to([P, op_rows, n, n])
                    size = op_rows * n * n
                    gt, eq = w1[:, 0:size], w2[:, 0:size]
                    four = dict(m=op_rows, e=n, j=n)
                    own.add(dve.tensor_tensor(gt.rearrange("p (m e j) -> p m e j", **four), oth, its, ALU.is_gt))
                    own.add(dve.tensor_tensor(eq.rearrange("p (m e j) -> p m e j", **four), oth, its, ALU.is_equal))
                    own.settle()
                    rows = eq.rearrange("p (m n) -> p m n", n=n * n)
                    own.add(dve.tensor_tensor(rows, rows, table.rearrange("p (o n) -> p o n", o=1)
                                              .broadcast_to([P, op_rows, n * n]), ALU.mult))
                    own.settle()
                    own.add(dve.tensor_tensor(gt, gt, eq, ALU.add))
                    own.settle()
                    own.add(dve.reduce_sum(dst, gt.rearrange("p (n j) -> p n j", j=n), AX))
                    own.settle()

                dve.wait_ge(s["sc_out"], b + 1)
                dve.wait_ge(s["cbT_ps"], b)
                own.add(dve.tensor_tensor(sbias[:], sc[:], bias_r[:].rearrange("p (o e) -> p o e", o=1)
                                          .broadcast_to([P, TT, E1]), ALU.add))
                own.settle()
                NGR = TT * G4
                flat = sbias[:].rearrange("p t e -> p (t e)")
                in_groups = flat.rearrange("p (m e) -> p m e", e=E1 // G4)
                rank_in(rk[:, 0, :], in_groups, E1 // G4, before4[:], NGR)
                own.add(dve.scalar_tensor_tensor(rk[:, 1, :], rk[:, 0, :], 2.0, flat, ALU.is_lt, ALU.mult))
                own.settle()
                gsum = small[:, 0, 0:NGR]
                grank = small[:, 1, 0:NGR]
                gmask = small[:, 2, 0:NGR]
                gless = small[:, 3, 0:NGR]
                own.add(dve.reduce_sum(gsum, rk[:, 1, :].rearrange("p (m e) -> p m e", e=E1 // G4), AX))
                own.settle()
                rank_in(grank, gsum.rearrange("p (t m) -> p t m", m=G4), G4, before4[:], TT)
                own.add(dve.tensor_scalar(gmask, grank, 2.0, None, ALU.is_lt))
                own.settle()
                own.add(dve.tensor_scalar(gless, gmask, 1e30, -1e30, ALU.mult, ALU.add))
                spread = dict(o=1)
                own.add(dve.tensor_tensor(rk[:, 2, :].rearrange("p (m e) -> p m e", e=E1 // G4), in_groups,
                                          gmask.rearrange("p (m o) -> p m o", **spread)
                                          .broadcast_to([P, NGR, E1 // G4]), ALU.mult))
                own.settle()
                own.add(dve.tensor_tensor(rk[:, 3, :].rearrange("p (m e) -> p m e", e=E1 // G4),
                                          rk[:, 2, :].rearrange("p (m e) -> p m e", e=E1 // G4),
                                          gless.rearrange("p (m o) -> p m o", **spread)
                                          .broadcast_to([P, NGR, E1 // G4]), ALU.add))
                own.settle()
                rank_in(rk[:, 0, :], rk[:, 3, :].rearrange("p (t e) -> p t e", e=E1), E1, before16[:], TT)
                own.add(dve.scalar_tensor_tensor(rk[:, 1, :], rk[:, 0, :], 4.0,
                                                 sc[:].rearrange("p t e -> p (t e)"), ALU.is_lt, ALU.mult))
                own.settle()
                total = small[:, 4, 0:TT]
                own.add(dve.reduce_sum(total, rk[:, 1, :].rearrange("p (t e) -> p t e", e=E1), AX))
                own.settle()
                own.add(dve.tensor_scalar(total, total, 1e-20, None, ALU.add))
                own.settle()
                own.add(dve.reciprocal(small[:, 4, TT:2 * TT], total))
                own.settle()
                weight = rk[:, 2, :].rearrange("p (t e) -> p t e", e=E1)
                own.add(dve.tensor_tensor(weight, rk[:, 1, :].rearrange("p (t e) -> p t e", e=E1),
                                          small[:, 4, TT:2 * TT].rearrange("p (t o) -> p t o", o=1)
                                          .broadcast_to([P, TT, E1]), ALU.mult))
                own.settle()
                own.add(dve.tensor_copy(cbp[:, :, 0, :], weight))
                own.settle()
                own.add(dve.tensor_tensor(crest[:], weight, cbp[:, :, 0, :], ALU.subtract))
                own.settle()
                own.add(dve.tensor_copy(cbp[:, :, 1, :], crest[:]))
                own.settle()
                dve.tensor_tensor(cbp[:, :, 2, :], crest[:], cbp[:, :, 1, :], ALU.subtract).then_inc(s["cb_made"], 1)

                for n, m in enumerate(ORDER):
                    dve.wait_ge(s["silu_made"], b * MT1 + n + 1)
                    if m >= RT1:
                        ins = dve.tensor_tensor(hid[:, m], silu[:, n % 2], bank[2 + n % 2][:], ALU.mult)
                        ins.then_inc(s["prod_made"], 1)
                    else:
                        dve.tensor_tensor(prod[:, n % 2], silu[:, n % 2], bank[2 + n % 2][:], ALU.mult)\
                           .then_inc(s["prod_made"], 1)
                        dve.wait_ge(s["prod_made"], b * MT1 + n + 1)
                        dve.wait_ge(s["cb_ps"], b * RT1 + m + 1)
                        dve.tensor_tensor(hid[:, m], prod[:, n % 2], bank[4 + m % 2][:], ALU.mult)\
                           .then_inc(s["hid_made"], 1)
                for layer in range(2):
                    L2 = 2 * b + layer
                    if layer == 0:
                        for h in range(2):
                            dve.wait_ge(s["fy_ps"], 4 * b + 2 * h + 2)
                            part = x1[:, 2 * h:2 * h + 2]
                            dve.tensor_tensor(part, bank[6 + h][:].rearrange("p (t n) -> p t n", n=D), part, ALU.add)\
                               .then_inc(s["fy_used"], 1)
                    dve.wait_ge(s["rms_made"], L2 + 1)
                    dve.wait_ge(s["qkv_out"], 4 * L2)
                    dve.reciprocal(rs[:], rms_std[:]).then_inc(s["rs_made"], 1)
                    dve.wait_ge(s["qkv_out"], 4 * L2 + 4)
                    qk_in = qkv[:, :, 0:QK]
                    wide = "p (t n) -> p t n"
                    a_all = rope_a.rearrange(wide, n=QK)
                    b_all = rope_b.rearrange(wide, n=QK)
                    own.add(dve.tensor_tensor(a_all, qk_in, rope[:, layer, 0], ALU.mult))
                    for t in range(TT):
                        swapped = qkv[:, t, 0:QK].rearrange("p (n two) -> p n two", two=2)[:, :, ::-1]
                        own.add(dve.tensor_tensor(b_all[:, t].rearrange("p (n two) -> p n two", two=2), swapped,
                                                  rope[:, layer, 1, t].rearrange("p (n two) -> p n two", two=2),
                                                  ALU.mult))
                    own.settle()
                    own.add(dve.tensor_tensor(rope_a, rope_a, rope_b, ALU.add))
                    own.settle()
                    own.add(dve.tensor_tensor(rope_b, rope_a, rope_a, ALU.mult))
                    own.settle()
                    dve.reduce_sum(small[:, 0, :], rope_b.rearrange("p (n d) -> p n d", d=K), AX)\
                       .then_inc(s["qn_sum"], 1)
                    dve.wait_ge(s["qn_std"], L2 + 1)
                    own.add(dve.reciprocal(small[:, 2, :], small[:, 1, :]))
                    own.settle()
                    for t in range(TT):
                        own.add(dve.tensor_tensor(
                            qk[:, t, 0:QK].rearrange("p (n d) -> p n d", d=K),
                            a_all[:, t].rearrange("p (n d) -> p n d", d=K),
                            small[:, 2, 20 * t:20 * t + 20].rearrange("p (n o) -> p n o", o=1)
                            .broadcast_to([P, 20, K]), ALU.mult))
                    own.settle()
                    dve.tensor_copy(qk[:, :, QK:QKV], qk[:, :, D:QK]).then_inc(s["qk_made"], 1)
                    dve.wait_ge(s["qkT_out"], 6 * b + 3 * layer + 3)
                    for n in range(8):
                        dve.tensor_scalar(kz[:, n], kT[:], slot_of[:, n:n + 1], None, ALU.mult)\
                           .then_inc(s["kz_made"], 1)
                    for j in range(4):
                        dve.wait_ge(s["ot_ps"], 8 * b + 4 * layer + j + 1)
                        ps = bank[6 + j % 2][:].rearrange("p (n d) -> p n d", d=32)
                        own.add(dve.reciprocal(den[:, j], ps[:, :, K]))
                        own.settle()
                        for t in range(TT):
                            ins = dve.tensor_tensor(
                                o_tok[:, t, 64 * j:64 * j + 64].rearrange("p (g d) -> p g d", d=K),
                                ps[:, 4 * t:4 * t + 4, 0:K],
                                den[:, j, 4 * t:4 * t + 4].rearrange("p (n o) -> p n o", o=1).broadcast_to([P, 4, K]),
                                ALU.mult)
                            if t < TT - 1:
                                own.add(ins)
                        ins.then_inc(s["o_made"], 1)
                        own.settle()
                    for h in range(2):
                        dve.wait_ge(s["ao_ps"], 8 * b + 4 * layer + 2 * h + 2)
                        ps = bank[2 + h][:].rearrange("p (t n) -> p t n", n=D)
                        part = slice(2 * h, 2 * h + 2)
                        if layer == 0:
                            dve.tensor_tensor(xb[:, part], ps, xn[:, part], ALU.add).then_inc(s["xb_made"], 1)
                        else:
                            dve.wait_ge(s["acc_made"], b + 1)
                            dve.wait_ge(s["stored"], 16 * b)
                            dve.tensor_tensor(fin[:, part], ps, x1[:, part], ALU.add).then_inc(s["fin_made"], 1)
                own.end()

        @block.scalar
        def _(act):
            act.wait_ge(s["weights_in"], 16 * len(loads))
            with act.Fori(0, NB) as b:
                for h in range(2):
                    act.wait_ge(s["yT_ps"], 4 * b + 2 * h + 2)
                    act.wait_ge(s["qkT_ps"], 6 * b)
                    act.activation(w1[:, 512 * h:512 * h + 512], bank[h][:], ACT.Copy, scale=0.5)\
                       .then_inc(s["yt_out"], 1)
                act.wait_ge(s["gn_var"], b + 1)
                act.activation(small[:, 2, 0:NH], small[:, 1, 0:NH], ACT.Sqrt, bias=eps[:, 0:1], scale=1.0 / K)\
                   .then_inc(s["gn_std"], 1)
                for c in range(C2):
                    act.wait_ge(s["ynT_ps"], 2 * b + c + 1)
                    act.wait_ge(s["wo_ps"], 4 * b)
                    act.activation(yl[:, c], bank[2 + c][:], ACT.Identity, bias=ln_wb[:, 1, c:c + 1],
                                   scale=ln_wb[:, 0, c:c + 1]).then_inc(s["yl_made"], 1)
                act.wait_ge(s["ln_var"], b + 1)
                act.activation(std[:], mv[:, :, 1], ACT.Sqrt, bias=eps[:, 1:2]).then_inc(s["ln_std"], 1)

                def rms(layer, src, ready, count):
                    for t in range(TT):
                        act.wait_ge(ready, count)
                        act.wait_ge(s["ss_made"], 8 * b + 4 * layer + t)
                        act.activation(sq[:], src[:, t], ACT.Square, accum_out=ss[:, layer, t:t + 1])\
                           .then_inc(s["ss_made"], 1)
                    act.wait_ge(s["ss_made"], 8 * b + 4 * layer + 4)
                    act.wait_ge(s["rs_made"], 2 * b + layer)
                    act.activation(rms_std[:], ss[:, layer], ACT.Sqrt, bias=eps[:, 2:3], scale=1.0 / D)\
                       .then_inc(s["rms_made"], 1)

                rms(0, xn, s["xn_made"], 4 * b + 4)
                for c in range(C2):
                    act.wait_ge(s["xT_ps"], 4 * b + c + 1)
                    act.activation(xT[:, c], bank[c][:], ACT.Copy).then_inc(s["xT_out"], 1)
                act.wait_ge(s["route_ps"], b + 1)
                act.wait_ge(s["cb_made"], b)
                act.activation(sc[:], bank[7][:, 0:TT * E1].rearrange("p (t e) -> p t e", e=E1), ACT.Sigmoid)\
                   .then_inc(s["sc_out"], 1)
                for n in range(MT1):
                    act.wait_ge(s["up_ps"], b * MT1 + n + 1)
                    act.wait_ge(s["prod_made"], at(b, MT1, n - 1))
                    act.activation(silu[:, n % 2], bank[n % 2][:], ACT.Silu).then_inc(s["silu_made"], 1)
                    if n == MT1 - RT1 - 1:
                        act.wait_ge(s["cbT_ps"], b + 1)
                        act.activation(cbT[:], bank[6][0:48, 0:T // 2].bitcast(BF16), ACT.Copy)\
                           .then_inc(s["cbT_out"], 1)
                for layer in range(2):
                    L2 = 2 * b + layer
                    if layer:
                        rms(1, xb, s["xb_made"], 2 * b + 2)
                        for c in range(C2):
                            act.wait_ge(s["xT_ps"], 4 * b + 2 + c + 1)
                            act.activation(xT[:, c], bank[c][:], ACT.Copy).then_inc(s["xT_out"], 1)
                    if layer == 0:
                        act.wait_ge(s["lat_ps"], b + 1)
                        act.activation(lat[:], bank[4][0:LAT, :], ACT.Copy).then_inc(s["lat_out"], 1)
                    act.wait_ge(s["rs_made"], L2 + 1)
                    act.wait_ge(s["v_made"], L2)
                    for t in range(TT):
                        act.wait_ge(s["qkv_ps"], 4 * L2 + t + 1)
                        act.activation(qkv[:, t], bank[t][:, 0:QKV], ACT.Copy, scale=rs[:, t:t + 1])\
                           .then_inc(s["qkv_out"], 1)
                    act.wait_ge(s["qn_sum"], L2 + 1)
                    act.activation(small[:, 1, :], small[:, 0, :], ACT.Sqrt, bias=eps[:, 2:3], scale=1.0 / K)\
                       .then_inc(s["qn_std"], 1)
                    for n in range(3):
                        act.wait_ge(s["qkT_ps"], 3 * L2 + n + 1)
                        dst = qT[:, n] if n < 2 else kT[:]
                        act.activation(dst, bank[4 + n][:], ACT.Copy).then_inc(s["qkT_out"], 1)
                    mine = [x for x in enumerate(groups) if x[1][0] == layer]
                    act.wait_ge(s["kz_made"], 8 * L2 + 8)
                    for j in range(4):
                        for n, (_, jj, i, heads, start, width) in mine:
                            if jj != j:
                                continue
                            act.wait_ge(s["score_ps"], b * NG + n + 1)
                            act.wait_ge(s["pv_ps"], at(b, 32, 16 * layer + 4 * j + i - 1))
                            cols = len(heads) * width
                            src = bank[n % 4][:, 0:cols].rearrange("p (h t) -> p h t", t=width)
                            act.activation(prob[:, i % 2, heads[0]:heads[0] + len(heads), 0:width], src, ACT.Exp,
                                           scale=0.25).then_inc(s["exp_out"], 1)
                        act.wait_ge(s["pv_ps"], 32 * b + 16 * layer + 4 * j + 4)
                        act.wait_ge(s["ot_ps"], at(b, 8, 4 * layer + j - 1))
                        act.activation(oT[:, j % 2], bank[4 + j % 2][:], ACT.Copy).then_inc(s["oT_out"], 1)
                    for c in range(C2):
                        act.wait_ge(s["onT_ps"], 4 * b + 2 * layer + c + 1)
                        act.activation(onT[:, c], bank[c][:], ACT.Copy).then_inc(s["onT_out"], 1)

        @block.tensor
        def _(pe):
            pe.wait_ge(s["weights_in"], 16 * len(loads))
            pe.wait_ge(s["setup"], SETUP)
            with pe.Fori(0, NB) as b:
                pe.wait_ge(s["ya_made"], 2 * b + 2)
                pe.wait_ge(s["onT_out"], 4 * b)
                for t in range(TT):
                    for c in range(C2):
                        at_col = (t % 2) * D + c * P
                        ins = pe.transpose(bank[t // 2][:, at_col:at_col + P], ya[:, c, t * P:(t + 1) * P], ident[:])
                    ins.then_inc(s["yT_ps"], 1)
                pe.wait_ge(s["yn_made"], b + 1)
                pe.wait_ge(s["fin_made"], 2 * b)
                ytok = w1[:, 0:TT * D].rearrange("p (t n) -> p t n", n=D)
                for c in range(C2):
                    for t in range(TT):
                        ins = pe.transpose(bank[2 + c][:, t * P:(t + 1) * P], ytok[:, t, c * P:(c + 1) * P], ident[:])
                    ins.then_inc(s["ynT_ps"], 1)
                pe.wait_ge(s["ag_made"], 2 * b + 2)
                for t in range(TT):
                    for c in range(C2):
                        ins = pe.matmul(bank[4 + t // 2][:, (t % 2) * D:(t % 2) * D + D],
                                        yl[:, c, t * P:(t + 1) * P], wo0[:, c], start=c == 0, stop=c == C2 - 1)
                    ins.then_inc(s["wo_ps"], 1)
                for c in range(C2):
                    for t in range(TT):
                        if c == 0:
                            pe.wait_ge(s["xn_made"], 4 * b + t + 1)
                        ins = pe.transpose(bank[c][:, t * P:(t + 1) * P], xn[:, t, c * P:(c + 1) * P], ident[:])
                    ins.then_inc(s["xT_ps"], 1)
                pe.wait_ge(s["xT_out"], 4 * b + 2)
                for t in range(TT):
                    for c in range(C2):
                        ins = pe.matmul(bank[7][:, t * E1:(t + 1) * E1], xT[:, c, t * P:(t + 1) * P],
                                        route_w[:, c, :], start=c == 0, stop=c == C2 - 1)
                ins.then_inc(s["route_ps"], 1)
                for n, m in enumerate(ORDER):
                    if n == MT1 - RT1:
                        for t in range(TT):
                            ins = pe.transpose(bank[6][0:48, 64 * t:64 * t + 64].bitcast(BF16),
                                               cbp[:, t].rearrange("p s e -> p (s e)"), identb[:])
                        ins.then_inc(s["cbT_ps"], 1)
                    pe.wait_ge(s["prod_made"], at(b, MT1, n - 1))
                    if n == MT1 - RT1 - 1:
                        pe.wait_ge(s["cb_made"], b + 1)
                    for half in range(2):
                        for c in range(C2):
                            ins = pe.matmul(bank[2 * half + n % 2][:], up_w[:, half, c, m * P:(m + 1) * P],
                                            xT[:, c], start=c == 0, stop=c == C2 - 1)
                    ins.then_inc(s["up_ps"], 1)
                    if m < RT1:
                        pe.wait_ge(s["cbT_out"], b + 1)
                        pe.wait_ge(s["hid_made"], at(b, RT1, m - 1))
                        pe.matmul(bank[4 + m % 2][:], sel[:, m], cbT[:], start=True, stop=True)\
                          .then_inc(s["cb_ps"], 1)
                pe.wait_ge(s["sc_out"], b + 1)
                pe.wait_ge(s["hid_made"], b * RT1 + RT1)
                for t in range(TT):
                    for m in range(MT1):
                        ins = pe.matmul(bank[6 + t // 2][:, (t % 2) * D:(t % 2) * D + D],
                                        hid[:, m, t * P:(t + 1) * P], down_w[:, m], start=m == 0, stop=m == MT1 - 1)
                    ins.then_inc(s["fy_ps"], 1)

                for layer in range(2):
                    L2 = 2 * b + layer
                    if layer:
                        for c in range(C2):
                            for t in range(TT):
                                pe.wait_ge(s["xb_made"], 2 * b + t // 2 + 1)
                                ins = pe.transpose(bank[c][:, t * P:(t + 1) * P], xb[:, t, c * P:(c + 1) * P],
                                                   ident[:])
                            ins.then_inc(s["xT_ps"], 1)
                        pe.wait_ge(s["xT_out"], 4 * b + 4)
                    if layer == 0:
                        for c in range(C2):
                            ins = pe.matmul(bank[4][0:LAT, :], wd[:, c], xT[:, c], start=c == 0, stop=c == C2 - 1)
                        ins.then_inc(s["lat_ps"], 1)
                    for t in range(TT):
                        tok = slice(t * P, (t + 1) * P)
                        if layer == 0:
                            for c in range(C2):
                                pe.matmul(bank[t][:, 0:D], xT[:, c, tok], wq[0][:, c], start=c == 0, stop=c == C2 - 1)
                            if t == 0:
                                pe.wait_ge(s["lat_out"], b + 1)
                            ins = pe.matmul(bank[t][:, D:QKV], lat[:, tok], kv_up[:], start=True, stop=True)
                        else:
                            for c in range(C2):
                                ins = pe.matmul(bank[t][:, 0:QKV], xT[:, c, tok], wq[1][:, c],
                                                start=c == 0, stop=c == C2 - 1)
                        ins.then_inc(s["qkv_ps"], 1)
                    pe.wait_ge(s["qk_made"], L2 + 1)
                    for n in range(3):
                        for t in range(TT):
                            ins = pe.transpose(bank[4 + n][:, t * P:(t + 1) * P], qk[:, t, n * P:(n + 1) * P],
                                               ident[:])
                        ins.then_inc(s["qkT_ps"], 1)
                    mine = [x for x in enumerate(groups) if x[1][0] == layer]
                    first = mine[0][0]

                    def score(n, j, i, heads, start, width):
                        pe.wait_ge(s["exp_out"], at(b, NG, n - 3 if n - first >= 4 else first))
                        for x, h in enumerate(heads):
                            ps = bank[n % 4][:, x * width:(x + 1) * width]
                            pe.matmul(ps, kz[:, 4 * (j % 2) + h, i * P:(i + 1) * P],
                                      qT[:, j // 2, start:start + width], start=True, stop=False)
                            masked = min(width, P if layer == 0 else P + 64)
                            mask = causal if layer == 0 else window
                            ins = pe.matmul(ps[:, 0:masked], identb[:], mask[:, 0:masked], start=False, stop=True)
                        ins.then_inc(s["score_ps"], 1)

                    def weigh(j, i):
                        pe.wait_ge(s["exp_out"], b * NG + groups_until(layer, j, i))
                        start = P * i
                        end = T if layer == 0 else min(T, P * i + P + 64)
                        parts = [(start, end)] if i == 0 or layer == 0 else [(start, start + 64), (start + 64, end)]
                        for lo, hi in parts:
                            for h in range(KVH):
                                ins = pe.matmul(bank[4 + j % 2][32 * h:32 * h + 32, lo:hi], v1[:, i, h],
                                                prob[:, i % 2, h, lo - start:hi - start],
                                                start=i == 0, stop=hi == T and i == TT - 1)
                        ins.then_inc(s["pv_ps"], 1)

                    def turn(j):
                        pe.wait_ge(s["oT_out"], 8 * b + 4 * layer + j + 1)
                        pe.wait_ge(s["o_made"], at(b, 8, 4 * layer + j - 1))
                        for t in range(TT):
                            ins = pe.transpose(bank[6 + j % 2][:, t * P:(t + 1) * P],
                                               oT[:, j % 2, t * P:(t + 1) * P], ident[:])
                        ins.then_inc(s["ot_ps"], 1)

                    pe.wait_ge(s["qkT_out"], 3 * L2 + 3)
                    pe.wait_ge(s["kz_made"], 8 * L2 + 8)
                    pe.wait_ge(s["v_made"], L2 + 1)
                    pend = []
                    for j in range(4):
                        for i in range(TT):
                            for n, (_, _, _, heads, start, width) in [x for x in mine if x[1][1:3] == (j, i)]:
                                score(n, j, i, heads, start, width)
                            if i == 0 and j >= 2:
                                pe.wait_ge(s["oT_out"], 8 * b + 4 * layer + j - 1)
                            pend.append((j, i))
                            if len(pend) > 1:
                                weigh(*pend.pop(0))
                            if i == 1 and j:
                                turn(j - 1)
                    weigh(*pend.pop(0))
                    turn(3)
                    pe.wait_ge(s["o_made"], 8 * b + 4 * layer + 4)
                    for c in range(C2):
                        for t in range(TT):
                            ins = pe.transpose(bank[c][:, t * P:(t + 1) * P], o_tok[:, t, c * P:(c + 1) * P],
                                               ident[:])
                        ins.then_inc(s["onT_ps"], 1)
                    pe.wait_ge(s["onT_out"], 4 * b + 2 * layer + 2)
                    for t in range(TT):
                        for c in range(C2):
                            ins = pe.matmul(bank[2 + t // 2][:, (t % 2) * D:(t % 2) * D + D],
                                            onT[:, c, t * P:(t + 1) * P], wo[layer][:, c],
                                            start=c == 0, stop=c == C2 - 1)
                        ins.then_inc(s["ao_ps"], 1)


def _constants(np):
    bf16 = np.dtype("bfloat16")
    eye = np.eye(P, dtype=np.float32)
    before = lambda n: np.tile((np.arange(n)[None, :] < np.arange(n)[:, None]).astype(np.float32).reshape(1, n * n),
                               (P, 1))
    s, t = np.arange(P)[:, None], np.arange(P + 64)[None, :]
    causal = np.where(t[:, :P] < s, np.float32(-1e30), np.float32(0))
    window = np.where((t < s) | (t - s >= 64), np.float32(-1e30), np.float32(0))
    rope = np.zeros((P, 2, 2, TT, 20, K // 2, 2), np.float32)
    for layer, base in enumerate((1000000.0, 10000.0)):
        inv = (1.0 / np.float32(base) ** (np.arange(0, K, 2, dtype=np.float32) / np.float32(K))).astype(np.float32)
        ang = np.arange(T, dtype=np.float32)[:, None] * inv[None, :]
        cos = np.cos(ang).astype(np.float32).reshape(TT, P, 8).transpose(1, 0, 2)
        sin = np.sin(ang).astype(np.float32).reshape(TT, P, 8).transpose(1, 0, 2)
        rope[:, layer, 0] = cos[:, :, None, :, None]
        rope[:, layer, 1, :, :, :, 0] = -sin[:, :, None, :]
        rope[:, layer, 1, :, :, :, 1] = sin[:, :, None, :]
    slot = (np.arange(P)[:, None] // K == np.arange(8)[None, :]).astype(np.float32)
    sel = np.zeros((48, RT1, P), np.float32)
    for m in range(RT1):
        for p in range(P):
            sel[[2 * m + p // H1, E1 + 2 * m + p // H1, 2 * E1 + 2 * m + p // H1], m, p] = 1.0
    return {
        "c_ident": eye, "c_before8": before(E0), "c_identb": eye.astype(bf16),
        "c_causal": causal.astype(bf16), "c_window": window.astype(bf16),
        "c_rope": rope.reshape(P, 2, 2, TT, 320), "c_slot": slot,
        "c_eps": np.tile(np.array([[1e-5 * 64.0, 1e-5, 1e-6]], np.float32), (P, 1)),
        "c_sel": sel.astype(bf16), "c_before16": before(E1), "c_before4": before(G4),
    }


def _layouts(np, i):
    def rows(w):
        w = np.asarray(w)
        return np.ascontiguousarray(w.reshape(C2, P, -1).transpose(1, 0, 2))

    def vec(v):
        return np.ascontiguousarray(np.asarray(v).reshape(C2, P).T)

    n = {k: np.asarray(v) for k, v in i.items()}
    l0, f0, l1, f1 = "L0_attn_", "L0_ffn_", "L1_attn_", "L1_ffn_"
    conv = n[l0 + "conv_w"]
    heads = np.array([4 * g + j for j in range(4) for g in range(KVH)])
    cols = (heads[:, None] * K + np.arange(K)[None, :]).reshape(-1)
    token = lambda x: np.ascontiguousarray(x.reshape(NB, TT, P, D).transpose(0, 2, 1, 3))
    up0 = np.stack([n[f0 + "W1"], n[f0 + "W2"]], 1)
    up1 = np.stack([np.concatenate([n[f1 + "gate_w"].transpose(1, 0, 2).reshape(D, E1 * H1),
                                    n[f1 + "shared_gate_w"].T], 1),
                    np.concatenate([n[f1 + "up_w"].transpose(1, 0, 2).reshape(D, E1 * H1),
                                    n[f1 + "shared_up_w"].T], 1)], 0)
    down1 = np.concatenate([n[f1 + "down_w"].reshape(E1 * H1, D), n[f1 + "shared_down_w"].T], 0)
    c = np.ascontiguousarray
    return {
        "x": token(n[l0 + "x"]),
        "c_vecs": c(np.stack([vec(v) for v in (conv[:, 0, 0], conv[:, 0, 1], conv[:, 0, 2], n[l0 + "maa_x"],
                                               n[l0 + "maa_w"], n[l0 + "maa_k"], n[l0 + "maa_v"], n[l0 + "maa_r"],
                                               n[l0 + "maa_g"], n[l0 + "gate_b"])], 1)),
        "time_decay": vec(n[l0 + "time_decay"]),
        "maa_w1": rows(n[l0 + "maa_w1"]), "maa_w2": c(n[l0 + "maa_w2"]),
        "gate_w": rows(n[l0 + "gate_w"]), "Wk": rows(n[l0 + "Wk"]), "Wv": rows(n[l0 + "Wv"]),
        "Wr": rows(n[l0 + "Wr"]), "Wg": rows(n[l0 + "Wg"]), "Wo": rows(n[l0 + "Wo"]),
        "decay_w1": rows(n[l0 + "decay_w1"]), "decay_w2": c(n[l0 + "decay_w2"]),
        "ffn_Wg": rows(n[f0 + "Wg"].T),
        "ffn_up": c(up0.reshape(E0, 2, H0, C2, P).transpose(0, 4, 1, 3, 2)),
        "ffn_down": c(n[f0 + "W3"].transpose(0, 2, 1)),
        "ln_wb": c(np.stack([vec(n[l0 + "ln_w"]), vec(n[l0 + "ln_b"])], 1)),
        "norm_w": c(np.stack([vec(n[l1 + "norm1_w"]), vec(n[l1 + "norm2_w"])], 1)),
        "g_wq": rows(n[l1 + "g_wq"][:, cols]), "g_kv_down": rows(n[l1 + "g_kv_down"]),
        "g_kv_up": c(np.concatenate([n[l1 + "g_k_up"], n[l1 + "g_v_up"]], 1)),
        "l_wqkv": rows(np.concatenate([n[l1 + "l_wq"][:, cols], n[l1 + "l_wk"], n[l1 + "l_wv"]], 1)),
        "g_wo": rows(n[l1 + "g_wo"][cols]), "l_wo": rows(n[l1 + "l_wo"][cols]),
        "router_w": rows(n[f1 + "router_w"].T), "bias_r": c(np.tile(n[f1 + "correction_bias"][None, :], (P, 1))),
        "ffn1_up": c(up1.reshape(2, C2, P, MT1 * P).transpose(2, 0, 1, 3)),
        "ffn1_down": c(down1.reshape(MT1, P, D).transpose(1, 0, 2)),
    }


def kernel(**inputs):
    import concourse.bacc as bacc
    import numpy as np
    from concourse.bass_utils import run_bass_kernel_spmd

    arrays = {**_layouts(np, inputs), **_constants(np)}
    nc = bacc.Bacc("TRN2", target_bir_lowering=False, num_devices=1)
    a = {k: nc.dram_tensor("in_" + k, v.shape, mybir.dt.from_np(v.dtype), kind="ExternalInput").ap()
         for k, v in arrays.items()}
    out = nc.dram_tensor("out", (NB, P, TT, D), F32, kind="ExternalOutput").ap()
    build(nc, a, out)
    r = run_bass_kernel_spmd(nc, [{"in_" + k: v for k, v in arrays.items()}], core_ids=[0])
    got = r.results[0]["out"]
    return np.ascontiguousarray(got.transpose(0, 2, 1, 3)).reshape(NB, T, D)
```

```python
from contextlib import ExitStack

import concourse.bass as bass
from concourse import mybir

F32 = mybir.dt.float32
BF16 = mybir.dt.bfloat16
F16 = mybir.dt.float16
ALU = mybir.AluOpType
ACT = mybir.ActivationFunctionType
AX = mybir.AxisListType.X

P = 128
NB, T, D = 8, 512, 256
C2 = D // P
TT = T // P
H, K = 16, 16
E0, H0 = 8, 704
HT0 = (H0 + P - 1) // P
E1, H1, HS = 16, 64, 512
MT1 = (E1 * H1 + HS) // P
RT1 = E1 * H1 // P
KVH = 4
G4 = 4
LAT = 64


class Steps:

    def __init__(self, engine, semaphore, per_round):
        self.engine, self.semaphore, self.per_round, self.done = engine, semaphore, per_round, 0
        self.base = 0

    def round(self, number):
        self.base, self.done = number * self.per_round, 0

    def add(self, instruction):
        instruction.then_inc(self.semaphore, 1)
        self.done += 1

    def settle(self):
        self.engine.wait_ge(self.semaphore, self.base + self.done)

    def end(self):
        assert self.done == self.per_round, (self.semaphore, self.done)


def at(number, per_round, n):
    return number * per_round + max(n, 0)


def build(nc, a, out):
    ctx = ExitStack()
    with ctx:
        scratch = {n: nc.dram_tensor("scratch_" + n, shape, F32, kind="Internal").ap() for n, shape in
                   (("rkw", [3, NB * D, T]), ("v", [NB * D, T]), ("gate", [NB * D, T]), ("g", [NB * D, T]),
                    ("y", [NB * D, T]), ("ffn", [P, NB * TT, D]))}
        keep = {"ident": ctx.enter_context(nc.sbuf_tensor("ident", [P, P], F32))}
        with ExitStack() as first:
            keep["xh"] = first.enter_context(nc.sbuf_tensor("xh", [P, C2, NB * T], F16))
            keep["xl"] = first.enter_context(nc.sbuf_tensor("xl", [P, C2, NB * T], F16))
            keep["w0"] = first.enter_context(nc.sbuf_tensor("route0", [P, NB * TT, E0], F32))
            project(nc, a, scratch, keep)
            scan_and_experts(nc, a, scratch, keep)
        layer_one(nc, a, scratch, keep, out)


def project(nc, a, scratch, keep):
    with ExitStack() as ctx:
        def sb(name, shape, dt=F32):
            return ctx.enter_context(nc.sbuf_tensor("b1_" + name, shape, dt))

        def sem(name):
            return ctx.enter_context(nc.semaphore("b1_" + name))

        bank = [ctx.enter_context(nc.psum_tensor(f"b1_bank{n}", [P, 512], F32)) for n in range(8)]
        ident, xh, xl, w0 = (keep[n] for n in ("ident", "xh", "xl", "w0"))
        xnT = sb("xnT", [P, C2, NB * T])
        x_tok = sb("x_tok", [P, 2, TT, D])
        xn_tok = sb("xn_tok", [P, 2, TT, D])
        stats = sb("stats", [P, 2, TT, 6])
        mv = sb("mv", [P, 2, TT, 2])
        std = sb("std", [P, 2, TT])
        rstd = sb("rstd", [P, 2, TT])
        eps = sb("eps", [P, 1])
        holds_wait = sb("holds_wait", [P, 1])
        pool_wait = sb("pool_wait", [P, 9])
        dx = sb("dx", [P, C2, NB * T])
        xxx = sb("xxx", [P, 2, C2, T])
        t5 = sb("t5", [P, 2, NB * T])
        vecs = sb("vecs", [P, 10, C2])
        td = sb("time_decay", [P, C2])
        maa_w1 = sb("maa_w1", [P, C2, 160])
        mix_w = sb("mix_w", [P, 5, D])
        proj_w = sb("proj_w", [P, 5, C2, D])
        dec_w1 = sb("dec_w1", [P, C2, P])
        dec_w2 = sb("dec_w2", [P, D])
        tmp = xxx
        xf = x_tok[:].rearrange("p u t n -> p (u t n)").rearrange("p (s c t) -> p s c t", s=2, c=C2)
        route_w = sb("route_w", [P, C2, E0])
        before = sb("before", [P, E0 * E0])
        sc = sb("sc", [P, NB * TT, E0])
        rank = sb("rank", [P, NB * TT, E0])
        tw = sb("tw", [P, T])
        ew = sb("ew", [P, 2, T])
        stage = sb("stage", [P, 6, C2, T])

        more = xxx[:].rearrange("p u c t -> p (u c t)")
        same = x_tok[:].rearrange("p u t n -> p (u t n)")
        assert more.shape[1] == same.shape[1] == NB * TT * E0 * E0

        weights_in, zeroed = sem("weights_in"), sem("zeroed")
        xl_made, route_ps, route_own = (sem(n) for n in ("xl_made", "route_ps", "route_own"))
        x_in = [sem(f"x_in{u}") for u in range(2)]
        vec_ready, var_ready, std_ready = sem("vec_ready"), sem("var_ready"), sem("std_ready")
        xn_made = [sem(f"xn_made{u}") for u in range(2)]
        xT_ps = sem("xT_ps")
        xT_out = [sem(f"xT_out{u}") for u in range(2)]
        xxx_made = [sem(f"xxx_made{u}") for u in range(2)]
        t5_ps = sem("t5_ps")
        t5_out = [sem(f"t5_out{u}") for u in range(2)]
        own1 = sem("dve_own1")
        m_ps, m_used, xf_made = sem("m_ps"), sem("m_used"), sem("xf_made")
        unit_ps, unit_out, act_own = sem("unit_ps"), sem("unit_out"), sem("act_own")
        staged = [sem(f"staged{n}") for n in range(6)]

        WEIGHT_LOADS = 18
        UNITS = [("gate", 0), ("gate", 1), ("tw", 0), ("k", 0), ("k", 1), ("v", 0), ("v", 1), ("r", 0), ("r", 1),
                 ("decay", 0), ("decay", 1), ("g", 0), ("g", 1)]
        NU = len(UNITS)
        UB = 5
        SLOT = {"gate": 0, "k": 1, "v": 2, "r": 3, "decay": 4, "g": 5}
        USED = [3, 5, 7, 9, 13]

        block = ctx.enter_context(nc.Block())

        @block.sync
        def _(sp):
            for dst, src in ((ident[:], a["c_ident"]), (vecs[:], a["c_vecs"]), (maa_w1[:], a["maa_w1"]),
                             (proj_w[:, 0], a["gate_w"]), (proj_w[:, 1], a["Wk"]), (proj_w[:, 2], a["Wv"]),
                             (proj_w[:, 3], a["Wr"]), (proj_w[:, 4], a["Wg"]), (td[:], a["time_decay"]),
                             (route_w[:], a["ffn_Wg"]), (before[:], a["c_before8"])):
                sp.dma_start(dst, src).then_inc(weights_in, 16)
            sp.wait_ge(zeroed, 4)
            for f in range(4):
                sp.dma_start(mix_w[32 * f:32 * f + 32, f, :], a["maa_w2"][f]).then_inc(weights_in, 16)
            sp.dma_start(mix_w[0:32, 4, :], a["maa_w2"][4]).then_inc(weights_in, 16)
            sp.dma_start(dec_w1[:, :, 0:64], a["decay_w1"]).then_inc(weights_in, 16)
            sp.dma_start(dec_w2[0:64, :], a["decay_w2"]).then_inc(weights_in, 16)
            with sp.Fori(0, NB // 2) as i:
                for u in range(2):
                    sp.wait_ge(xn_made[u], TT * i)
                    sp.dma_start(x_tok[:, u], a["x"][2 * i + u]).then_inc(x_in[u], 16)
            outs = [(0, scratch["gate"], 2), (1, scratch["rkw"][1], 5), (2, scratch["v"], 7),
                    (3, scratch["rkw"][0], 9), (4, scratch["rkw"][2], 11), (5, scratch["g"], 13)]
            with sp.Fori(0, NB) as b:
                for n, dram, units in outs:
                    sp.wait_ge(unit_out, b * NU + units)
                    dst = dram.rearrange("(b c p) t -> b p c t", c=C2, p=P)[b]
                    sp.dma_start(dst, stage[:, n]).then_inc(staged[n], 16)
            for n in range(6):
                sp.wait_ge(staged[n], 16 * NB)

        @block.gpsimd
        def _(pool):
            pool.memset(mix_w[:], 0.0).then_inc(zeroed, 1)
            pool.memset(dec_w1[:], 0.0).then_inc(zeroed, 1)
            pool.memset(dec_w2[:], 0.0).then_inc(zeroed, 1)
            pool.memset(t5[:, 1, :], 0.0).then_inc(zeroed, 1)
            pool.memset(eps[:], 1e-5).then_inc(zeroed, 1)
            with pool.Fori(0, NB // 2) as i:
                for u in range(2):
                    for c in range(C2):
                        pool.wait_ge(xl_made, 2 * C2 * i)
                        pool.wait_ge(xT_out[u], 4 * i + 2 * c + 2)
                        pool.tensor_tensor(pool_wait[:, 5 + 2 * u + c:6 + 2 * u + c], eps[:], eps[:], ALU.add)
                        cols = bass.ds((2 * i + u) * T, T)
                        pool.tensor_tensor(xl[:, c, cols], xnT[:, c, cols], xh[:, c, cols], ALU.subtract)\
                            .then_inc(xl_made, 1)
            pool.wait_ge(xl_made, C2 * NB)
            with pool.Fori(0, NB) as b:
                for f in range(5):
                    pool.wait_ge(m_used, b * 10 + 2 * f + 2)
                    pool.wait_ge(unit_ps, at(b, NU, USED[f - 2] if f >= 2 else 0))
                    pool.tensor_tensor(pool_wait[:, f:f + 1], eps[:], eps[:], ALU.add)
                    for c in range(C2):
                        pool.tensor_tensor(xf[:, f % 2, c], tmp[:, f % 2, c], xnT[:, c, bass.ds(b * T, T)],
                                           ALU.add).then_inc(xf_made, 1)

        @block.vector
        def _(dve):
            own = Steps(dve, own1, 32)
            dve.wait_ge(weights_in, 16 * WEIGHT_LOADS)
            dve.tensor_scalar(vecs[:, 1, :], vecs[:, 1, :], -1.0, None, ALU.add).then_inc(vec_ready, 1)
            dve.tensor_scalar(vecs[:, 9, :], vecs[:, 9, :], 0.5, None, ALU.mult).then_inc(vec_ready, 1)
            dve.wait_ge(vec_ready, 2)
            with dve.Fori(0, NB // 2) as i:
                own.round(i)
                for u in range(2):
                    dve.wait_ge(x_in[u], 16 * i + 16)
                    for t in range(TT):
                        own.add(dve.bn_stats(stats[:, u, t], x_tok[:, u, t]))
                    own.settle()
                    own.add(dve.memset(holds_wait[:, 0:1], 0.0))
                    for t in range(TT):
                        ins = dve.bn_aggr(mv[:, u, t], stats[:, u, t])
                        if t < TT - 1:
                            own.add(ins)
                    ins.then_inc(var_ready, 1)
                for u in range(2):
                    dve.wait_ge(std_ready, 2 * i + u + 1)
                    dve.wait_ge(xT_out[u], 4 * i)
                    own.add(dve.reciprocal(rstd[:, u], std[:, u]))
                    own.settle()
                    for t in range(TT):
                        ins = dve.tensor_scalar(xn_tok[:, u, t], x_tok[:, u, t], mv[:, u, t, 0:1],
                                                rstd[:, u, t:t + 1], ALU.subtract, ALU.mult)
                        ins.then_inc(xn_made[u], 1)
                for u in range(2):
                    dve.wait_ge(xT_out[u], 4 * i + 4)
                    x = [xnT[:, c, bass.ds((2 * i + u) * T, T)] for c in range(C2)]
                    x_head = [xnT[:, c, bass.ds((2 * i + u) * T, T - 1)] for c in range(C2)]
                    x_tail = [xnT[:, c, bass.ds((2 * i + u) * T + 1, T - 1)] for c in range(C2)]
                    d = [dx[:, c, bass.ds((2 * i + u) * T, T)] for c in range(C2)]
                    d_head = [dx[:, c, bass.ds((2 * i + u) * T, T - 1)] for c in range(C2)]
                    d_tail = [dx[:, c, bass.ds((2 * i + u) * T + 1, T - 1)] for c in range(C2)]
                    for c in range(C2):
                        own.add(dve.tensor_scalar(d[c], x[c], vecs[:, 1, c:c + 1], None, ALU.mult))
                    own.settle()
                    for c in range(C2):
                        own.add(dve.scalar_tensor_tensor(d_tail[c], x_head[c], vecs[:, 0, c:c + 1], d_tail[c],
                                                         ALU.mult, ALU.add))
                    own.settle()
                    for c in range(C2):
                        own.add(dve.scalar_tensor_tensor(d_head[c], x_tail[c], vecs[:, 2, c:c + 1], d_head[c],
                                                         ALU.mult, ALU.add))
                    own.settle()
                    dve.wait_ge(t5_out[u], 2 * i)
                    for c in range(C2):
                        ins = dve.scalar_tensor_tensor(xxx[:, u, c], d[c], vecs[:, 3, c:c + 1], x[c],
                                                       ALU.mult, ALU.add)
                        if c == 0:
                            own.add(ins)
                    ins.then_inc(xxx_made[u], 1)
                own.end()
            dve.wait_ge(route_ps, 1)
            dve.wait_ge(xn_made[1], TT * (NB // 2))
            n_rows = NB * TT
            own = Steps(dve, route_own, 7)
            own.add(dve.tensor_copy(sc[:], bank[7][:, 0:n_rows * E0].rearrange("p (t e) -> p t e", e=E0)))
            own.settle()
            others = sc[:].rearrange("p t (o e) -> p t o e", o=1).broadcast_to([P, n_rows, E0, E0])
            itself = sc[:].rearrange("p t (e o) -> p t e o", o=1).broadcast_to([P, n_rows, E0, E0])
            square = "p (t e j) -> p t e j"
            own.add(dve.tensor_tensor(more.rearrange(square, e=E0, j=E0), others, itself, ALU.is_gt))
            own.add(dve.tensor_tensor(same.rearrange(square, e=E0, j=E0), others, itself, ALU.is_equal))
            own.settle()
            same_rows = same.rearrange("p (t n) -> p t n", n=E0 * E0)
            own.add(dve.tensor_tensor(same_rows, same_rows, before[:].rearrange("p (o n) -> p o n", o=1)
                                      .broadcast_to([P, n_rows, E0 * E0]), ALU.mult))
            own.settle()
            own.add(dve.tensor_tensor(more, more, same, ALU.add))
            own.settle()
            own.add(dve.reduce_sum(rank[:], more.rearrange("p (n j) -> p n j", j=E0), AX))
            own.settle()
            own.add(dve.scalar_tensor_tensor(w0[:], rank[:], 2.0, sc[:], ALU.is_lt, ALU.mult))
            own.settle()
            with dve.Fori(0, NB) as b:
                for f in range(5):
                    for c in range(C2):
                        dve.wait_ge(m_ps, b * 10 + 2 * f + c + 1)
                        dve.wait_ge(xf_made, at(b, 10, 2 * (f - 2) + c + 1))
                        dve.scalar_tensor_tensor(tmp[:, f % 2, c], bank[(2 * f + c) % 2][:], vecs[:, 4 + f, c:c + 1],
                                                 dx[:, c, bass.ds(b * T, T)], ALU.add, ALU.mult).then_inc(m_used, 1)

        @block.scalar
        def _(act):
            act.wait_ge(zeroed, 5)
            with act.Fori(0, NB // 2) as i:
                for u in range(2):
                    act.wait_ge(var_ready, 2 * i + u + 1)
                    act.activation(std[:, u], mv[:, u, :, 1], ACT.Sqrt, bias=eps[:]).then_inc(std_ready, 1)
                for u in range(2):
                    for c in range(C2):
                        act.wait_ge(xT_ps, 4 * i + 2 * u + c + 1)
                        for dst in (xh, xnT):
                            act.activation(dst[:, c, bass.ds((2 * i + u) * T, T)], bank[2 * u + c][:], ACT.Copy)\
                               .then_inc(xT_out[u], 1)
                for u in range(2):
                    act.wait_ge(t5_ps, 2 * i + u + 1)
                    act.activation(t5[:, 0, bass.ds((2 * i + u) * T, T)], bank[4 + 2 * u][:], ACT.Tanh)\
                       .then_inc(t5_out[u], 1)
                    act.activation(t5[0:32, 1, bass.ds((2 * i + u) * T, T)], bank[5 + 2 * u][0:32, :], ACT.Tanh)\
                       .then_inc(t5_out[u], 1)
            act.wait_ge(vec_ready, 2)
            with act.Fori(0, NB) as b:
                for n, (what, c) in enumerate(UNITS):
                    act.wait_ge(unit_ps, b * NU + n + 1)
                    ps = bank[2 + n % UB][:]
                    if what in SLOT and c == 0:
                        act.wait_ge(staged[SLOT[what]], 16 * b)
                    if what == "gate":
                        ins = act.activation(stage[:, 0, c], ps, ACT.Tanh, bias=vecs[:, 9, c:c + 1], scale=0.5)
                    elif what == "tw":
                        ins = act.activation(tw[:], ps, ACT.Tanh)
                    elif what == "decay":
                        act.activation(ew[:, c], ps, ACT.Exp, bias=td[:, c:c + 1]).then_inc(act_own, 1)
                        act.wait_ge(act_own, 2 * b + c + 1)
                        ins = act.activation(stage[:, 4, c], ew[:, c], ACT.Exp, scale=-1.0)
                    elif what == "g":
                        ins = act.activation(stage[:, 5, c], ps, ACT.Silu)
                    else:
                        ins = act.activation(stage[:, SLOT[what], c], ps, ACT.Copy)
                    ins.then_inc(unit_out, 1)

        @block.tensor
        def _(pe):
            pe.wait_ge(weights_in, 16 * WEIGHT_LOADS)
            pe.wait_ge(zeroed, 5)
            with pe.Fori(0, NB // 2) as i:
                for u in range(2):
                    pe.wait_ge(xT_out[u], 4 * i)
                    for c in range(C2):
                        for t in range(TT):
                            if c == 0:
                                pe.wait_ge(xn_made[u], TT * i + t + 1)
                            ins = pe.transpose(bank[2 * u + c][:, t * P:(t + 1) * P],
                                               xn_tok[:, u, t, c * P:(c + 1) * P], ident[:])
                        ins.then_inc(xT_ps, 1)
                for u in range(2):
                    pe.wait_ge(xxx_made[u], i + 1)
                    pe.wait_ge(t5_out[u], 2 * i)
                    for n, (lo, hi) in enumerate(((0, P), (P, 160))):
                        for c in range(C2):
                            ins = pe.matmul(bank[4 + 2 * u + n][0:hi - lo, :], maa_w1[:, c, lo:hi], xxx[:, u, c],
                                            start=c == 0, stop=c == C2 - 1)
                    ins.then_inc(t5_ps, 1)
            for u in range(2):
                pe.wait_ge(xT_out[u], 4 * (NB // 2))
                pe.wait_ge(t5_out[u], 2 * (NB // 2))
            for t in range(NB * TT):
                for c in range(C2):
                    ins = pe.matmul(bank[7][:, t * E0:(t + 1) * E0], xnT[:, c, t * P:(t + 1) * P],
                                    route_w[:, c], start=c == 0, stop=c == C2 - 1)
            ins.then_inc(route_ps, 1)

            with pe.Fori(0, NB) as b:
                def mix(f):
                    for c in range(C2):
                        pe.wait_ge(m_used, at(b, 10, 2 * f + c - 1))
                        pe.matmul(bank[(2 * f + c) % 2][:], mix_w[:, f, c * P:(c + 1) * P],
                                  t5[:, f // 4, bass.ds(b * T, T)], start=True, stop=True).then_inc(m_ps, 1)

                def unit(n):
                    what, o = UNITS[n]
                    pe.wait_ge(unit_out, at(b, NU, n - UB + 1))
                    cols = slice(o * P, (o + 1) * P)
                    ps = bank[2 + n % UB][:]
                    if what == "gate":
                        for c in range(C2):
                            ins = pe.matmul(ps, proj_w[:, 0, c, cols], dx[:, c, bass.ds(b * T, T)],
                                            start=c == 0, stop=c == C2 - 1)
                    elif what == "tw":
                        pe.wait_ge(xf_made, b * 10 + 2)
                        for c in range(C2):
                            ins = pe.matmul(ps, dec_w1[:, c, :], xf[:, 0, c], start=c == 0, stop=c == C2 - 1)
                    elif what == "decay":
                        pe.wait_ge(unit_out, b * NU + 3)
                        ins = pe.matmul(ps, dec_w2[:, cols], tw[:], start=True, stop=True)
                    else:
                        f = {"k": 1, "v": 2, "r": 3, "g": 4}[what]
                        pe.wait_ge(xf_made, b * 10 + 2 * f + 2)
                        for c in range(C2):
                            ins = pe.matmul(ps, proj_w[:, f, c, cols], xf[:, f % 2, c],
                                            start=c == 0, stop=c == C2 - 1)
                    ins.then_inc(unit_ps, 1)

                mix(0)
                mix(1)
                unit(0)
                unit(1)
                unit(2)
                mix(2)
                unit(3)
                unit(4)
                mix(3)
                unit(5)
                unit(6)
                mix(4)
                for n in range(7, NU):
                    unit(n)


def scan_and_experts(nc, a, scratch, keep):
    with ExitStack() as ctx:
        def sb(name, shape, dt=F32):
            return ctx.enter_context(nc.sbuf_tensor("b2_" + name, shape, dt))

        def sem(name):
            return ctx.enter_context(nc.semaphore("b2_" + name))

        bank = [ctx.enter_context(nc.psum_tensor(f"b2_bank{n}", [P, 512], F32)) for n in range(8)]
        xh, xl, w0 = keep["xh"], keep["xl"], keep["w0"]
        VH, VQ = 8, 2
        KR = K // 4
        CK = VH // VQ
        NCH = 4 * CK
        assert NCH == 2 * NB and 2 * KR == E0
        HALF = H0 - P * (HT0 - 1)
        assert 2 * HALF == P
        ffn = sb("ffn", [P, NB * TT, D])
        up_raw = sb("up_raw", [P, C2, 2 * H0])
        up_h = sb("up_h", [P, C2, 2 * H0], F16)
        up_l = sb("up_l", [P, C2, 2 * H0], F16)
        down_raw = sb("down_raw", [P, HT0, D])
        down_h = sb("down_h", [P, HT0, D], F16)
        down_l = sb("down_l", [P, HT0, D], F16)
        hid_h = sb("hid_h", [P, 2, HT0, T], BF16)
        hid_l = sb("hid_l", [P, 2, HT0, T], F16)
        prod = sb("prod", [P, 3, T])
        silu = sb("silu", [P, 2, T])
        rkw = sb("rkw", [P, 2, 3, T])
        v = sb("v", [P, VH, T])
        y = sb("y", [P, VH, T])
        kv = sb("kv", [P, 2, VQ, T])
        fwd = sb("fwd", [P, VQ, T])
        bwd = sb("bwd", [P, VQ, T])

        up_in, down_in, up_h_made, up_made, down_h_made, down_made = (
            sem(n) for n in ("up_in", "down_in", "up_h_made", "up_made", "down_h_made", "down_made"))
        v_in, y_stored, ffn_stored = sem("v_in"), sem("y_stored"), sem("ffn_stored")
        rkw_in = [sem(f"rkw_in{n}") for n in range(2)]
        cleared, x_in = sem("cleared"), sem("x_in")
        kv_made, summed, y_done = sem("kv_made"), sem("summed"), sem("y_done")
        scanned = [sem(f"scanned{n}") for n in range(2)]
        y_added = [sem(f"y_added{n}") for n in range(2)]
        up_ps, silu_made, prod_made, hid_h_made, hid_made, down_ps, combined = (
            sem(n) for n in ("up_ps", "silu_made", "prod_made", "hid_h_made", "hid_made", "down_ps", "combined"))
        NHID = NB * HT0
        NY = NB * TT
        rows = [P] * (HT0 - 1) + [HALF]
        view = "(p k) t -> p k t"
        rkw_rows = scratch["rkw"].rearrange("n (p k) t -> k p n t", k=K)
        v_rows = scratch["v"].rearrange(view, k=K)
        y_rows = scratch["y"].rearrange(view, k=K)

        block = ctx.enter_context(nc.Block())

        @block.sync
        def _(sp):
            with sp.Fori(0, E0) as e:
                sp.wait_ge(up_made, e)
                sp.dma_start(up_raw[:], a["ffn_up"][e]).then_inc(up_in, 16)
                sp.wait_ge(down_made, e)
                sp.dma_start(down_raw[:], a["ffn_down"][e]).then_inc(down_in, 16)
            for tb in range(NB):
                sp.wait_ge(combined, (E0 - 1) * NY + (tb + 1) * TT)
                tiles = slice(tb * TT, (tb + 1) * TT)
                sp.dma_start(scratch["ffn"][:, tiles], ffn[:, tiles]).then_inc(ffn_stored, 16)
            sp.wait_ge(ffn_stored, 16 * NB)

        @block.gpsimd
        def _(pool):
            pool.dma_start(ffn[:].rearrange("p (b t) n -> p b t n", t=TT), a["x"].rearrange("b p t n -> p b t n"))\
                .then_inc(x_in, 16)
            pool.memset(bwd[:], 0.0).then_inc(cleared, 1)
            pool.memset(hid_h[:, :, HT0 - 1], 0.0).then_inc(cleared, 1)
            pool.memset(hid_l[:, :, HT0 - 1], 0.0).then_inc(cleared, 1)
            for half in range(2):
                if half:
                    pool.wait_ge(y_stored, 16)
                pool.memset(y[:], 0.0).then_inc(cleared, 1)
                if half:
                    pool.wait_ge(kv_made, KR * NCH)
                pool.dma_start(v[:], v_rows[:, half * VH:(half + 1) * VH, :]).then_inc(v_in, 16)
                pool.wait_ge(v_in, 16 * half + 16)
                with pool.Fori(0, KR) as i:
                    rnd = half * KR + i

                    def low(n):
                        r = rows[n % HT0]
                        pool.wait_ge(hid_h_made, rnd * NHID + n + 1)
                        slot = (n // HT0) % 2
                        pool.tensor_tensor(hid_l[0:r, slot, n % HT0], prod[0:r, n % 3], hid_h[0:r, slot, n % HT0],
                                           ALU.subtract).then_inc(hid_made, 1)

                    def outer(n):
                        s, q = n // CK, n % CK
                        if q == 0:
                            if s == 0:
                                load(0)
                            if s < 3:
                                load(s + 1)
                            pool.wait_ge(rkw_in[s % 2], 32 * rnd + 16 * (s // 2) + 16)
                        pool.wait_ge(scanned[n % 2], VQ * NCH * rnd + 2 * VQ * (n // 2))
                        key = rkw[:, s % 2, 1, :].rearrange("p (o t) -> p o t", o=1).broadcast_to([P, VQ, T])
                        pool.tensor_tensor(kv[:, n % 2], key, v[:, q * VQ:(q + 1) * VQ, :], ALU.mult)\
                            .then_inc(kv_made, 1)

                    def load(s):
                        pool.wait_ge(y_added[s % 2], 2 * CK * rnd + CK * (s // 2))
                        pool.dma_start(rkw[:, s % 2], rkw_rows[4 * i + s]).then_inc(rkw_in[s % 2], 16)

                    outer(0)
                    pool.wait_ge(up_h_made, rnd + 1)
                    pool.tensor_tensor(up_l[:], up_raw[:], up_h[:], ALU.subtract).then_inc(up_made, 1)
                    pool.wait_ge(down_h_made, rnd + 1)
                    pool.tensor_tensor(down_l[:], down_raw[:], down_h[:], ALU.subtract).then_inc(down_made, 1)
                    for tb in range(NB):
                        for m in range(HT0):
                            low(tb * HT0 + m)
                            if m == 0:
                                outer(2 * tb + 1)
                            if m == 3 and tb < NB - 1:
                                outer(2 * tb + 2)

        @block.vector
        def _(dve):
            dve.wait_ge(x_in, 16)
            for half in range(2):
                dve.wait_ge(cleared, 4 + half)
                with dve.Fori(0, KR) as i:
                    rnd = half * KR + i

                    def hidden(tb, m):
                        n = tb * HT0 + m
                        r = rows[m]
                        dve.wait_ge(silu_made, rnd * NHID + n + 1)
                        dve.wait_ge(hid_made, at(rnd, NHID, n - 2))
                        up = bank[3 + n % 3][:] if r == P else bank[n % 3][HALF:P, :]
                        dve.tensor_tensor(prod[0:r, n % 3, :], silu[0:r, n % 2, :], up, ALU.mult)\
                           .then_inc(prod_made, 1)

                    def scan(n, step):
                        s, q = n // CK, n % CK
                        k_row = rkw[:, s % 2]
                        k_base = 2 * CK * rnd + CK * (s // 2)
                        if step < VQ:
                            if step == 0:
                                dve.wait_ge(kv_made, rnd * NCH + n + 1)
                                if q:
                                    dve.wait_ge(y_added[s % 2], k_base + q)
                                elif s:
                                    dve.wait_ge(y_added[(s - 1) % 2], 2 * CK * rnd + CK * ((s - 1) // 2) + CK)
                                else:
                                    dve.wait_ge(y_added[1], 2 * CK * rnd)
                            dve.tensor_tensor_scan(fwd[:, step, :], k_row[:, 2, :], kv[:, n % 2, step, :], 0.0,
                                                   ALU.mult, ALU.add).then_inc(scanned[n % 2], 1)
                            dve.tensor_tensor_scan(bwd[:, step, T - 2::-1], kv[:, n % 2, step, T - 1:0:-1],
                                                   k_row[:, 2, T - 1:0:-1], 0.0, ALU.add, ALU.mult)\
                               .then_inc(scanned[n % 2], 1)
                        elif step == VQ:
                            dve.wait_ge(scanned[n % 2], VQ * NCH * rnd + 2 * VQ * (n // 2) + 2 * VQ)
                            dve.tensor_tensor(fwd[:], fwd[:], bwd[:], ALU.add).then_inc(summed, 1)
                            dve.wait_ge(summed, 2 * (rnd * NCH + n) + 1)
                            rr = k_row[:, 0, :].rearrange("p (o t) -> p o t", o=1).broadcast_to([P, VQ, T])
                            dve.tensor_tensor(fwd[:], fwd[:], rr, ALU.mult).then_inc(summed, 1)
                        else:
                            dve.wait_ge(summed, 2 * (rnd * NCH + n) + 2)
                            part = y[:, q * VQ:(q + 1) * VQ, :]
                            dve.tensor_tensor(part, part, fwd[:], ALU.add).then_inc(y_added[s % 2], 1)

                    def combine(tb):
                        for t in range(TT):
                            n = tb * TT + t
                            dve.wait_ge(down_ps, rnd * NY + n + 1)
                            dve.wait_ge(combined, rnd * NY)
                            row = ffn[:, n, :]
                            dve.scalar_tensor_tensor(row, bank[6 + n % 2][:, 0:D], w0[:, n, bass.ds(rnd, 1)], row,
                                                     ALU.mult, ALU.add).then_inc(combined, 1)

                    spread = [[(0, 0)], [(0, 1)], [(0, 2)], [(0, 3), (1, 0)], [(1, 1)], [(1, 2), (1, 3)]]
                    for tb in range(NB):
                        for m in range(HT0):
                            hidden(tb, m)
                            for chunk, step in spread[m]:
                                scan(2 * tb + chunk, step)
                        if tb:
                            combine(tb - 1)
                    combine(NB - 1)
                for slot in range(2):
                    dve.wait_ge(y_added[slot], (half + 1) * KR * 2 * CK)
                dve.nop().then_inc(y_done, 1)

        @block.scalar
        def _(act):
            for half in range(2):
                with act.Fori(0, KR) as i:
                    rnd = half * KR + i
                    act.wait_ge(up_in, 16 * rnd + 16)
                    act.wait_ge(up_ps, rnd * NHID)
                    act.activation(up_h[:], up_raw[:], ACT.Copy).then_inc(up_h_made, 1)
                    act.wait_ge(down_in, 16 * rnd + 16)
                    act.wait_ge(down_ps, rnd * NY)
                    act.activation(down_h[:], down_raw[:], ACT.Copy).then_inc(down_h_made, 1)
                    for n in range(NHID + 1):
                        if n < NHID:
                            r = rows[n % HT0]
                            act.wait_ge(up_ps, rnd * NHID + n + 1)
                            act.wait_ge(prod_made, at(rnd, NHID, n - 1))
                            act.activation(silu[0:r, n % 2, :], bank[n % 3][0:r, :], ACT.Silu)\
                               .then_inc(silu_made, 1)
                        if n:
                            k = n - 1
                            r = rows[k % HT0]
                            act.wait_ge(prod_made, rnd * NHID + k + 1)
                            act.wait_ge(down_ps, at(rnd, NY, (k // HT0 - 1) * TT))
                            act.activation(hid_h[0:r, (k // HT0) % 2, k % HT0], prod[0:r, k % 3, :], ACT.Copy)\
                               .then_inc(hid_h_made, 1)
                act.wait_ge(y_done, half + 1)
                act.dma_start(y_rows[:, half * VH:(half + 1) * VH, :], y[:]).then_inc(y_stored, 16)
            act.wait_ge(y_stored, 32)

        @block.tensor
        def _(pe):
            pe.wait_ge(cleared, 3)
            with pe.Fori(0, E0) as e:
                def three(ps, wh, wl, xs, first, last):
                    for n, (w, x) in enumerate(((wh, xs[0]), (wh, xs[1]), (wl, xs[0]))):
                        ins = pe.matmul(ps, w, x, start=first and n == 0, stop=last and n == 2)
                    return ins

                def up(tb):
                    for m in range(HT0):
                        n = tb * HT0 + m
                        pe.wait_ge(prod_made, at(e, NHID, n - 2))
                        for j, tile in enumerate([m, HT0 + m] if m < HT0 - 1 else [HT0 - 1]):
                            cols = slice(tile * P, (tile + 1) * P)
                            for c in range(C2):
                                toks = slice(tb * T, (tb + 1) * T)
                                ins = three(bank[3 * j + n % 3][:], up_h[:, c, cols], up_l[:, c, cols],
                                            (xh[:, c, toks], xl[:, c, toks]), c == 0, c == C2 - 1)
                        ins.then_inc(up_ps, 1)

                def down(tb):
                    pe.wait_ge(hid_made, e * NHID + (tb + 1) * HT0)
                    for t in range(TT):
                        n = tb * TT + t
                        pe.wait_ge(combined, at(e, NY, n - 1))
                        cols = slice(t * P, (t + 1) * P)
                        for m in range(HT0):
                            hs = (hid_h[:, tb % 2, m, cols], hid_l[:, tb % 2, m, cols])
                            ws = (down_h[:, m], down_l[:, m])
                            for k, (hp, wp) in enumerate(((0, 0), (0, 1), (1, 0))):
                                ins = pe.matmul(bank[6 + n % 2][:, 0:D], hs[hp], ws[wp],
                                                start=m == 0 and k == 0, stop=m == HT0 - 1 and k == 2)
                        ins.then_inc(down_ps, 1)

                pe.wait_ge(up_made, e + 1)
                for tb in range(NB):
                    up(tb)
                    if tb == 1:
                        pe.wait_ge(down_made, e + 1)
                    if tb:
                        down(tb - 1)
                down(NB - 1)


def layer_one(nc, a, scratch, keep, out):
    with ExitStack() as ctx:
        def sb(name, shape, dt=F32):
            return ctx.enter_context(nc.sbuf_tensor("b3_" + name, shape, dt))

        def sem(name):
            return ctx.enter_context(nc.semaphore("b3_" + name))

        bank = [ctx.enter_context(nc.psum_tensor(f"b3_bank{n}", [P, 512], F32)) for n in range(8)]
        ident = keep["ident"]
        NH = H * TT
        QK, QKV = 320, 384
        NQ = QK // K
        identb = sb("identb", [P, P], BF16)
        causal = sb("causal", [P, P], BF16)
        window = sb("window", [P, P + 64], BF16)
        rope = sb("rope", [P, 2, 2, TT, K])
        slot_of = sb("slot_of", [P, 8])
        eps = sb("eps", [P, 16])
        sel = sb("sel", [48, RT1, P], BF16)
        before16 = sb("before16", [P, E1 * E1])
        before4 = sb("before4", [P, G4 * G4])
        bias_r = sb("bias_r", [P, E1])
        ln_wb = sb("ln_wb", [P, 2, C2])
        norm_w = sb("norm_w", [P, 2, C2])
        wo0 = sb("rwkv_wo", [P, C2, D])
        wq = [sb(f"wq{n}", [P, C2, QKV if n else D]) for n in range(2)]
        wd = sb("wd", [P, C2, LAT])
        kv_up = sb("kv_up", [LAT, P])
        wo = [sb(f"attn_wo{n}", [P, C2, D]) for n in range(2)]
        route_w = sb("route_w", [P, C2, E1])
        up_h = sb("up_h", [P, 2, C2, MT1 * P], F16)
        up_l = sb("up_l", [P, 2, C2, MT1 * P], F16)
        down_h = sb("down_h", [P, MT1, D], F16)
        down_l = sb("down_l", [P, MT1, D], F16)
        y = sb("y", [P, C2, T])
        gate = sb("gate", [P, C2, T])
        g = sb("g", [P, C2, T])
        x_tok = sb("x_tok", [P, TT, D])
        g1 = sb("g1", [P, TT * D])
        g2 = sb("g2", [P, TT * D])
        w1 = sb("w1", [P, TT * QK])
        w2 = sb("w2", [P, TT * QK])
        qk = sb("qk", [P, TT, QKV])
        gn = sb("gn", [P, 4, NH])
        small = sb("small", [P, 5, NH])
        qn = sb("qn", [P, 3, TT * NQ])
        x1 = sb("x1", [P, TT, D])
        acc = sb("acc", [P, TT, D])
        stats = sb("stats", [P, TT, 6])
        mv = sb("mv", [P, TT, 2])
        rstd = sb("rstd", [P, 2, TT])
        xn = sb("xn", [P, TT, D])
        xT = sb("xT", [P, C2, T])
        xh = sb("xh", [P, C2, T], F16)
        xl = sb("xl", [P, C2, T], F16)
        holds_wait = sb("holds_wait", [P, 3])
        arena = sb("arena", [P, 26 * T + 4 * T + 384 * 4])
        th = sb("th", [P, 2, T])
        prod = sb("prod", [P, 2, T])
        ss = sb("ss", [P, 2, TT])
        rs = sb("rs", [P, 2, 2, TT])
        qkv = sb("qkv", [P, TT, QKV])
        qT = sb("qT", [P, C2, T])
        kT = sb("kT", [P, T])
        v1 = sb("v1", [P, TT, KVH, 32])
        den = sb("den", [P, 4, NH // 4])
        sc = sb("sc", [P, TT, E1])
        cbp = sb("cbp", [P, TT, 3, E1], BF16)
        cbT = sb("cbT", [48, T], BF16)

        hid_h = arena[:, 0:MT1 * T // 2].bitcast(BF16).rearrange("p (m t) -> p m t", t=T)
        hid_l = arena[:, MT1 * T // 2:MT1 * T].bitcast(F16).rearrange("p (m t) -> p m t", t=T)
        KZ = MT1 * T
        kz = arena[:, KZ:KZ + 8 * T].rearrange("p (m t) -> p m t", t=T)
        PR = KZ + 8 * T
        prob = [arena[:, PR:PR + 4 * T].rearrange("p (h t) -> p h t", t=T),
                arena[:, PR + 4 * T:PR + 4 * T + 4 * 384].rearrange("p (h t) -> p h t", t=384)]
        up_raw = arena[:, 0:2 * C2 * MT1 * P].rearrange("p (n c m) -> p n c m", n=2, c=C2)
        RAW = 2 * C2 * MT1 * P
        down_raw = arena[:, RAW:RAW + MT1 * D].rearrange("p (m n) -> p m n", n=D)
        yt = g1[:].rearrange("p (n d) -> p n d", d=K)
        ysq = g2[:].rearrange("p (n d) -> p n d", d=K)
        yl = g2[:].rearrange("p (c t) -> p c t", t=T)
        o_tok = qk[:].rearrange("p t n -> p (t n)")[:, 0:TT * D].rearrange("p (t n) -> p t n", n=D)
        onT = qT
        oT = kT
        xb = g1[:].rearrange("p (t n) -> p t n", n=D)
        lat = prod[0:LAT, 1]
        sq = th[:, 0, 0:D]
        rk = w1[:, TT * E1 * E1:TT * E1 * E1 + 4 * TT * E1].rearrange("p (s n) -> p s n", s=4)
        sbias = w2[:, TT * E1 * E1:TT * E1 * E1 + TT * E1]
        crest = w2[:, TT * E1 * E1 + TT * E1:TT * E1 * E1 + 2 * TT * E1].rearrange("p (t e) -> p t e", e=E1)

        names = ("weights_in", "raw_in", "setup", "ones_made", "wh_made", "wl_made", "y_in", "gate_in", "g_in",
                 "x_in", "ya_made", "yT_ps", "yt_out", "gn_var", "gn_std", "yn_made", "ynT_ps", "yl_made",
                 "ag_made", "wo_ps", "x1_made", "ln_var", "ln_sum", "ln_std", "xn_made", "xT_ps", "xT_out", "xl_made",
                 "route_ps", "sc_out", "cb_made", "cbT_ps", "cbT_out", "up_ps", "tanh_made", "gated", "prod_made",
                 "cb_ps", "hid_made", "hid_h_made", "hid_l_made", "fy_ps", "fy_used", "ss_made", "rs_sum", "rs_made",
                 "xbT_ps", "xbT_out", "lat_ps", "lat_out", "qkv_ps", "qkv_out", "qn_sum", "qn_std",
                 "qk_made", "v_made", "qkT_ps", "qkT_out", "kz_made", "score_ps", "exp_out", "pv_ps", "oT_out",
                 "ot_ps", "o_made", "onT_ps", "onT_out", "ao_ps", "xb_made", "acc_made", "fin_made", "stored")
        s = {n: sem(n) for n in names}
        own_head, own_sem = sem("dve_own_head"), sem("dve_own")

        ORDER = list(range(RT1, MT1)) + list(range(RT1))
        NSH = MT1 - RT1
        groups = []
        for layer in range(2):
            for j in range(4):
                for i in range(TT):
                    width = T - P * i if layer == 0 else min(P + 64, T - P * i)
                    per = 4 if 4 * width <= 512 else 2 if 2 * width <= 512 else 1
                    for g0 in range(0, KVH, per):
                        groups.append((layer, j, i, list(range(g0, g0 + per)), P * i, width))
        NG = len(groups)

        def groups_of(layer, j, i):
            return [(n, x[3], x[4], x[5]) for n, x in enumerate(groups) if x[:3] == (layer, j, i)]

        def groups_until(layer, j, i):
            return sum(1 for x in groups if x[:3] <= (layer, j, i))

        block = ctx.enter_context(nc.Block())

        loads = [(identb[:], "c_identb"), (causal[:], "c_causal"), (window[:], "c_window"), (rope[:], "c_rope"),
                 (slot_of[:], "c_slot"), (eps[:], "c_eps"), (sel[:], "c_sel"), (before16[:], "c_before16"),
                 (before4[:], "c_before4"), (bias_r[:], "bias_r"), (ln_wb[:], "ln_wb"), (norm_w[:], "norm_w"),
                 (wo0[:], "Wo"), (wq[0][:], "g_wq"), (wq[1][:], "l_wqkv"), (wd[:], "g_kv_down"),
                 (kv_up[:], "g_kv_up"), (wo[0][:], "g_wo"), (wo[1][:], "l_wo"), (route_w[:], "router_w")]
        LOADED = 16 * len(loads)
        SETUP = 3 * C2

        @block.sync
        def _(sp):
            chan = "(b c p) t -> b p c t"

            def load_head(n):
                sp.wait_ge(s["yT_ps"], TT * n)
                sp.dma_start(y[:], scratch["y"].rearrange(chan, c=C2, p=P)[n]).then_inc(s["y_in"], 16)
                sp.dma_start(gate[:], scratch["gate"].rearrange(chan, c=C2, p=P)[n]).then_inc(s["gate_in"], 16)
                sp.wait_ge(s["ag_made"], 2 * n)
                sp.dma_start(g[:], scratch["g"].rearrange(chan, c=C2, p=P)[n]).then_inc(s["g_in"], 16)
                sp.wait_ge(s["x1_made"], 2 * n)
                sp.dma_start(x_tok[:], scratch["ffn"][:, bass.ds(n * TT, TT), :]).then_inc(s["x_in"], 16)

            def store(b):
                sp.wait_ge(s["fin_made"], 2 * b + 2)
                sp.dma_start(out[b], acc[:]).then_inc(s["stored"], 16)

            load_head(0)
            for dst, name in loads:
                sp.dma_start(dst, a[name]).then_inc(s["weights_in"], 16)
            sp.dma_start(up_raw, a["ffn1_up"]).then_inc(s["raw_in"], 16)
            sp.dma_start(down_raw, a["ffn1_down"]).then_inc(s["raw_in"], 16)
            with sp.Fori(0, NB - 1) as b:
                load_head(b + 1)
                store(b)
            store(NB - 1)
            sp.wait_ge(s["stored"], 16 * NB)

        @block.gpsimd
        def _(pool):
            pool.memset(v1[:], 1.0).then_inc(s["ones_made"], 1)
            pool.wait_ge(s["ones_made"], 1)
            pool.wait_ge(s["weights_in"], LOADED)

            def gate_heads(n):
                pool.wait_ge(s["g_in"], 16 * n + 16)
                for c in range(C2):
                    pool.wait_ge(s["yl_made"], 2 * n + c + 1)
                    pool.tensor_tensor(yl[:, c], yl[:, c], g[:, c], ALU.mult).then_inc(s["ag_made"], 1)

            def layer_norm_factor(n):
                pool.wait_ge(s["ln_var"], n + 1)
                pool.wait_ge(s["xn_made"], TT * n)
                pool.tensor_tensor(rstd[:, 0], mv[:, :, 1], eps[:, 4:8], ALU.add).then_inc(s["ln_sum"], 1)
                pool.wait_ge(s["ln_sum"], n + 1)
                pool.tensor_tensor(rstd[:, 1], rstd[:, 0], eps[:, 12:16], ALU.pow).then_inc(s["ln_std"], 1)

            def rms_factor(layer, count, n):
                pool.wait_ge(s["ss_made"], 2 * TT * n + TT * layer + TT)
                pool.wait_ge(s["qkv_out"], count)
                pool.tensor_tensor(rs[:, layer, 0], ss[:, layer], eps[:, 8:12], ALU.add).then_inc(s["rs_sum"], 1)
                pool.wait_ge(s["rs_sum"], 2 * n + layer + 1)
                pool.tensor_tensor(rs[:, layer, 1], rs[:, layer, 0], eps[:, 12:16], ALU.pow)\
                    .then_inc(s["rs_made"], 1)

            def low_x(n):
                for c in range(C2):
                    pool.wait_ge(s["xT_out"], 4 * n + 2 * c + 2)
                    pool.wait_ge(s["up_ps"], MT1 * n)
                    pool.tensor_tensor(xl[:, c], xT[:, c], xh[:, c], ALU.subtract).then_inc(s["xl_made"], 1)

            def low_hidden(b, n):
                pool.wait_ge(s["hid_h_made"], b * MT1 + n + 1)
                src = prod[:, n % 2]
                pool.tensor_tensor(hid_l[:, ORDER[n]], src, hid_h[:, ORDER[n]], ALU.subtract)\
                    .then_inc(s["hid_l_made"], 1)

            def values(b, layer):
                pool.wait_ge(s["qkv_out"], 8 * b + 4 * layer + 4)
                pool.wait_ge(s["pv_ps"], 32 * b + 16 * layer)
                pool.tensor_tensor(holds_wait[:, 1 + layer:2 + layer], eps[:, 0:1], eps[:, 0:1], ALU.add)
                pool.tensor_copy(v1[:, :, :, 0:K], qkv[:, :, QK:QKV].rearrange("p t (g d) -> p t g d", d=K))\
                    .then_inc(s["v_made"], 1)

            def head(n):
                gate_heads(n)
                layer_norm_factor(n)
                low_x(n)
                rms_factor(0, 8 * n, n)

            def body(b, more):
                for n in range(NSH):
                    low_hidden(b, n)
                    if n == 0:
                        values(b, 0)
                for n in range(NSH, MT1):
                    low_hidden(b, n)
                rms_factor(1, 8 * b, b)
                values(b, 1)
                pool.wait_ge(s["xb_made"], 2 * b + 2)
                pool.wait_ge(s["fy_used"], 2 * b + 2)
                pool.tensor_tensor(acc[:], acc[:], xb[:], ALU.add).then_inc(s["acc_made"], 1)
                if more:
                    head(b + 1)

            pool.wait_ge(s["wh_made"], 1)
            pool.tensor_tensor(up_l[:], up_raw, up_h[:], ALU.subtract).then_inc(s["wl_made"], 1)
            pool.wait_ge(s["wh_made"], 2)
            pool.tensor_tensor(down_l[:], down_raw, down_h[:], ALU.subtract).then_inc(s["wl_made"], 1)
            head(0)
            with pool.Fori(0, NB - 1) as b:
                body(b, True)
            body(NB - 1, False)

        each = "p (n o) -> p n o"

        @block.vector
        def _(dve):
            dve.wait_ge(s["weights_in"], LOADED)
            for c in range(C2):
                for w, layer in ((wq[0], 0), (wd, 0), (wq[1], 1)):
                    dve.tensor_scalar(w[:, c], w[:, c], norm_w[:, layer, c:c + 1], None, ALU.mult)\
                       .then_inc(s["setup"], 1)
            mine = Steps(dve, own_head, 13)
            own = Steps(dve, own_sem, 103)

            def gate_y(n):
                dve.wait_ge(s["y_in"], 16 * n + 16)
                dve.wait_ge(s["gate_in"], 16 * n + 16)
                for c in range(C2):
                    dve.scalar_tensor_tensor(y[:, c], gate[:, c], 1.0, y[:, c], ALU.add, ALU.mult)\
                       .then_inc(s["ya_made"], 1)

            mean, var, gstd, grstd = (gn[:, n] for n in range(4))

            def center_heads(n):
                mine.round(n)
                mine.settle()
                dve.wait_ge(s["yt_out"], 2 * n + 2)
                mine.add(dve.reduce_sum(mean, yt, AX))
                mine.settle()
                mine.add(dve.tensor_scalar(mean, mean, 1.0 / K, None, ALU.mult))
                mine.settle()
                mine.add(dve.tensor_tensor(yt, yt, mean.rearrange(each, o=1).broadcast_to([P, NH, K]), ALU.subtract))
                mine.settle()
                dve.wait_ge(s["wo_ps"], TT * n)
                mine.add(dve.tensor_tensor(ysq, yt, yt, ALU.mult))
                mine.settle()
                dve.reduce_sum(var, ysq, AX).then_inc(s["gn_var"], 1)

            def scale_heads(n):
                dve.wait_ge(s["gn_std"], n + 1)
                mine.add(dve.reciprocal(grstd, gstd))
                mine.settle()
                dve.tensor_tensor(yt, yt, grstd.rearrange(each, o=1).broadcast_to([P, NH, K]), ALU.mult)\
                   .then_inc(s["yn_made"], 1)

            def residual(n):
                dve.wait_ge(s["x_in"], 16 * n + 16)
                dve.wait_ge(s["fy_used"], 2 * n)
                for h in range(2):
                    dve.wait_ge(s["wo_ps"], TT * n + 2 * h + 2)
                    dve.tensor_tensor(x1[:, 2 * h:2 * h + 2], bank[4 + h][:].rearrange("p (t n) -> p t n", n=D),
                                      x_tok[:, 2 * h:2 * h + 2], ALU.add).then_inc(s["x1_made"], 1)
                dve.wait_ge(s["x1_made"], 2 * n + 2)
                for t in range(TT):
                    mine.add(dve.bn_stats(stats[:, t], x1[:, t]))
                mine.settle()
                mine.add(dve.memset(holds_wait[:, 0:1], 0.0))
                for t in range(TT):
                    ins = dve.bn_aggr(mv[:, t], stats[:, t])
                    if t < TT - 1:
                        mine.add(ins)
                ins.then_inc(s["ln_var"], 1)

            def norm(n):
                dve.wait_ge(s["ln_std"], n + 1)
                dve.wait_ge(s["xb_made"], 2 * n)
                for t in range(TT):
                    dve.tensor_scalar(xn[:, t], x1[:, t], mv[:, t, 0:1], rstd[:, 1, t:t + 1],
                                      ALU.subtract, ALU.mult).then_inc(s["xn_made"], 1)

            def rank_in(dst, scores, n, table, op_rows):
                oth = scores.rearrange("p m (o e) -> p m o e", o=1).broadcast_to([P, op_rows, n, n])
                its = scores.rearrange("p m (e o) -> p m e o", o=1).broadcast_to([P, op_rows, n, n])
                size = op_rows * n * n
                gt, eq = w1[:, 0:size], w2[:, 0:size]
                four = dict(m=op_rows, e=n, j=n)
                own.add(dve.tensor_tensor(gt.rearrange("p (m e j) -> p m e j", **four), oth, its, ALU.is_gt))
                own.add(dve.tensor_tensor(eq.rearrange("p (m e j) -> p m e j", **four), oth, its, ALU.is_equal))
                own.settle()
                rows = eq.rearrange("p (m n) -> p m n", n=n * n)
                own.add(dve.tensor_tensor(rows, rows, table.rearrange("p (o n) -> p o n", o=1)
                                          .broadcast_to([P, op_rows, n * n]), ALU.mult))
                own.settle()
                own.add(dve.tensor_tensor(gt, gt, eq, ALU.add))
                own.settle()
                own.add(dve.reduce_sum(dst, gt.rearrange("p (n j) -> p n j", j=n), AX))
                own.settle()

            def route(b):
                dve.wait_ge(s["sc_out"], b + 1)
                dve.wait_ge(s["cbT_ps"], b)
                own.add(dve.tensor_scalar(sc[:], sc[:], 0.5, 0.5, ALU.mult, ALU.add))
                own.settle()
                own.add(dve.tensor_tensor(sbias.rearrange("p (t e) -> p t e", e=E1), sc[:], bias_r[:].rearrange("p (o e) -> p o e", o=1)
                                          .broadcast_to([P, TT, E1]), ALU.add))
                own.settle()
                NGR, EG = TT * G4, E1 // G4
                flat = sbias
                in_groups = flat.rearrange("p (m e) -> p m e", e=EG)
                rank_in(rk[:, 0, :], in_groups, EG, before4[:], NGR)
                own.add(dve.scalar_tensor_tensor(rk[:, 1, :], rk[:, 0, :], 2.0, flat, ALU.is_lt, ALU.mult))
                own.settle()
                gsum, grank, gmask, gless = (small[:, n, 0:NGR] for n in range(4))
                own.add(dve.reduce_sum(gsum, rk[:, 1, :].rearrange("p (m e) -> p m e", e=EG), AX))
                own.settle()
                rank_in(grank, gsum.rearrange("p (t m) -> p t m", m=G4), G4, before4[:], TT)
                own.add(dve.tensor_scalar(gmask, grank, 2.0, None, ALU.is_lt))
                own.settle()
                own.add(dve.tensor_scalar(gless, gmask, 1e30, -1e30, ALU.mult, ALU.add))
                wide = "p (m o) -> p m o"
                inside = rk[:, 2, :].rearrange("p (m e) -> p m e", e=EG)
                own.add(dve.tensor_tensor(inside, in_groups,
                                          gmask.rearrange(wide, o=1).broadcast_to([P, NGR, EG]), ALU.mult))
                own.settle()
                own.add(dve.tensor_tensor(rk[:, 3, :].rearrange("p (m e) -> p m e", e=EG), inside,
                                          gless.rearrange(wide, o=1).broadcast_to([P, NGR, EG]), ALU.add))
                own.settle()
                rank_in(rk[:, 0, :], rk[:, 3, :].rearrange("p (t e) -> p t e", e=E1), E1, before16[:], TT)
                own.add(dve.scalar_tensor_tensor(rk[:, 1, :], rk[:, 0, :], 4.0,
                                                 sc[:].rearrange("p t e -> p (t e)"), ALU.is_lt, ALU.mult))
                own.settle()
                total = small[:, 4, 0:TT]
                own.add(dve.reduce_sum(total, rk[:, 1, :].rearrange("p (t e) -> p t e", e=E1), AX))
                own.settle()
                own.add(dve.tensor_scalar(total, total, 1e-20, None, ALU.add))
                own.settle()
                own.add(dve.reciprocal(small[:, 4, TT:2 * TT], total))
                own.settle()
                weight = rk[:, 2, :].rearrange("p (t e) -> p t e", e=E1)
                own.add(dve.tensor_tensor(weight, rk[:, 1, :].rearrange("p (t e) -> p t e", e=E1),
                                          small[:, 4, TT:2 * TT].rearrange("p (t o) -> p t o", o=1)
                                          .broadcast_to([P, TT, E1]), ALU.mult))
                own.settle()
                own.add(dve.tensor_copy(cbp[:, :, 0, :], weight))
                own.settle()
                own.add(dve.tensor_tensor(crest, weight, cbp[:, :, 0, :], ALU.subtract))
                own.settle()
                own.add(dve.tensor_copy(cbp[:, :, 1, :], crest))
                own.settle()
                dve.tensor_tensor(cbp[:, :, 2, :], crest, cbp[:, :, 1, :], ALU.subtract).then_inc(s["cb_made"], 1)

            def product(b, n):
                pair = 4 + 2 * (n % 2)
                dve.wait_ge(s["tanh_made"], b * MT1 + n + 1)
                dve.wait_ge(s["hid_l_made"], at(b, MT1, n - 1))
                dve.scalar_tensor_tensor(prod[:, n % 2], th[:, n % 2], 1.0, bank[pair][:], ALU.add, ALU.mult)\
                   .then_inc(s["gated"], 1)
                dve.wait_ge(s["gated"], b * MT1 + n + 1)
                dve.tensor_tensor(prod[:, n % 2], prod[:, n % 2], bank[pair + 1][:], ALU.mult)\
                   .then_inc(s["prod_made"], 1)

            def weigh(b, n):
                dve.wait_ge(s["cb_ps"], b * RT1 + ORDER[n] + 1)
                dve.wait_ge(s["prod_made"], b * MT1 + n + 1)
                dve.tensor_tensor(prod[:, n % 2], prod[:, n % 2], bank[4 + 2 * (n % 2)][:], ALU.mult)\
                   .then_inc(s["hid_made"], 1)

            def experts_out(b):
                for h in range(2):
                    for t in range(2 * h, 2 * h + 2):
                        dve.wait_ge(s["fy_ps"], TT * b + t + 1)
                        dve.wait_ge(s["stored"], 16 * b)
                        ins = dve.scalar_tensor_tensor(acc[:, t], bank[4 + t][:, 0:D], 0.5, x1[:, t],
                                                       ALU.mult, ALU.add)
                        if t % 2 == 0:
                            own.add(ins)
                    ins.then_inc(s["fy_used"], 1)

            a_all = w1[:].rearrange("p (t n) -> p t n", n=QK)
            b_all = w2[:].rearrange("p (t n) -> p t n", n=QK)
            heads16 = "p (n d) -> p n d"

            def rotate(b, layer, t):
                if t == 0:
                    own.settle()
                dve.wait_ge(s["qkv_out"], 8 * b + 4 * layer + t + 1)
                cos, sin = (rope[:, layer, n, t].rearrange("p (o d) -> p o d", o=1).broadcast_to([P, NQ, K])
                            for n in range(2))
                own.add(dve.tensor_tensor(a_all[:, t].rearrange(heads16, d=K),
                                          qkv[:, t, 0:QK].rearrange(heads16, d=K), cos, ALU.mult))
                pairs = "p (n m two) -> p n m two"
                sin4 = rope[:, layer, 1, t].rearrange("p (o m two) -> p o m two", o=1, two=2)\
                    .broadcast_to([P, NQ, K // 2, 2])
                for e in range(2):
                    own.add(dve.tensor_tensor(
                        b_all[:, t].rearrange(pairs, m=K // 2, two=2)[:, :, :, e],
                        qkv[:, t, 0:QK].rearrange(pairs, m=K // 2, two=2)[:, :, :, 1 - e],
                        sin4[:, :, :, e], ALU.mult))

            def rotated(b, layer):
                own.settle()
                own.add(dve.tensor_tensor(w1[:], w1[:], w2[:], ALU.add))
                own.settle()

            def square_sums(b, layer):
                own.add(dve.tensor_tensor(w2[:], w1[:], w1[:], ALU.mult))
                own.settle()
                dve.reduce_sum(qn[:, 0], w2[:].rearrange(heads16, d=K), AX).then_inc(s["qn_sum"], 1)

            def norm_qk(b, layer):
                L2 = 2 * b + layer
                dve.wait_ge(s["qn_std"], L2 + 1)
                dve.wait_ge(s["onT_ps"], 2 * L2)
                own.add(dve.reciprocal(qn[:, 2], qn[:, 1]))
                own.settle()
                for t in range(TT):
                    own.add(dve.tensor_tensor(
                        qk[:, t, 0:QK].rearrange(heads16, d=K), a_all[:, t].rearrange(heads16, d=K),
                        qn[:, 2, NQ * t:NQ * t + NQ].rearrange(each, o=1).broadcast_to([P, NQ, K]), ALU.mult))
                own.settle()
                dve.tensor_copy(qk[:, :, QK:QKV], qk[:, :, D:QK]).then_inc(s["qk_made"], 1)

            def mask_k(b, layer):
                dve.wait_ge(s["qkT_out"], 6 * b + 3 * layer + 3)
                for n in range(8):
                    dve.tensor_scalar(kz[:, n], kT[:], slot_of[:, n:n + 1], None, ALU.mult)\
                       .then_inc(s["kz_made"], 1)

            def over_sums(b, layer, j):
                dve.wait_ge(s["ot_ps"], 8 * b + 4 * layer + j + 1)
                ps = bank[3][:].rearrange("p (n d) -> p n d", d=32)
                own.add(dve.reciprocal(den[:, j], ps[:, :, K]))
                own.settle()
                for t in range(TT):
                    ins = dve.tensor_tensor(
                        o_tok[:, t, 64 * j:64 * j + 64].rearrange("p (g d) -> p g d", d=K),
                        ps[:, 4 * t:4 * t + 4, 0:K],
                        den[:, j, 4 * t:4 * t + 4].rearrange(each, o=1).broadcast_to([P, 4, K]), ALU.mult)
                    if t < TT - 1:
                        own.add(ins)
                ins.then_inc(s["o_made"], 1)

            def attention_out(b, layer):
                for h in range(2):
                    dve.wait_ge(s["ao_ps"], 8 * b + 4 * layer + 2 * h + 2)
                    ps = bank[2 + h][:].rearrange("p (t n) -> p t n", n=D)
                    part = slice(2 * h, 2 * h + 2)
                    if layer == 0:
                        dve.wait_ge(s["acc_made"], b)
                        dve.wait_ge(s["ynT_ps"], 2 * b + 2)
                        dve.tensor_tensor(xb[:, part], ps, xn[:, part], ALU.add).then_inc(s["xb_made"], 1)
                    else:
                        dve.wait_ge(s["acc_made"], b + 1)
                        dve.tensor_tensor(acc[:, part], ps, acc[:, part], ALU.add).then_inc(s["fin_made"], 1)

            def body(b, more):
                own.round(b)
                for t in range(TT):
                    rotate(b, 0, t)
                rotated(b, 0)
                product(b, 0)
                square_sums(b, 0)
                product(b, 1)
                norm_qk(b, 0)
                product(b, 2)
                product(b, 3)
                mask_k(b, 0)
                route(b)
                for j in range(4):
                    if j:
                        over_sums(b, 0, j - 1)
                    product(b, NSH + 2 * j)
                    if j:
                        weigh(b, NSH + 2 * j - 1)
                    product(b, NSH + 2 * j + 1)
                    weigh(b, NSH + 2 * j)
                over_sums(b, 0, 3)
                weigh(b, MT1 - 1)
                attention_out(b, 0)
                for t in range(TT):
                    rotate(b, 1, t)
                rotated(b, 1)
                square_sums(b, 1)
                norm_qk(b, 1)
                experts_out(b)
                mask_k(b, 1)
                if more:
                    gate_y(b + 1)
                over_sums(b, 1, 0)
                if more:
                    center_heads(b + 1)
                over_sums(b, 1, 1)
                if more:
                    scale_heads(b + 1)
                over_sums(b, 1, 2)
                if more:
                    residual(b + 1)
                over_sums(b, 1, 3)
                if more:
                    norm(b + 1)
                    mine.end()
                attention_out(b, 1)
                own.end()

            gate_y(0)
            center_heads(0)
            scale_heads(0)
            residual(0)
            norm(0)
            mine.end()
            with dve.Fori(0, NB - 1) as b:
                body(b, True)
            body(NB - 1, False)

        @block.scalar
        def _(act):
            act.wait_ge(s["raw_in"], 32)
            act.activation(up_h[:].rearrange("p n c m -> p (n c m)"), up_raw.rearrange("p n c m -> p (n c m)"),
                           ACT.Copy).then_inc(s["wh_made"], 1)
            act.activation(down_h[:].rearrange("p m n -> p (m n)"), down_raw.rearrange("p m n -> p (m n)"),
                           ACT.Copy).then_inc(s["wh_made"], 1)
            act.wait_ge(s["weights_in"], LOADED)

            def half_y(n):
                for h in range(2):
                    act.wait_ge(s["yT_ps"], TT * n + 2 * h + 2)
                    act.wait_ge(s["ynT_ps"], 2 * n)
                    act.wait_ge(s["acc_made"], n)
                    act.activation(g1[:, 512 * h:512 * h + 512], bank[4 + h][:], ACT.Copy, scale=0.5)\
                       .then_inc(s["yt_out"], 1)

            def head_std(n):
                act.wait_ge(s["gn_var"], n + 1)
                act.wait_ge(s["yn_made"], n)
                act.activation(gn[:, 2], gn[:, 1], ACT.Sqrt, bias=eps[:, 0:1], scale=1.0 / K)\
                   .then_inc(s["gn_std"], 1)

            def affine(n):
                for c in range(C2):
                    act.wait_ge(s["ynT_ps"], 2 * n + c + 1)
                    act.wait_ge(s["wo_ps"], TT * n)
                    act.activation(yl[:, c], bank[6 + c][:], ACT.Identity, bias=ln_wb[:, 1, c:c + 1],
                                   scale=ln_wb[:, 0, c:c + 1]).then_inc(s["yl_made"], 1)

            def square_mean(layer, n, src, ready, count):
                for t in range(TT):
                    act.wait_ge(ready, count)
                    act.wait_ge(s["ss_made"], 2 * TT * n + TT * layer + t)
                    act.activation(sq, src[:, t], ACT.Square, scale=1.0 / 16.0,
                                   accum_out=ss[:, layer, t:t + 1]).then_inc(s["ss_made"], 1)

            assert D == 16 * 16

            def copy_xT(n):
                for c in range(C2):
                    act.wait_ge(s["xT_ps"], 2 * n + c + 1)
                    act.wait_ge(s["qkv_ps"], 8 * n)
                    act.wait_ge(s["up_ps"], MT1 * n)
                    act.wait_ge(s["xl_made"], 2 * n)
                    act.activation(xh[:, c], bank[6 + c][:], ACT.Copy).then_inc(s["xT_out"], 1)
                    act.activation(xT[:, c], bank[6 + c][:], ACT.Copy).then_inc(s["xT_out"], 1)

            def gate_tanh(b, n):
                act.wait_ge(s["up_ps"], b * MT1 + n + 1)
                act.wait_ge(s["gated"], at(b, MT1, n - 1))
                act.activation(th[:, n % 2], bank[4 + 2 * (n % 2)][:], ACT.Tanh, scale=0.5)\
                   .then_inc(s["tanh_made"], 1)

            def high_hidden(b, n):
                if n < NSH:
                    act.wait_ge(s["prod_made"], b * MT1 + n + 1)
                else:
                    act.wait_ge(s["hid_made"], b * RT1 + ORDER[n] + 1)
                act.wait_ge(s["fy_ps"], TT * b)
                act.activation(hid_h[:, ORDER[n]], prod[:, n % 2], ACT.Copy).then_inc(s["hid_h_made"], 1)

            def copy_qkv(b, layer):
                L2 = 2 * b + layer
                if layer == 0:
                    act.wait_ge(s["lat_ps"], b + 1)
                    act.wait_ge(s["hid_l_made"], MT1 * b)
                    act.activation(lat, bank[4][0:LAT, :], ACT.Copy).then_inc(s["lat_out"], 1)
                act.wait_ge(s["rs_made"], L2 + 1)
                act.wait_ge(s["v_made"], L2)
                for t in range(TT):
                    act.wait_ge(s["qkv_ps"], 4 * L2 + t + 1)
                    act.activation(qkv[:, t], bank[t][:, 0:QKV], ACT.Copy, scale=rs[:, layer, 1, t:t + 1])\
                       .then_inc(s["qkv_out"], 1)

            def qk_std(b, layer):
                act.wait_ge(s["qn_sum"], 2 * b + layer + 1)
                act.wait_ge(s["qk_made"], 2 * b + layer)
                act.activation(qn[:, 1], qn[:, 0], ACT.Sqrt, bias=eps[:, 2:3], scale=1.0 / K)\
                   .then_inc(s["qn_std"], 1)

            def copy_qkT(b, layer):
                L2 = 2 * b + layer
                for n in range(3):
                    act.wait_ge(s["qkT_ps"], 3 * L2 + n + 1)
                    act.wait_ge(s["kz_made"], 8 * L2)
                    act.wait_ge(s["ot_ps"], 4 * L2)
                    act.wait_ge(s["ao_ps"], 4 * L2)
                    dst = qT[:, n] if n < 2 else kT[:]
                    act.activation(dst, bank[n][:], ACT.Copy).then_inc(s["qkT_out"], 1)

            def exponentials(b, layer, j, i):
                for n, heads, start, width in groups_of(layer, j, i):
                    act.wait_ge(s["score_ps"], b * NG + n + 1)
                    act.wait_ge(s["pv_ps"], at(b, 32, 16 * layer + 4 * j + i - 1))
                    src = bank[n % 2][:, 0:len(heads) * width].rearrange("p (h t) -> p h t", t=width)
                    act.activation(prob[i % 2][:, heads[0]:heads[0] + len(heads), 0:width], src, ACT.Exp,
                                   scale=0.25).then_inc(s["exp_out"], 1)

            def copy_oT(b, layer, j):
                act.wait_ge(s["pv_ps"], 32 * b + 16 * layer + 4 * j + 4)
                act.wait_ge(s["ot_ps"], 8 * b + 4 * layer + j)
                act.wait_ge(s["kz_made"], 16 * b + 8 * layer + 8)
                act.activation(oT[:], bank[2][:], ACT.Copy).then_inc(s["oT_out"], 1)

            def copy_onT(b, layer):
                for c in range(C2):
                    act.wait_ge(s["onT_ps"], 4 * b + 2 * layer + c + 1)
                    act.activation(onT[:, c], bank[c][:], ACT.Copy).then_inc(s["onT_out"], 1)

            def body(b, more):
                act.wait_ge(s["route_ps"], b + 1)
                act.wait_ge(s["cb_made"], b)
                copy_qkv(b, 0)
                act.activation(sc[:], bank[7][:, 0:TT * E1].rearrange("p (t e) -> p t e", e=E1), ACT.Tanh, scale=0.5)\
                   .then_inc(s["sc_out"], 1)
                gate_tanh(b, 0)
                gate_tanh(b, 1)
                high_hidden(b, 0)
                qk_std(b, 0)
                gate_tanh(b, 2)
                high_hidden(b, 1)
                gate_tanh(b, 3)
                high_hidden(b, 2)
                copy_qkT(b, 0)
                high_hidden(b, 3)
                for j in range(4):
                    exponentials(b, 0, j, 0)
                    if j:
                        copy_oT(b, 0, j - 1)
                    exponentials(b, 0, j, 1)
                    if j == 0:
                        act.wait_ge(s["cbT_ps"], b + 1)
                        act.activation(cbT[:], bank[3][0:48, 0:T // 2].bitcast(BF16), ACT.Copy)\
                           .then_inc(s["cbT_out"], 1)
                    gate_tanh(b, NSH + 2 * j)
                    exponentials(b, 0, j, 2)
                    if j:
                        high_hidden(b, NSH + 2 * j - 1)
                    exponentials(b, 0, j, 3)
                    gate_tanh(b, NSH + 2 * j + 1)
                    high_hidden(b, NSH + 2 * j)
                copy_oT(b, 0, 3)
                high_hidden(b, MT1 - 1)
                copy_onT(b, 0)
                square_mean(1, b, xb, s["xb_made"], 2 * b + 2)
                for c in range(C2):
                    act.wait_ge(s["xbT_ps"], 2 * b + c + 1)
                    act.activation(xT[:, c], bank[c][:], ACT.Copy).then_inc(s["xbT_out"], 1)
                copy_qkv(b, 1)
                qk_std(b, 1)
                copy_qkT(b, 1)
                if more:
                    half_y(b + 1)
                for j in range(4):
                    exponentials(b, 1, j, 0)
                    if j:
                        copy_oT(b, 1, j - 1)
                    for i in range(1, TT):
                        exponentials(b, 1, j, i)
                    if more and j == 1:
                        head_std(b + 1)
                    if more and j == 2:
                        affine(b + 1)
                copy_oT(b, 1, 3)
                if more:
                    square_mean(0, b + 1, xn, s["xn_made"], TT * (b + 1) + TT)
                    copy_xT(b + 1)
                copy_onT(b, 1)

            half_y(0)
            head_std(0)
            affine(0)
            square_mean(0, 0, xn, s["xn_made"], TT)
            copy_xT(0)
            with act.Fori(0, NB - 1) as b:
                body(b, True)
            body(NB - 1, False)

        @block.tensor
        def _(pe):
            pe.wait_ge(s["weights_in"], LOADED)
            pe.wait_ge(s["setup"], SETUP)

            def turn_y(n):
                pe.wait_ge(s["ya_made"], 2 * n + 2)
                pe.wait_ge(s["fy_used"], 2 * n)
                for t in range(TT):
                    for c in range(C2):
                        at_col = (t % 2) * D + c * P
                        ins = pe.transpose(bank[4 + t // 2][:, at_col:at_col + P], y[:, c, t * P:(t + 1) * P],
                                           ident[:])
                    ins.then_inc(s["yT_ps"], 1)

            def turn_yn(n):
                pe.wait_ge(s["yn_made"], n + 1)
                ytok = g1[:].rearrange("p (t n) -> p t n", n=D)
                for c in range(C2):
                    for t in range(TT):
                        ins = pe.transpose(bank[6 + c][:, t * P:(t + 1) * P], ytok[:, t, c * P:(c + 1) * P], ident[:])
                    ins.then_inc(s["ynT_ps"], 1)

            def rwkv_out(n):
                pe.wait_ge(s["ag_made"], 2 * n + 2)
                for t in range(TT):
                    for c in range(C2):
                        ins = pe.matmul(bank[4 + t // 2][:, (t % 2) * D:(t % 2) * D + D],
                                        yl[:, c, t * P:(t + 1) * P], wo0[:, c], start=c == 0, stop=c == C2 - 1)
                    ins.then_inc(s["wo_ps"], 1)

            def turn_x(n):
                for c in range(C2):
                    for t in range(TT):
                        if c == 0:
                            pe.wait_ge(s["xn_made"], TT * n + t + 1)
                        ins = pe.transpose(bank[6 + c][:, t * P:(t + 1) * P], xn[:, t, c * P:(c + 1) * P], ident[:])
                    ins.then_inc(s["xT_ps"], 1)

            def three(ps, wh, wl, vh, vl, first, last):
                for n, (w, v) in enumerate(((wh, vh), (wh, vl), (wl, vh))):
                    ins = pe.matmul(ps, w, v, start=first and n == 0, stop=last and n == 2)
                return ins

            def scores_of_experts(b):
                pe.wait_ge(s["xT_out"], 4 * b + 4)
                for t in range(TT):
                    for c in range(C2):
                        ins = pe.matmul(bank[7][:, t * E1:(t + 1) * E1], xT[:, c, t * P:(t + 1) * P],
                                        route_w[:, c, :], start=c == 0, stop=c == C2 - 1)
                ins.then_inc(s["route_ps"], 1)

            def up(b, n):
                m = ORDER[n]
                pair = 4 + 2 * (n % 2)
                if n >= 2 + NSH:
                    pe.wait_ge(s["hid_made"], b * RT1 + n - 2 - NSH + 1)
                else:
                    pe.wait_ge(s["prod_made"], at(b, MT1, n - 1))
                if n == 0:
                    pe.wait_ge(s["xl_made"], 2 * b + 2)
                    pe.wait_ge(s["lat_out"], b + 1)
                if n == 1:
                    pe.wait_ge(s["sc_out"], b + 1)
                for half in range(2):
                    for c in range(C2):
                        cols = slice(m * P, (m + 1) * P)
                        ins = three(bank[pair + half][:], up_h[:, half, c, cols], up_l[:, half, c, cols],
                                    xh[:, c], xl[:, c], c == 0, c == C2 - 1)
                ins.then_inc(s["up_ps"], 1)

            def turn_weights(b):
                for t in range(TT):
                    ins = pe.transpose(bank[3][0:48, 64 * t:64 * t + 64].bitcast(BF16),
                                       cbp[:, t].rearrange("p s e -> p (s e)"), identb[:])
                ins.then_inc(s["cbT_ps"], 1)

            def spread_weights(b, n):
                pe.wait_ge(s["cbT_out"], b + 1)
                pe.wait_ge(s["gated"], b * MT1 + n + 1)
                pe.matmul(bank[4 + 2 * (n % 2)][:], sel[:, ORDER[n]], cbT[:], start=True, stop=True)\
                  .then_inc(s["cb_ps"], 1)

            def down(b, t):
                pe.wait_ge(s["hid_l_made"], b * MT1 + MT1)
                cols = slice(t * P, (t + 1) * P)
                for m in range(MT1):
                    ins = three(bank[4 + t][:, 0:D], hid_h[:, m, cols], hid_l[:, m, cols], down_h[:, m],
                                down_l[:, m], m == 0, m == MT1 - 1)
                ins.then_inc(s["fy_ps"], 1)

            def project_qkv(b, layer):
                if layer == 0:
                    pe.wait_ge(s["xT_out"], 4 * b + 4)
                    for c in range(C2):
                        ins = pe.matmul(bank[4][0:LAT, :], wd[:, c], xT[:, c], start=c == 0, stop=c == C2 - 1)
                    ins.then_inc(s["lat_ps"], 1)
                    pe.wait_ge(s["fin_made"], 2 * b)
                else:
                    pe.wait_ge(s["xbT_out"], 2 * b + 2)
                for t in range(TT):
                    tok = slice(t * P, (t + 1) * P)
                    if layer == 0:
                        for c in range(C2):
                            pe.matmul(bank[t][:, 0:D], xT[:, c, tok], wq[0][:, c], start=c == 0, stop=c == C2 - 1)
                        if t == 0:
                            pe.wait_ge(s["lat_out"], b + 1)
                        ins = pe.matmul(bank[t][:, D:QKV], lat[:, tok], kv_up[:], start=True, stop=True)
                    else:
                        for c in range(C2):
                            ins = pe.matmul(bank[t][:, 0:QKV], xT[:, c, tok], wq[1][:, c],
                                            start=c == 0, stop=c == C2 - 1)
                    ins.then_inc(s["qkv_ps"], 1)

            def turn_qk(b, layer):
                L2 = 2 * b + layer
                pe.wait_ge(s["qk_made"], L2 + 1)
                for n in range(3):
                    for t in range(TT):
                        ins = pe.transpose(bank[n][:, t * P:(t + 1) * P], qk[:, t, n * P:(n + 1) * P], ident[:])
                    ins.then_inc(s["qkT_ps"], 1)

            def score(b, layer, j, i):
                for n, heads, start, width in groups_of(layer, j, i):
                    first = 0 if layer == 0 else groups_until(0, 4, 4)
                    pe.wait_ge(s["exp_out"], at(b, NG, n - 1 if n - first >= 2 else first))
                    for x, h in enumerate(heads):
                        ps = bank[n % 2][:, x * width:(x + 1) * width]
                        pe.matmul(ps, kz[:, 4 * (j % 2) + h, i * P:(i + 1) * P],
                                  qT[:, j // 2, start:start + width], start=True, stop=False)
                        masked = min(width, P if layer == 0 else P + 64)
                        mask = causal if layer == 0 else window
                        ins = pe.matmul(ps[:, 0:masked], identb[:], mask[:, 0:masked], start=False, stop=True)
                    ins.then_inc(s["score_ps"], 1)

            def attend(b, layer, j, i):
                pe.wait_ge(s["exp_out"], b * NG + groups_until(layer, j, i))
                if i == 0:
                    pe.wait_ge(s["oT_out"], 8 * b + 4 * layer + j)
                start = P * i
                end = T if layer == 0 else min(T, P * i + P + 64)
                parts = [(start, end)] if i == 0 or layer == 0 else [(start, start + 64), (start + 64, end)]
                for lo, hi in parts:
                    for h in range(KVH):
                        ins = pe.matmul(bank[2][32 * h:32 * h + 32, lo:hi], v1[:, i, h],
                                        prob[i % 2][:, h, lo - start:hi - start],
                                        start=i == 0, stop=hi == T and i == TT - 1)
                ins.then_inc(s["pv_ps"], 1)

            def turn_o(b, layer, j):
                pe.wait_ge(s["oT_out"], 8 * b + 4 * layer + j + 1)
                pe.wait_ge(s["o_made"], 8 * b + 4 * layer + j)
                for t in range(TT):
                    ins = pe.transpose(bank[3][:, t * P:(t + 1) * P], oT[:, t * P:(t + 1) * P], ident[:])
                ins.then_inc(s["ot_ps"], 1)

            def turn_heads(b, layer):
                pe.wait_ge(s["o_made"], 8 * b + 4 * layer + 4)
                for c in range(C2):
                    for t in range(TT):
                        ins = pe.transpose(bank[c][:, t * P:(t + 1) * P], o_tok[:, t, c * P:(c + 1) * P], ident[:])
                    ins.then_inc(s["onT_ps"], 1)

            def project_out(b, layer):
                pe.wait_ge(s["onT_out"], 4 * b + 2 * layer + 2)
                for t in range(TT):
                    for c in range(C2):
                        ins = pe.matmul(bank[2 + t // 2][:, (t % 2) * D:(t % 2) * D + D],
                                        onT[:, c, t * P:(t + 1) * P], wo[layer][:, c], start=c == 0, stop=c == C2 - 1)
                    ins.then_inc(s["ao_ps"], 1)

            def turn_xb(b):
                for c in range(C2):
                    for t in range(TT):
                        pe.wait_ge(s["xb_made"], 2 * b + t // 2 + 1)
                        ins = pe.transpose(bank[c][:, t * P:(t + 1) * P], xb[:, t, c * P:(c + 1) * P], ident[:])
                    ins.then_inc(s["xbT_ps"], 1)

            def body(b, more):
                scores_of_experts(b)
                project_qkv(b, 0)
                up(b, 0)
                up(b, 1)
                up(b, 2)
                turn_qk(b, 0)
                up(b, 3)
                pe.wait_ge(s["qkT_out"], 6 * b + 3)
                pe.wait_ge(s["kz_made"], 16 * b + 8)
                pe.wait_ge(s["v_made"], 2 * b + 1)
                for j in range(4):
                    score(b, 0, j, 0)
                    if j:
                        attend(b, 0, j - 1, 3)
                    else:
                        pe.wait_ge(s["cb_made"], b + 1)
                    score(b, 0, j, 1)
                    if j == 0:
                        turn_weights(b)
                    attend(b, 0, j, 0)
                    if j:
                        turn_o(b, 0, j - 1)
                    up(b, NSH + 2 * j)
                    if j:
                        spread_weights(b, NSH + 2 * j - 1)
                    score(b, 0, j, 2)
                    attend(b, 0, j, 1)
                    score(b, 0, j, 3)
                    attend(b, 0, j, 2)
                    up(b, NSH + 2 * j + 1)
                    spread_weights(b, NSH + 2 * j)
                attend(b, 0, 3, 3)
                spread_weights(b, MT1 - 1)
                turn_o(b, 0, 3)
                turn_heads(b, 0)
                project_out(b, 0)
                turn_xb(b)
                project_qkv(b, 1)
                for t in range(TT):
                    down(b, t)
                turn_qk(b, 1)
                if more:
                    turn_y(b + 1)
                pe.wait_ge(s["qkT_out"], 6 * b + 6)
                pe.wait_ge(s["kz_made"], 16 * b + 16)
                pe.wait_ge(s["v_made"], 2 * b + 2)
                for j in range(4):
                    score(b, 1, j, 0)
                    if j:
                        attend(b, 1, j - 1, 3)
                    score(b, 1, j, 1)
                    attend(b, 1, j, 0)
                    if j:
                        turn_o(b, 1, j - 1)
                    if more and j == 2:
                        turn_yn(b + 1)
                    score(b, 1, j, 2)
                    attend(b, 1, j, 1)
                    score(b, 1, j, 3)
                    attend(b, 1, j, 2)
                    if more and j == 3:
                        rwkv_out(b + 1)
                attend(b, 1, 3, 3)
                turn_o(b, 1, 3)
                if more:
                    turn_x(b + 1)
                turn_heads(b, 1)
                project_out(b, 1)

            turn_y(0)
            turn_yn(0)
            rwkv_out(0)
            turn_x(0)
            pe.wait_ge(s["wl_made"], 2)
            with pe.Fori(0, NB - 1) as b:
                body(b, True)
            body(NB - 1, False)


def _constants(np):
    bf16 = np.dtype("bfloat16")
    eye = np.eye(P, dtype=np.float32)
    before = lambda n: np.tile((np.arange(n)[None, :] < np.arange(n)[:, None]).astype(np.float32).reshape(1, n * n),
                               (P, 1))
    s, t = np.arange(P)[:, None], np.arange(P + 64)[None, :]
    causal = np.where(t[:, :P] < s, np.float32(-1e30), np.float32(0))
    window = np.where((t < s) | (t - s >= 64), np.float32(-1e30), np.float32(0))
    rope = np.zeros((P, 2, 2, TT, K // 2, 2), np.float32)
    for layer, base in enumerate((1000000.0, 10000.0)):
        inv = (1.0 / np.float32(base) ** (np.arange(0, K, 2, dtype=np.float32) / np.float32(K))).astype(np.float32)
        ang = np.arange(T, dtype=np.float32)[:, None] * inv[None, :]
        cos = np.cos(ang).astype(np.float32).reshape(TT, P, 8).transpose(1, 0, 2)
        sin = np.sin(ang).astype(np.float32).reshape(TT, P, 8).transpose(1, 0, 2)
        rope[:, layer, 0] = cos[:, :, :, None]
        rope[:, layer, 1, :, :, 0] = -sin
        rope[:, layer, 1, :, :, 1] = sin
    slot = (np.arange(P)[:, None] // K == np.arange(8)[None, :]).astype(np.float32)
    sel = np.zeros((48, RT1, P), np.float32)
    for m in range(RT1):
        for p in range(P):
            sel[[2 * m + p // H1, E1 + 2 * m + p // H1, 2 * E1 + 2 * m + p // H1], m, p] = 1.0
    return {
        "c_ident": eye, "c_before8": before(E0), "c_identb": eye.astype(bf16),
        "c_causal": causal.astype(bf16), "c_window": window.astype(bf16),
        "c_rope": rope.reshape(P, 2, 2, TT, K), "c_slot": slot,
        "c_eps": np.tile(np.array([[1e-5 * 64.0, 1e-5, 1e-6, 0.0] + [1e-5] * 4 + [1e-6] * 4 + [-0.5] * 4], np.float32),
                         (P, 1)),
        "c_sel": sel.astype(bf16), "c_before16": before(E1), "c_before4": before(G4),
    }


def _layouts(np, i):
    def rows(w):
        w = np.asarray(w)
        return np.ascontiguousarray(w.reshape(C2, P, -1).transpose(1, 0, 2))

    def vec(v):
        return np.ascontiguousarray(np.asarray(v).reshape(C2, P).T)

    n = {k: np.asarray(v) for k, v in i.items()}
    l0, f0, l1, f1 = "L0_attn_", "L0_ffn_", "L1_attn_", "L1_ffn_"
    conv = n[l0 + "conv_w"]
    heads = np.array([4 * g + j for j in range(4) for g in range(KVH)])
    cols = (heads[:, None] * K + np.arange(K)[None, :]).reshape(-1)
    token = lambda x: np.ascontiguousarray(x.reshape(NB, TT, P, D).transpose(0, 2, 1, 3))
    full = P * (HT0 - 1)
    w1, w2 = n[f0 + "W1"], n[f0 + "W2"]
    up0 = np.concatenate([w1[:, :full], w1[:, full:], w2[:, full:], w2[:, :full]], 1)
    down0 = np.concatenate([n[f0 + "W3"].transpose(0, 2, 1), np.zeros((E0, HT0 * P - H0, D), np.float32)], 1)
    up1 = np.stack([np.concatenate([n[f1 + "gate_w"].transpose(1, 0, 2).reshape(D, E1 * H1),
                                    n[f1 + "shared_gate_w"].T], 1),
                    np.concatenate([n[f1 + "up_w"].transpose(1, 0, 2).reshape(D, E1 * H1),
                                    n[f1 + "shared_up_w"].T], 1)], 0)
    down1 = np.concatenate([n[f1 + "down_w"].reshape(E1 * H1, D), n[f1 + "shared_down_w"].T], 0)
    c = np.ascontiguousarray
    return {
        "x": token(n[l0 + "x"]),
        "c_vecs": c(np.stack([vec(v) for v in (conv[:, 0, 0], conv[:, 0, 1], conv[:, 0, 2], n[l0 + "maa_x"],
                                               n[l0 + "maa_w"], n[l0 + "maa_k"], n[l0 + "maa_v"], n[l0 + "maa_r"],
                                               n[l0 + "maa_g"], n[l0 + "gate_b"])], 1)),
        "time_decay": vec(n[l0 + "time_decay"]),
        "maa_w1": rows(n[l0 + "maa_w1"]), "maa_w2": c(n[l0 + "maa_w2"]),
        "gate_w": rows(n[l0 + "gate_w"]), "Wk": rows(n[l0 + "Wk"]), "Wv": rows(n[l0 + "Wv"]),
        "Wr": rows(n[l0 + "Wr"]), "Wg": rows(n[l0 + "Wg"]), "Wo": rows(n[l0 + "Wo"]),
        "decay_w1": rows(n[l0 + "decay_w1"]), "decay_w2": c(n[l0 + "decay_w2"]),
        "ffn_Wg": rows(n[f0 + "Wg"].T),
        "ffn_up": c(up0.reshape(E0, 2 * H0, C2, P).transpose(0, 3, 2, 1)),
        "ffn_down": c(down0.reshape(E0, HT0, P, D).transpose(0, 2, 1, 3)),
        "ln_wb": c(np.stack([vec(n[l0 + "ln_w"]), vec(n[l0 + "ln_b"])], 1)),
        "norm_w": c(np.stack([vec(n[l1 + "norm1_w"]), vec(n[l1 + "norm2_w"])], 1)),
        "g_wq": rows(n[l1 + "g_wq"][:, cols]), "g_kv_down": rows(n[l1 + "g_kv_down"]),
        "g_kv_up": c(np.concatenate([n[l1 + "g_k_up"], n[l1 + "g_v_up"]], 1)),
        "l_wqkv": rows(np.concatenate([n[l1 + "l_wq"][:, cols], n[l1 + "l_wk"], n[l1 + "l_wv"]], 1)),
        "g_wo": rows(n[l1 + "g_wo"][cols]), "l_wo": rows(n[l1 + "l_wo"][cols]),
        "router_w": rows(n[f1 + "router_w"].T), "bias_r": c(np.tile(n[f1 + "correction_bias"][None, :], (P, 1))),
        "ffn1_up": c(up1.reshape(2, C2, P, MT1 * P).transpose(2, 0, 1, 3)),
        "ffn1_down": c(down1.reshape(MT1, P, D).transpose(1, 0, 2)),
    }


def kernel(**inputs):
    import concourse.bacc as bacc
    import numpy as np
    from concourse.bass_utils import run_bass_kernel_spmd

    arrays = {**_layouts(np, inputs), **_constants(np)}
    nc = bacc.Bacc("TRN2", target_bir_lowering=False, num_devices=1)
    a = {k: nc.dram_tensor("in_" + k, v.shape, mybir.dt.from_np(v.dtype), kind="ExternalInput").ap()
         for k, v in arrays.items()}
    out = nc.dram_tensor("out", (NB, P, TT, D), F32, kind="ExternalOutput").ap()
    build(nc, a, out)
    r = run_bass_kernel_spmd(nc, [{"in_" + k: v for k, v in arrays.items()}], core_ids=[0])
    got = r.results[0]["out"]
    return np.ascontiguousarray(got.transpose(0, 2, 1, 3)).reshape(NB, T, D)
```

```python
from contextlib import ExitStack

import concourse.bass as bass
from concourse import mybir

F32 = mybir.dt.float32
BF16 = mybir.dt.bfloat16
F16 = mybir.dt.float16
ALU = mybir.AluOpType
ACT = mybir.ActivationFunctionType
AX = mybir.AxisListType.X

P = 128
NB, T, D = 8, 512, 256
C2 = D // P
TT = T // P
H, K = 16, 16
E0, H0 = 8, 704
HT0 = (H0 + P - 1) // P
E1, H1, HS = 16, 64, 512
MT1 = (E1 * H1 + HS) // P
RT1 = E1 * H1 // P
KVH = 4
G4 = 4
LAT = 64


class Steps:

    def __init__(self, engine, semaphore, per_round):
        self.engine, self.semaphore, self.per_round, self.done = engine, semaphore, per_round, 0
        self.base = 0

    def round(self, number):
        self.base, self.done = number * self.per_round, 0

    def add(self, instruction):
        instruction.then_inc(self.semaphore, 1)
        self.done += 1

    def settle(self):
        self.engine.wait_ge(self.semaphore, self.base + self.done)

    def end(self):
        assert self.done == self.per_round, (self.semaphore, self.done)


def at(number, per_round, n):
    return number * per_round + max(n, 0)


def build(nc, a, out):
    ctx = ExitStack()
    with ctx:
        scratch = {n: nc.dram_tensor("scratch_" + n, shape, F32, kind="Internal").ap() for n, shape in
                   (("rkw", [3, NB * D, T]), ("v", [NB * D, T]), ("gate", [NB * D, T]), ("g", [NB * D, T]),
                    ("y", [NB * D, T]), ("ffn", [P, NB * TT, D]))}
        keep = {"ident": ctx.enter_context(nc.sbuf_tensor("ident", [P, P], F32))}
        with ExitStack() as first:
            keep["xh"] = first.enter_context(nc.sbuf_tensor("xh", [P, C2, NB * T], F16))
            keep["xl"] = first.enter_context(nc.sbuf_tensor("xl", [P, C2, NB * T], F16))
            keep["w0"] = first.enter_context(nc.sbuf_tensor("route0", [P, NB * TT, E0], F32))
            project(nc, a, scratch, keep)
            scan_and_experts(nc, a, scratch, keep)
        layer_one(nc, a, scratch, keep, out)


def project(nc, a, scratch, keep):
    with ExitStack() as ctx:
        def sb(name, shape, dt=F32):
            return ctx.enter_context(nc.sbuf_tensor("b1_" + name, shape, dt))

        def sem(name):
            return ctx.enter_context(nc.semaphore("b1_" + name))

        bank = [ctx.enter_context(nc.psum_tensor(f"b1_bank{n}", [P, 512], F32)) for n in range(8)]
        ident, xh, xl, w0 = (keep[n] for n in ("ident", "xh", "xl", "w0"))
        xnT = sb("xnT", [P, C2, NB * T])
        x_tok = sb("x_tok", [P, 2, TT, D])
        xn_tok = sb("xn_tok", [P, 2, TT, D])
        stats = sb("stats", [P, 2, TT, 6])
        mv = sb("mv", [P, 2, TT, 2])
        std = sb("std", [P, 2, TT])
        rstd = sb("rstd", [P, 2, TT])
        eps = sb("eps", [P, 1])
        holds_wait = sb("holds_wait", [P, 1])
        pool_wait = sb("pool_wait", [P, 9])
        dx = sb("dx", [P, C2, NB * T])
        xxx = sb("xxx", [P, 2, C2, T])
        t5 = sb("t5", [P, 2, NB * T])
        vecs = sb("vecs", [P, 10, C2])
        td = sb("time_decay", [P, C2])
        maa_w1 = sb("maa_w1", [P, C2, 160])
        mix_w = sb("mix_w", [P, 5, D])
        proj_w = sb("proj_w", [P, 5, C2, D])
        dec_w1 = sb("dec_w1", [P, C2, P])
        dec_w2 = sb("dec_w2", [P, D])
        tmp = xxx
        xf = x_tok[:].rearrange("p u t n -> p (u t n)").rearrange("p (s c t) -> p s c t", s=2, c=C2)
        route_w = sb("route_w", [P, C2, E0])
        before = sb("before", [P, E0 * E0])
        sc = sb("sc", [P, NB * TT, E0])
        rank = sb("rank", [P, NB * TT, E0])
        tw = sb("tw", [P, T])
        ew = sb("ew", [P, 2, T])
        stage = sb("stage", [P, 6, C2, T])

        more = xxx[:].rearrange("p u c t -> p (u c t)")
        same = x_tok[:].rearrange("p u t n -> p (u t n)")
        assert more.shape[1] == same.shape[1] == NB * TT * E0 * E0

        weights_in, zeroed = sem("weights_in"), sem("zeroed")
        xl_made, route_ps, route_own = (sem(n) for n in ("xl_made", "route_ps", "route_own"))
        x_in = [sem(f"x_in{u}") for u in range(2)]
        vec_ready, var_ready, std_ready = sem("vec_ready"), sem("var_ready"), sem("std_ready")
        xn_made = [sem(f"xn_made{u}") for u in range(2)]
        xT_ps = sem("xT_ps")
        xT_out = [sem(f"xT_out{u}") for u in range(2)]
        xxx_made = [sem(f"xxx_made{u}") for u in range(2)]
        t5_ps = sem("t5_ps")
        t5_out = [sem(f"t5_out{u}") for u in range(2)]
        own1 = sem("dve_own1")
        m_ps, m_used, xf_made = sem("m_ps"), sem("m_used"), sem("xf_made")
        unit_ps, unit_out, act_own = sem("unit_ps"), sem("unit_out"), sem("act_own")
        staged = [sem(f"staged{n}") for n in range(6)]

        WEIGHT_LOADS = 18
        UNITS = [("gate", 0), ("gate", 1), ("tw", 0), ("k", 0), ("k", 1), ("v", 0), ("v", 1), ("r", 0), ("r", 1),
                 ("decay", 0), ("decay", 1), ("g", 0), ("g", 1)]
        NU = len(UNITS)
        UB = 5
        SLOT = {"gate": 0, "k": 1, "v": 2, "r": 3, "decay": 4, "g": 5}
        USED = [3, 5, 7, 9, 13]

        block = ctx.enter_context(nc.Block())

        @block.sync
        def _(sp):
            for dst, src in ((ident[:], a["c_ident"]), (vecs[:], a["c_vecs"]), (maa_w1[:], a["maa_w1"]),
                             (proj_w[:, 0], a["gate_w"]), (proj_w[:, 1], a["Wk"]), (proj_w[:, 2], a["Wv"]),
                             (proj_w[:, 3], a["Wr"]), (proj_w[:, 4], a["Wg"]), (td[:], a["time_decay"]),
                             (route_w[:], a["ffn_Wg"]), (before[:], a["c_before8"])):
                sp.dma_start(dst, src).then_inc(weights_in, 16)
            sp.wait_ge(zeroed, 4)
            for f in range(4):
                sp.dma_start(mix_w[32 * f:32 * f + 32, f, :], a["maa_w2"][f]).then_inc(weights_in, 16)
            sp.dma_start(mix_w[0:32, 4, :], a["maa_w2"][4]).then_inc(weights_in, 16)
            sp.dma_start(dec_w1[:, :, 0:64], a["decay_w1"]).then_inc(weights_in, 16)
            sp.dma_start(dec_w2[0:64, :], a["decay_w2"]).then_inc(weights_in, 16)
            with sp.Fori(0, NB // 2) as i:
                for u in range(2):
                    sp.wait_ge(xn_made[u], TT * i)
                    sp.dma_start(x_tok[:, u], a["x"][2 * i + u]).then_inc(x_in[u], 16)
            outs = [(0, scratch["gate"], 2), (1, scratch["rkw"][1], 5), (2, scratch["v"], 7),
                    (3, scratch["rkw"][0], 9), (4, scratch["rkw"][2], 11), (5, scratch["g"], 13)]
            with sp.Fori(0, NB) as b:
                for n, dram, units in outs:
                    sp.wait_ge(unit_out, b * NU + units)
                    dst = dram.rearrange("(b c p) t -> b p c t", c=C2, p=P)[b]
                    sp.dma_start(dst, stage[:, n]).then_inc(staged[n], 16)
            for n in range(6):
                sp.wait_ge(staged[n], 16 * NB)

        @block.gpsimd
        def _(pool):
            pool.memset(mix_w[:], 0.0).then_inc(zeroed, 1)
            pool.memset(dec_w1[:], 0.0).then_inc(zeroed, 1)
            pool.memset(dec_w2[:], 0.0).then_inc(zeroed, 1)
            pool.memset(t5[:, 1, :], 0.0).then_inc(zeroed, 1)
            pool.memset(eps[:], 1e-5).then_inc(zeroed, 1)
            with pool.Fori(0, NB // 2) as i:
                for u in range(2):
                    for c in range(C2):
                        pool.wait_ge(xl_made, 2 * C2 * i)
                        pool.wait_ge(xT_out[u], 4 * i + 2 * c + 2)
                        pool.tensor_tensor(pool_wait[:, 5 + 2 * u + c:6 + 2 * u + c], eps[:], eps[:], ALU.add)
                        cols = bass.ds((2 * i + u) * T, T)
                        pool.tensor_tensor(xl[:, c, cols], xnT[:, c, cols], xh[:, c, cols], ALU.subtract)\
                            .then_inc(xl_made, 1)
            pool.wait_ge(xl_made, C2 * NB)
            with pool.Fori(0, NB) as b:
                for f in range(5):
                    pool.wait_ge(m_used, b * 10 + 2 * f + 2)
                    pool.wait_ge(unit_ps, at(b, NU, USED[f - 2] if f >= 2 else 0))
                    pool.tensor_tensor(pool_wait[:, f:f + 1], eps[:], eps[:], ALU.add)
                    for c in range(C2):
                        pool.tensor_tensor(xf[:, f % 2, c], tmp[:, f % 2, c], xnT[:, c, bass.ds(b * T, T)],
                                           ALU.add).then_inc(xf_made, 1)

        @block.vector
        def _(dve):
            own = Steps(dve, own1, 32)
            dve.wait_ge(weights_in, 16 * WEIGHT_LOADS)
            dve.tensor_scalar(vecs[:, 1, :], vecs[:, 1, :], -1.0, None, ALU.add).then_inc(vec_ready, 1)
            dve.tensor_scalar(vecs[:, 9, :], vecs[:, 9, :], 0.5, None, ALU.mult).then_inc(vec_ready, 1)
            dve.wait_ge(vec_ready, 2)
            with dve.Fori(0, NB // 2) as i:
                own.round(i)
                for u in range(2):
                    dve.wait_ge(x_in[u], 16 * i + 16)
                    for t in range(TT):
                        own.add(dve.bn_stats(stats[:, u, t], x_tok[:, u, t]))
                    own.settle()
                    own.add(dve.memset(holds_wait[:, 0:1], 0.0))
                    for t in range(TT):
                        ins = dve.bn_aggr(mv[:, u, t], stats[:, u, t])
                        if t < TT - 1:
                            own.add(ins)
                    ins.then_inc(var_ready, 1)
                for u in range(2):
                    dve.wait_ge(std_ready, 2 * i + u + 1)
                    dve.wait_ge(xT_out[u], 4 * i)
                    own.add(dve.reciprocal(rstd[:, u], std[:, u]))
                    own.settle()
                    for t in range(TT):
                        ins = dve.tensor_scalar(xn_tok[:, u, t], x_tok[:, u, t], mv[:, u, t, 0:1],
                                                rstd[:, u, t:t + 1], ALU.subtract, ALU.mult)
                        ins.then_inc(xn_made[u], 1)
                for u in range(2):
                    dve.wait_ge(xT_out[u], 4 * i + 4)
                    x = [xnT[:, c, bass.ds((2 * i + u) * T, T)] for c in range(C2)]
                    x_head = [xnT[:, c, bass.ds((2 * i + u) * T, T - 1)] for c in range(C2)]
                    x_tail = [xnT[:, c, bass.ds((2 * i + u) * T + 1, T - 1)] for c in range(C2)]
                    d = [dx[:, c, bass.ds((2 * i + u) * T, T)] for c in range(C2)]
                    d_head = [dx[:, c, bass.ds((2 * i + u) * T, T - 1)] for c in range(C2)]
                    d_tail = [dx[:, c, bass.ds((2 * i + u) * T + 1, T - 1)] for c in range(C2)]
                    for c in range(C2):
                        own.add(dve.tensor_scalar(d[c], x[c], vecs[:, 1, c:c + 1], None, ALU.mult))
                    own.settle()
                    for c in range(C2):
                        own.add(dve.scalar_tensor_tensor(d_tail[c], x_head[c], vecs[:, 0, c:c + 1], d_tail[c],
                                                         ALU.mult, ALU.add))
                    own.settle()
                    for c in range(C2):
                        own.add(dve.scalar_tensor_tensor(d_head[c], x_tail[c], vecs[:, 2, c:c + 1], d_head[c],
                                                         ALU.mult, ALU.add))
                    own.settle()
                    dve.wait_ge(t5_out[u], 2 * i)
                    for c in range(C2):
                        ins = dve.scalar_tensor_tensor(xxx[:, u, c], d[c], vecs[:, 3, c:c + 1], x[c],
                                                       ALU.mult, ALU.add)
                        if c == 0:
                            own.add(ins)
                    ins.then_inc(xxx_made[u], 1)
                own.end()
            dve.wait_ge(route_ps, 1)
            dve.wait_ge(xn_made[1], TT * (NB // 2))
            n_rows = NB * TT
            own = Steps(dve, route_own, 7)
            own.add(dve.tensor_copy(sc[:], bank[7][:, 0:n_rows * E0].rearrange("p (t e) -> p t e", e=E0)))
            own.settle()
            others = sc[:].rearrange("p t (o e) -> p t o e", o=1).broadcast_to([P, n_rows, E0, E0])
            itself = sc[:].rearrange("p t (e o) -> p t e o", o=1).broadcast_to([P, n_rows, E0, E0])
            square = "p (t e j) -> p t e j"
            own.add(dve.tensor_tensor(more.rearrange(square, e=E0, j=E0), others, itself, ALU.is_gt))
            own.add(dve.tensor_tensor(same.rearrange(square, e=E0, j=E0), others, itself, ALU.is_equal))
            own.settle()
            same_rows = same.rearrange("p (t n) -> p t n", n=E0 * E0)
            own.add(dve.tensor_tensor(same_rows, same_rows, before[:].rearrange("p (o n) -> p o n", o=1)
                                      .broadcast_to([P, n_rows, E0 * E0]), ALU.mult))
            own.settle()
            own.add(dve.tensor_tensor(more, more, same, ALU.add))
            own.settle()
            own.add(dve.reduce_sum(rank[:], more.rearrange("p (n j) -> p n j", j=E0), AX))
            own.settle()
            own.add(dve.scalar_tensor_tensor(w0[:], rank[:], 2.0, sc[:], ALU.is_lt, ALU.mult))
            own.settle()
            with dve.Fori(0, NB) as b:
                for f in range(5):
                    for c in range(C2):
                        dve.wait_ge(m_ps, b * 10 + 2 * f + c + 1)
                        dve.wait_ge(xf_made, at(b, 10, 2 * (f - 2) + c + 1))
                        dve.scalar_tensor_tensor(tmp[:, f % 2, c], bank[(2 * f + c) % 2][:], vecs[:, 4 + f, c:c + 1],
                                                 dx[:, c, bass.ds(b * T, T)], ALU.add, ALU.mult).then_inc(m_used, 1)

        @block.scalar
        def _(act):
            act.wait_ge(zeroed, 5)
            with act.Fori(0, NB // 2) as i:
                for u in range(2):
                    act.wait_ge(var_ready, 2 * i + u + 1)
                    act.activation(std[:, u], mv[:, u, :, 1], ACT.Sqrt, bias=eps[:]).then_inc(std_ready, 1)
                for u in range(2):
                    for c in range(C2):
                        act.wait_ge(xT_ps, 4 * i + 2 * u + c + 1)
                        for dst in (xh, xnT):
                            act.activation(dst[:, c, bass.ds((2 * i + u) * T, T)], bank[2 * u + c][:], ACT.Copy)\
                               .then_inc(xT_out[u], 1)
                for u in range(2):
                    act.wait_ge(t5_ps, 2 * i + u + 1)
                    act.activation(t5[:, 0, bass.ds((2 * i + u) * T, T)], bank[4 + 2 * u][:], ACT.Tanh)\
                       .then_inc(t5_out[u], 1)
                    act.activation(t5[0:32, 1, bass.ds((2 * i + u) * T, T)], bank[5 + 2 * u][0:32, :], ACT.Tanh)\
                       .then_inc(t5_out[u], 1)
            act.wait_ge(vec_ready, 2)
            with act.Fori(0, NB) as b:
                for n, (what, c) in enumerate(UNITS):
                    act.wait_ge(unit_ps, b * NU + n + 1)
                    ps = bank[2 + n % UB][:]
                    if what in SLOT and c == 0:
                        act.wait_ge(staged[SLOT[what]], 16 * b)
                    if what == "gate":
                        ins = act.activation(stage[:, 0, c], ps, ACT.Tanh, bias=vecs[:, 9, c:c + 1], scale=0.5)
                    elif what == "tw":
                        ins = act.activation(tw[:], ps, ACT.Tanh)
                    elif what == "decay":
                        act.activation(ew[:, c], ps, ACT.Exp, bias=td[:, c:c + 1]).then_inc(act_own, 1)
                        act.wait_ge(act_own, 2 * b + c + 1)
                        ins = act.activation(stage[:, 4, c], ew[:, c], ACT.Exp, scale=-1.0)
                    elif what == "g":
                        ins = act.activation(stage[:, 5, c], ps, ACT.Silu)
                    else:
                        ins = act.activation(stage[:, SLOT[what], c], ps, ACT.Copy)
                    ins.then_inc(unit_out, 1)

        @block.tensor
        def _(pe):
            pe.wait_ge(weights_in, 16 * WEIGHT_LOADS)
            pe.wait_ge(zeroed, 5)
            with pe.Fori(0, NB // 2) as i:
                for u in range(2):
                    pe.wait_ge(xT_out[u], 4 * i)
                    for c in range(C2):
                        for t in range(TT):
                            if c == 0:
                                pe.wait_ge(xn_made[u], TT * i + t + 1)
                            ins = pe.transpose(bank[2 * u + c][:, t * P:(t + 1) * P],
                                               xn_tok[:, u, t, c * P:(c + 1) * P], ident[:])
                        ins.then_inc(xT_ps, 1)
                for u in range(2):
                    pe.wait_ge(xxx_made[u], i + 1)
                    pe.wait_ge(t5_out[u], 2 * i)
                    for n, (lo, hi) in enumerate(((0, P), (P, 160))):
                        for c in range(C2):
                            ins = pe.matmul(bank[4 + 2 * u + n][0:hi - lo, :], maa_w1[:, c, lo:hi], xxx[:, u, c],
                                            start=c == 0, stop=c == C2 - 1)
                    ins.then_inc(t5_ps, 1)
            for u in range(2):
                pe.wait_ge(xT_out[u], 4 * (NB // 2))
                pe.wait_ge(t5_out[u], 2 * (NB // 2))
            for t in range(NB * TT):
                for c in range(C2):
                    ins = pe.matmul(bank[7][:, t * E0:(t + 1) * E0], xnT[:, c, t * P:(t + 1) * P],
                                    route_w[:, c], start=c == 0, stop=c == C2 - 1)
            ins.then_inc(route_ps, 1)

            with pe.Fori(0, NB) as b:
                def mix(f):
                    for c in range(C2):
                        pe.wait_ge(m_used, at(b, 10, 2 * f + c - 1))
                        pe.matmul(bank[(2 * f + c) % 2][:], mix_w[:, f, c * P:(c + 1) * P],
                                  t5[:, f // 4, bass.ds(b * T, T)], start=True, stop=True).then_inc(m_ps, 1)

                def unit(n):
                    what, o = UNITS[n]
                    pe.wait_ge(unit_out, at(b, NU, n - UB + 1))
                    cols = slice(o * P, (o + 1) * P)
                    ps = bank[2 + n % UB][:]
                    if what == "gate":
                        for c in range(C2):
                            ins = pe.matmul(ps, proj_w[:, 0, c, cols], dx[:, c, bass.ds(b * T, T)],
                                            start=c == 0, stop=c == C2 - 1)
                    elif what == "tw":
                        pe.wait_ge(xf_made, b * 10 + 2)
                        for c in range(C2):
                            ins = pe.matmul(ps, dec_w1[:, c, :], xf[:, 0, c], start=c == 0, stop=c == C2 - 1)
                    elif what == "decay":
                        pe.wait_ge(unit_out, b * NU + 3)
                        ins = pe.matmul(ps, dec_w2[:, cols], tw[:], start=True, stop=True)
                    else:
                        f = {"k": 1, "v": 2, "r": 3, "g": 4}[what]
                        pe.wait_ge(xf_made, b * 10 + 2 * f + 2)
                        for c in range(C2):
                            ins = pe.matmul(ps, proj_w[:, f, c, cols], xf[:, f % 2, c],
                                            start=c == 0, stop=c == C2 - 1)
                    ins.then_inc(unit_ps, 1)

                mix(0)
                mix(1)
                unit(0)
                unit(1)
                unit(2)
                mix(2)
                unit(3)
                unit(4)
                mix(3)
                unit(5)
                unit(6)
                mix(4)
                for n in range(7, NU):
                    unit(n)


def scan_and_experts(nc, a, scratch, keep):
    with ExitStack() as ctx:
        def sb(name, shape, dt=F32):
            return ctx.enter_context(nc.sbuf_tensor("b2_" + name, shape, dt))

        def sem(name):
            return ctx.enter_context(nc.semaphore("b2_" + name))

        bank = [ctx.enter_context(nc.psum_tensor(f"b2_bank{n}", [P, 512], F32)) for n in range(8)]
        xh, xl, w0 = keep["xh"], keep["xl"], keep["w0"]
        VH, VQ = 8, 2
        KR = K // 4
        CK = VH // VQ
        NCH = 4 * CK
        assert NCH == 2 * NB and 2 * KR == E0
        HALF = H0 - P * (HT0 - 1)
        assert 2 * HALF == P
        ffn = sb("ffn", [P, NB * TT, D])
        up_raw = sb("up_raw", [P, C2, 2 * H0])
        up_h = sb("up_h", [P, C2, 2 * H0], F16)
        up_l = sb("up_l", [P, C2, 2 * H0], F16)
        down_raw = sb("down_raw", [P, HT0, D])
        down_h = sb("down_h", [P, HT0, D], F16)
        down_l = sb("down_l", [P, HT0, D], F16)
        hid_h = sb("hid_h", [P, 2, HT0, T], BF16)
        hid_l = sb("hid_l", [P, 2, HT0, T], F16)
        prod = sb("prod", [P, 3, T])
        silu = sb("silu", [P, 2, T])
        rkw = sb("rkw", [P, 2, 3, T])
        v = sb("v", [P, VH + VQ, T])
        y = sb("y", [P, VH + VQ, T])
        kv = sb("kv", [P, 2, VQ, T])
        fwd = sb("fwd", [P, VQ, T])
        bwd = sb("bwd", [P, VQ, T])

        up_in, down_in, up_h_made, up_made, down_h_made, down_made = (
            sem(n) for n in ("up_in", "down_in", "up_h_made", "up_made", "down_h_made", "down_made"))
        ffn_stored = sem("ffn_stored")
        y_stored = [sem(f"y_stored{q}") for q in range(CK)]
        v_in = [sem(f"v_in{q}") for q in range(CK)]
        rkw_in = [sem(f"rkw_in{n}") for n in range(2)]
        cleared, cleared_again, x_in = sem("cleared"), sem("cleared_again"), sem("x_in")
        kv_made, summed = sem("kv_made"), sem("summed")
        scanned = [sem(f"scanned{n}") for n in range(2)]
        y_added = [sem(f"y_added{n}") for n in range(2)]
        up_ps, silu_made, prod_made, hid_h_made, hid_made, down_ps, combined = (
            sem(n) for n in ("up_ps", "silu_made", "prod_made", "hid_h_made", "hid_made", "down_ps", "combined"))
        NHID = NB * HT0
        NY = NB * TT
        rows = [P] * (HT0 - 1) + [HALF]
        view = "(p k) t -> p k t"
        rkw_rows = scratch["rkw"].rearrange("n (p k) t -> k p n t", k=K)
        v_rows = scratch["v"].rearrange(view, k=K)
        y_rows = scratch["y"].rearrange(view, k=K)

        def outputs(n):
            return bank[6 + n // 2 % 2][:, n % 2 * D:n % 2 * D + D]

        def slot(half, q):
            first = (q - half) % (CK + 1) * VQ
            return slice(first, first + VQ)

        def values(half, q):
            return slice(half * VH + q * VQ, half * VH + (q + 1) * VQ)

        block = ctx.enter_context(nc.Block())

        @block.sync
        def _(sp):
            def load_up(e):
                sp.wait_ge(up_made, e)
                sp.dma_start(up_raw[:], a["ffn_up"][e]).then_inc(up_in, 16)

            def load_down(e):
                sp.wait_ge(down_made, e)
                sp.dma_start(down_raw[:], a["ffn_down"][e]).then_inc(down_in, 16)

            def load_v(half, q):
                if half:
                    sp.wait_ge(kv_made, KR * NCH - CK + q)
                sp.dma_start(v[:, slot(half, q)], v_rows[:, values(half, q), :]).then_inc(v_in[q], 16)

            sp.dma_start(v[:, slot(0, 0)], v_rows[:, values(0, 0), :]).then_inc(v_in[0], 16)
            sp.dma_start(up_raw[:], a["ffn_up"][0]).then_inc(up_in, 16)
            sp.dma_start(down_raw[:], a["ffn_down"][0]).then_inc(down_in, 16)
            for q in range(1, CK):
                load_v(0, q)
            sp.wait_ge(kv_made, 1)
            sp.dma_start(ffn[:].rearrange("p (b t) n -> p b t n", t=TT), a["x"].rearrange("b p t n -> p b t n"))\
                .then_inc(x_in, 16)
            with sp.Fori(1, KR) as e:
                load_up(e)
                load_down(e)
            load_up(KR)
            load_down(KR)
            for q in range(CK):
                load_v(1, q)
                sp.wait_ge(y_added[1], KR * 2 * CK - CK + q + 1)
                sp.dma_start(y_rows[:, values(0, q), :], y[:, slot(0, q)]).then_inc(y_stored[q], 16)
            with sp.Fori(KR + 1, E0) as e:
                load_up(e)
                load_down(e)
            for q in range(CK):
                sp.wait_ge(y_added[1], 2 * KR * 2 * CK - CK + q + 1)
                sp.dma_start(y_rows[:, values(1, q), :], y[:, slot(1, q)]).then_inc(y_stored[q], 16)
            for tb in range(NB):
                sp.wait_ge(combined, (E0 - 1) * NY + (tb + 1) * TT)
                tiles = slice(tb * TT, (tb + 1) * TT)
                sp.dma_start(scratch["ffn"][:, tiles], ffn[:, tiles]).then_inc(ffn_stored, 16)
            sp.wait_ge(ffn_stored, 16 * NB)
            for q in range(CK):
                sp.wait_ge(y_stored[q], 32)

        @block.gpsimd
        def _(pool):
            for half in range(2):
                if half:
                    for q in range(CK - 1):
                        pool.wait_ge(y_stored[q], 16)
                    pool.memset(y[:, 0:(CK - 1) * VQ], 0.0).then_inc(cleared_again, 1)
                with pool.Fori(0, KR) as i:
                    rnd = half * KR + i

                    def low(n):
                        r = rows[n % HT0]
                        pool.wait_ge(hid_h_made, rnd * NHID + n + 1)
                        side = (n // HT0) % 2
                        pool.tensor_tensor(hid_l[0:r, side, n % HT0], prod[0:r, n % 3], hid_h[0:r, side, n % HT0],
                                           ALU.subtract).then_inc(hid_made, 1)

                    def outer(n):
                        s, q = n // CK, n % CK
                        if q == 0:
                            if s == 0:
                                load(0)
                            if s < 3:
                                load(s + 1)
                            pool.wait_ge(rkw_in[s % 2], 32 * rnd + 16 * (s // 2) + 16)
                        pool.wait_ge(v_in[q], 16 * half + 16)
                        pool.wait_ge(scanned[n % 2], VQ * NCH * rnd + 2 * VQ * (n // 2))
                        key = rkw[:, s % 2, 1, :].rearrange("p (o t) -> p o t", o=1).broadcast_to([P, VQ, T])
                        pool.tensor_tensor(kv[:, n % 2], key, v[:, slot(half, q), :], ALU.mult)\
                            .then_inc(kv_made, 1)

                    def load(s):
                        pool.wait_ge(y_added[s % 2], 2 * CK * rnd + CK * (s // 2))
                        pool.dma_start(rkw[:, s % 2], rkw_rows[4 * i + s]).then_inc(rkw_in[s % 2], 16)

                    outer(0)
                    pool.wait_ge(cleared, 4)
                    pool.wait_ge(up_h_made, rnd + 1)
                    pool.tensor_tensor(up_l[:], up_raw[:], up_h[:], ALU.subtract).then_inc(up_made, 1)
                    pool.wait_ge(down_h_made, rnd + 1)
                    pool.tensor_tensor(down_l[:], down_raw[:], down_h[:], ALU.subtract).then_inc(down_made, 1)
                    for tb in range(NB):
                        for m in range(HT0):
                            low(tb * HT0 + m)
                            if m == 0:
                                outer(2 * tb + 1)
                            if m == 3 and tb < NB - 1:
                                outer(2 * tb + 2)

        @block.vector
        def _(dve):
            dve.memset(bwd[:], 0.0).then_inc(cleared, 1)
            dve.memset(hid_h[:, :, HT0 - 1], 0.0).then_inc(cleared, 1)
            dve.memset(hid_l[:, :, HT0 - 1], 0.0).then_inc(cleared, 1)
            dve.memset(y[:], 0.0).then_inc(cleared, 1)
            dve.wait_ge(cleared, 4)
            for half in range(2):
                if half:
                    dve.wait_ge(cleared_again, 1)
                with dve.Fori(0, KR) as i:
                    rnd = half * KR + i

                    def hidden(tb, m):
                        n = tb * HT0 + m
                        r = rows[m]
                        dve.wait_ge(silu_made, rnd * NHID + n + 1)
                        dve.wait_ge(hid_made, at(rnd, NHID, n - 2))
                        up = bank[3 + n % 3][:] if r == P else bank[n % 3][HALF:P, :]
                        dve.tensor_tensor(prod[0:r, n % 3, :], silu[0:r, n % 2, :], up, ALU.mult)\
                           .then_inc(prod_made, 1)

                    def scan(n, step):
                        s, q = n // CK, n % CK
                        k_row = rkw[:, s % 2]
                        k_base = 2 * CK * rnd + CK * (s // 2)
                        if step < VQ:
                            if step == 0:
                                dve.wait_ge(kv_made, rnd * NCH + n + 1)
                                if q:
                                    dve.wait_ge(y_added[s % 2], k_base + q)
                                elif s:
                                    dve.wait_ge(y_added[(s - 1) % 2], 2 * CK * rnd + CK * ((s - 1) // 2) + CK)
                                else:
                                    dve.wait_ge(y_added[1], 2 * CK * rnd)
                            dve.tensor_tensor_scan(fwd[:, step, :], k_row[:, 2, :], kv[:, n % 2, step, :], 0.0,
                                                   ALU.mult, ALU.add).then_inc(scanned[n % 2], 1)
                            dve.tensor_tensor_scan(bwd[:, step, T - 2::-1], kv[:, n % 2, step, T - 1:0:-1],
                                                   k_row[:, 2, T - 1:0:-1], 0.0, ALU.add, ALU.mult)\
                               .then_inc(scanned[n % 2], 1)
                        elif step == VQ:
                            dve.wait_ge(scanned[n % 2], VQ * NCH * rnd + 2 * VQ * (n // 2) + 2 * VQ)
                            dve.tensor_tensor(fwd[:], fwd[:], bwd[:], ALU.add).then_inc(summed, 1)
                            dve.wait_ge(summed, 2 * (rnd * NCH + n) + 1)
                            rr = k_row[:, 0, :].rearrange("p (o t) -> p o t", o=1).broadcast_to([P, VQ, T])
                            dve.tensor_tensor(fwd[:], fwd[:], rr, ALU.mult).then_inc(summed, 1)
                        else:
                            dve.wait_ge(summed, 2 * (rnd * NCH + n) + 2)
                            part = y[:, slot(half, q), :]
                            dve.tensor_tensor(part, part, fwd[:], ALU.add).then_inc(y_added[s % 2], 1)

                    def combine(tb):
                        for t in range(TT):
                            n = tb * TT + t
                            dve.wait_ge(down_ps, rnd * NY + n // 2 * 2 + 2)
                            dve.wait_ge(x_in, 16)
                            dve.wait_ge(combined, rnd * NY)
                            row = ffn[:, n, :]
                            dve.scalar_tensor_tensor(row, outputs(n), w0[:, n, bass.ds(rnd, 1)], row,
                                                     ALU.mult, ALU.add).then_inc(combined, 1)

                    spread = [[(0, 0)], [(0, 1)], [(0, 2)], [(0, 3), (1, 0)], [(1, 1)], [(1, 2), (1, 3)]]
                    for tb in range(NB):
                        for m in range(HT0):
                            hidden(tb, m)
                            for chunk, step in spread[m]:
                                scan(2 * tb + chunk, step)
                        if tb:
                            combine(tb - 1)
                    combine(NB - 1)

        @block.scalar
        def _(act):
            for half in range(2):
                with act.Fori(0, KR) as i:
                    rnd = half * KR + i
                    act.wait_ge(up_in, 16 * rnd + 16)
                    act.wait_ge(up_ps, rnd * NHID)
                    act.activation(up_h[:], up_raw[:], ACT.Copy).then_inc(up_h_made, 1)
                    act.wait_ge(down_in, 16 * rnd + 16)
                    act.wait_ge(down_ps, rnd * NY)
                    act.activation(down_h[:], down_raw[:], ACT.Copy).then_inc(down_h_made, 1)
                    for n in range(NHID + 1):
                        if n < NHID:
                            r = rows[n % HT0]
                            act.wait_ge(up_ps, rnd * NHID + n + 1)
                            act.wait_ge(prod_made, at(rnd, NHID, n - 1))
                            act.activation(silu[0:r, n % 2, :], bank[n % 3][0:r, :], ACT.Silu)\
                               .then_inc(silu_made, 1)
                        if n:
                            k = n - 1
                            r = rows[k % HT0]
                            act.wait_ge(prod_made, rnd * NHID + k + 1)
                            act.wait_ge(down_ps, at(rnd, NY, (k // HT0 - 1) * TT))
                            act.activation(hid_h[0:r, (k // HT0) % 2, k % HT0], prod[0:r, k % 3, :], ACT.Copy)\
                               .then_inc(hid_h_made, 1)

        @block.tensor
        def _(pe):
            pe.wait_ge(cleared, 3)
            with pe.Fori(0, E0) as e:
                def three(ps, wh, wl, xs, first, last):
                    for n, (w, x) in enumerate(((wh, xs[0]), (wh, xs[1]), (wl, xs[0]))):
                        ins = pe.matmul(ps, w, x, start=first and n == 0, stop=last and n == 2)
                    return ins

                def up(tb):
                    for m in range(HT0):
                        n = tb * HT0 + m
                        pe.wait_ge(prod_made, at(e, NHID, n - 2))
                        for j, tile in enumerate([m, HT0 + m] if m < HT0 - 1 else [HT0 - 1]):
                            cols = slice(tile * P, (tile + 1) * P)
                            for c in range(C2):
                                toks = slice(tb * T, (tb + 1) * T)
                                ins = three(bank[3 * j + n % 3][:], up_h[:, c, cols], up_l[:, c, cols],
                                            (xh[:, c, toks], xl[:, c, toks]), c == 0, c == C2 - 1)
                        ins.then_inc(up_ps, 1)

                def down(tb):
                    pe.wait_ge(hid_made, e * NHID + (tb + 1) * HT0)
                    for t in range(TT):
                        n = tb * TT + t
                        pe.wait_ge(combined, at(e, NY, n // 2 * 2 - 2))
                        cols = slice(t * P, (t + 1) * P)
                        for m in range(HT0):
                            hs = (hid_h[:, tb % 2, m, cols], hid_l[:, tb % 2, m, cols])
                            ws = (down_h[:, m], down_l[:, m])
                            for k, (hp, wp) in enumerate(((0, 0), (0, 1), (1, 0))):
                                ins = pe.matmul(outputs(n), hs[hp], ws[wp],
                                                start=m == 0 and k == 0, stop=m == HT0 - 1 and k == 2)
                        ins.then_inc(down_ps, 1)

                pe.wait_ge(up_made, e + 1)
                for tb in range(NB):
                    up(tb)
                    if tb == 1:
                        pe.wait_ge(down_made, e + 1)
                    if tb:
                        down(tb - 1)
                down(NB - 1)


def layer_one(nc, a, scratch, keep, out):
    with ExitStack() as ctx:
        def sb(name, shape, dt=F32):
            return ctx.enter_context(nc.sbuf_tensor("b3_" + name, shape, dt))

        def sem(name):
            return ctx.enter_context(nc.semaphore("b3_" + name))

        bank = [ctx.enter_context(nc.psum_tensor(f"b3_bank{n}", [P, 512], F32)) for n in range(8)]
        ident = keep["ident"]
        NH = H * TT
        QK, QKV = 320, 384
        NQ = QK // K
        R3 = 3 * K
        R6 = 2 * R3
        QT = H // 2
        TURNED = (3, 0, 1, 2, 3)
        identb = sb("identb", [P, P], BF16)
        identh = sb("identh", [P, P], F16)
        causal = sb("causal", [P, P], BF16)
        window = sb("window", [P, P + 64], BF16)
        rope = sb("rope", [P, 2, 2, TT, K])
        slot_of = sb("slot_of", [P, 2])
        eps = sb("eps", [P, 16])
        sel = sb("sel", [48, RT1, P], BF16)
        before16 = sb("before16", [P, E1 * E1])
        before4 = sb("before4", [P, G4 * G4])
        bias_r = sb("bias_r", [P, E1])
        ln_wb = sb("ln_wb", [P, 2, C2])
        norm_w = sb("norm_w", [P, 2, C2])
        wo0 = sb("rwkv_wo", [P, C2, D])
        wq = [sb(f"wq{n}", [P, C2, QKV if n else D]) for n in range(2)]
        wd = sb("wd", [P, C2, LAT])
        kv_up = sb("kv_up", [LAT, P])
        wo = [sb(f"attn_wo{n}", [P, C2, D]) for n in range(2)]
        route_w = sb("route_w", [P, C2, E1])
        up_h = sb("up_h", [P, 2, C2, MT1 * P], F16)
        up_l = sb("up_l", [P, 2, C2, MT1 * P], F16)
        down_h = sb("down_h", [P, MT1, D], F16)
        down_l = sb("down_l", [P, MT1, D], F16)
        y = sb("y", [P, C2, T])
        gate = sb("gate", [P, C2, T])
        g = sb("g", [P, C2, T])
        x_tok = sb("x_tok", [P, TT, D])
        g1 = sb("g1", [P, TT * D])
        g2 = sb("g2", [P, TT * D])
        w1 = sb("w1", [P, TT * QK])
        w2 = sb("w2", [P, TT * QK])
        parts = sb("parts", [P, TT, NQ, 3, K], F16)
        gn = sb("gn", [P, 4, NH])
        small = sb("small", [P, 5, NH])
        qn = sb("qn", [P, 3, TT * NQ])
        x1 = sb("x1", [P, TT, D])
        acc = sb("acc", [P, TT, D])
        stats = sb("stats", [P, TT, 6])
        mv = sb("mv", [P, TT, 2])
        rstd = sb("rstd", [P, 2, TT])
        xn = sb("xn", [P, TT, D])
        xT = sb("xT", [P, C2, T])
        xh = sb("xh", [P, C2, T], F16)
        xl = sb("xl", [P, C2, T], F16)
        holds_wait = sb("holds_wait", [P, 3])
        arena = sb("arena", [P, MT1 * T + 2 * T + 4 * T + 384 * 4])
        th = sb("th", [P, 2, T])
        prod = sb("prod", [P, 2, T])
        ss = sb("ss", [P, 2, TT])
        rs = sb("rs", [P, 2, 2, TT])
        qkv = sb("qkv", [P, TT, QKV])
        qT = sb("qT", [P, QT, T], F16)
        onT = sb("onT", [P, C2, T])
        oT = sb("oT", [P, T])
        v1 = sb("v1", [P, TT, KVH, 32])
        den = sb("den", [P, 4, NH // 4])
        sc = sb("sc", [P, TT, E1])
        cbp = sb("cbp", [P, TT, 3, E1], BF16)
        cbT = sb("cbT", [48, T], BF16)

        hid_h = arena[:, 0:MT1 * T // 2].bitcast(BF16).rearrange("p (m t) -> p m t", t=T)
        hid_l = arena[:, MT1 * T // 2:MT1 * T].bitcast(F16).rearrange("p (m t) -> p m t", t=T)
        KZ = MT1 * T
        kz = arena[:, KZ:KZ + KVH * T // 2].bitcast(F16).rearrange("p (m t) -> p m t", t=T)
        PR = KZ + KVH * T // 2
        prob = [arena[:, PR:PR + 4 * T].rearrange("p (h t) -> p h t", t=T),
                arena[:, PR + 4 * T:PR + 4 * T + 4 * 384].rearrange("p (h t) -> p h t", t=384)]
        up_raw = arena[:, 0:2 * C2 * MT1 * P].rearrange("p (n c m) -> p n c m", n=2, c=C2)
        RAW = 2 * C2 * MT1 * P
        down_raw = arena[:, RAW:RAW + MT1 * D].rearrange("p (m n) -> p m n", n=D)
        yt = g1[:].rearrange("p (n d) -> p n d", d=K)
        ysq = g2[:].rearrange("p (n d) -> p n d", d=K)
        yl = g2[:].rearrange("p (c t) -> p c t", t=T)
        o_tok = w1[:, 0:TT * D].rearrange("p (t n) -> p t n", n=D)
        xb = y[:].rearrange("p c t -> p (c t)").rearrange("p (t n) -> p t n", n=D)
        lat = prod[0:LAT, 1]
        squares = parts[:].rearrange("p t n s d -> p (t n s d)")[:, 0:2 * TT * QK].bitcast(F32)
        sq = th[:, 0, 0:D]
        rk = w1[:, TT * E1 * E1:TT * E1 * E1 + 4 * TT * E1].rearrange("p (s n) -> p s n", s=4)
        sbias = w2[:, TT * E1 * E1:TT * E1 * E1 + TT * E1]
        crest = w2[:, TT * E1 * E1 + TT * E1:TT * E1 * E1 + 2 * TT * E1].rearrange("p (t e) -> p t e", e=E1)

        names = ("first_in", "weights_in", "raw_in", "setup", "ones_made", "wh_made", "wl_made", "y_in", "gate_in", "g_in",
                 "x_in", "ya_made", "yT_ps", "yt_out", "gn_var", "gn_std", "yn_made", "ynT_ps", "yl_made",
                 "ag_made", "wo_ps", "x1_made", "ln_var", "ln_sum", "ln_std", "xn_made", "xT_ps", "xT_out", "xl_made",
                 "route_ps", "sc_out", "cb_made", "cbT_ps", "cbT_out", "up_ps", "tanh_made", "gated", "prod_made",
                 "cb_ps", "hid_made", "hid_h_made", "hid_l_made", "fy_ps", "fy_used", "ss_made", "rs_sum", "rs_made",
                 "xbT_ps", "xbT_out", "lat_ps", "lat_out", "qkv_ps", "qkv_out", "squared", "qn_sum", "qn_std",
                 "hi_made", "hi_copied", "qk_made", "v_made", "qkT_ps", "qkT_out", "kz_made", "score_ps", "exp_out", "pv_ps", "oT_out",
                 "ot_ps", "o_made", "onT_ps", "onT_out", "ao_ps", "xb_made", "acc_made", "fin_made", "stored")
        s = {n: sem(n) for n in names}
        own_head, own_sem = sem("dve_own_head"), sem("dve_own")

        ORDER = list(range(RT1, MT1)) + list(range(RT1))
        NSH = MT1 - RT1
        assert (NSH, RT1) == (4, 8)
        MIDDLE, LAST = (None, 7, 9, 11), (6, 8, 10, None)
        groups = []
        for layer in range(2):
            for j in range(4):
                for i in range(TT):
                    width = T - P * i if layer == 0 else min(P + 64, T - P * i)
                    per = 4 if 4 * width <= 512 else 2 if 2 * width <= 512 else 1
                    for g0 in range(0, KVH, per):
                        groups.append((layer, j, i, list(range(g0, g0 + per)), P * i, width))
        NG = len(groups)

        def groups_of(layer, j, i):
            return [(n, x[3], x[4], x[5]) for n, x in enumerate(groups) if x[:3] == (layer, j, i)]

        def groups_until(layer, j, i):
            return sum(1 for x in groups if x[:3] <= (layer, j, i))

        block = ctx.enter_context(nc.Block())

        first_loads = [(eps[:], "c_eps"), (ln_wb[:], "ln_wb"), (wo0[:], "Wo")]
        loads = [(identb[:], "c_identb"), (identh[:], "c_identh"), (causal[:], "c_causal"), (window[:], "c_window"), (rope[:], "c_rope"),
                 (slot_of[:], "c_slot"), (sel[:], "c_sel"), (before16[:], "c_before16"),
                 (before4[:], "c_before4"), (bias_r[:], "bias_r"), (norm_w[:], "norm_w"),
                 (wq[0][:], "g_wq"), (wq[1][:], "l_wqkv"), (wd[:], "g_kv_down"),
                 (kv_up[:], "g_kv_up"), (wo[0][:], "g_wo"), (wo[1][:], "l_wo"), (route_w[:], "router_w")]
        FIRST_LOADED, LOADED = 16 * len(first_loads), 16 * len(loads)
        SETUP = 3 * C2

        @block.sync
        def _(sp):
            chan = "(b c p) t -> b p c t"

            def load_head(n, used=0, used_2=0):
                if not isinstance(n, int):
                    sp.wait_ge(s["acc_made"], used)
                    sp.wait_ge(s["v_made"], used_2)
                if not isinstance(n, int) or n:
                    sp.wait_ge(s["yT_ps"], TT * n)
                sp.dma_start(y[:], scratch["y"].rearrange(chan, c=C2, p=P)[n]).then_inc(s["y_in"], 16)
                sp.dma_start(gate[:], scratch["gate"].rearrange(chan, c=C2, p=P)[n]).then_inc(s["gate_in"], 16)
                if not isinstance(n, int) or n:
                    sp.wait_ge(s["ag_made"], 2 * n)
                sp.dma_start(g[:], scratch["g"].rearrange(chan, c=C2, p=P)[n]).then_inc(s["g_in"], 16)
                if not isinstance(n, int) or n:
                    sp.wait_ge(s["x1_made"], 2 * n)
                sp.dma_start(x_tok[:], scratch["ffn"][:, bass.ds(n * TT, TT), :]).then_inc(s["x_in"], 16)

            def store(b):
                sp.wait_ge(s["fin_made"], 2 * b + 2)
                sp.dma_start(out[b], acc[:]).then_inc(s["stored"], 16)

            load_head(0)
            load_head(1)
            with sp.Fori(0, NB - 2) as b:
                load_head(b + 2, b + 1, 2 * b + 2)
                store(b)
            store(NB - 2)
            store(NB - 1)
            sp.wait_ge(s["stored"], 16 * NB)

        @block.gpsimd
        def _(pool):
            pool.memset(v1[:], 1.0).then_inc(s["ones_made"], 1)
            pool.wait_ge(s["ones_made"], 1)

            def gate_heads(n):
                pool.wait_ge(s["g_in"], 16 * n + 16)
                for c in range(C2):
                    pool.wait_ge(s["yl_made"], 2 * n + c + 1)
                    pool.tensor_tensor(yl[:, c], yl[:, c], g[:, c], ALU.mult).then_inc(s["ag_made"], 1)

            def layer_norm_factor(n):
                pool.wait_ge(s["ln_var"], n + 1)
                pool.wait_ge(s["xn_made"], TT * n)
                pool.tensor_tensor(rstd[:, 0], mv[:, :, 1], eps[:, 4:8], ALU.add).then_inc(s["ln_sum"], 1)
                pool.wait_ge(s["ln_sum"], n + 1)
                pool.tensor_tensor(rstd[:, 1], rstd[:, 0], eps[:, 12:16], ALU.pow).then_inc(s["ln_std"], 1)

            def rms_factor(layer, count, n):
                pool.wait_ge(s["ss_made"], 2 * TT * n + TT * layer + TT)
                pool.wait_ge(s["qkv_out"], count)
                pool.tensor_tensor(rs[:, layer, 0], ss[:, layer], eps[:, 8:12], ALU.add).then_inc(s["rs_sum"], 1)
                pool.wait_ge(s["rs_sum"], 2 * n + layer + 1)
                pool.tensor_tensor(rs[:, layer, 1], rs[:, layer, 0], eps[:, 12:16], ALU.pow)\
                    .then_inc(s["rs_made"], 1)

            def low_x(n):
                for c in range(C2):
                    pool.wait_ge(s["xT_out"], 4 * n + 2 * c + 2)
                    pool.wait_ge(s["up_ps"], MT1 * n)
                    pool.tensor_tensor(xl[:, c], xT[:, c], xh[:, c], ALU.subtract).then_inc(s["xl_made"], 1)

            def low_hidden(b, n):
                pool.wait_ge(s["hid_h_made"], b * MT1 + n + 1)
                src = prod[:, n % 2]
                pool.tensor_tensor(hid_l[:, ORDER[n]], src, hid_h[:, ORDER[n]], ALU.subtract)\
                    .then_inc(s["hid_l_made"], 1)

            def values(b, layer):
                pool.wait_ge(s["qkv_out"], 8 * b + 4 * layer + 4)
                pool.wait_ge(s["pv_ps"], 32 * b + 16 * layer)
                pool.tensor_tensor(holds_wait[:, 1 + layer:2 + layer], eps[:, 0:1], eps[:, 0:1], ALU.add)
                pool.tensor_copy(v1[:, :, :, 0:K], qkv[:, :, QK:QKV].rearrange("p t (g d) -> p t g d", d=K))\
                    .then_inc(s["v_made"], 1)

            def head_end(n):
                layer_norm_factor(n)
                low_x(n)
                rms_factor(0, 8 * n, n)

            def body(b, more):
                for n in range(NSH):
                    low_hidden(b, n)
                    if n == 0:
                        values(b, 0)
                for n in range(NSH, MT1):
                    low_hidden(b, n)
                if more:
                    gate_heads(b + 1)
                pool.wait_ge(s["xb_made"], 2 * b + 2)
                pool.wait_ge(s["stored"], 16 * b)
                pool.tensor_tensor(acc[:], x1[:], xb[:], ALU.add).then_inc(s["acc_made"], 1)
                rms_factor(1, 8 * b, b)
                values(b, 1)
                if more:
                    head_end(b + 1)

            pool.wait_ge(s["first_in"], FIRST_LOADED)
            gate_heads(0)
            head_end(0)
            pool.wait_ge(s["wh_made"], 1)
            pool.tensor_tensor(up_l[:], up_raw, up_h[:], ALU.subtract).then_inc(s["wl_made"], 1)
            pool.wait_ge(s["wh_made"], 2)
            pool.tensor_tensor(down_l[:], down_raw, down_h[:], ALU.subtract).then_inc(s["wl_made"], 1)
            with pool.Fori(0, NB - 1) as b:
                body(b, True)
            body(NB - 1, False)

        each = "p (n o) -> p n o"

        @block.vector
        def _(dve):
            mine = Steps(dve, own_head, 44)
            own = Steps(dve, own_sem, 70)

            def gate_y(n):
                dve.wait_ge(s["y_in"], 16 * n + 16)
                dve.wait_ge(s["gate_in"], 16 * n + 16)
                for c in range(C2):
                    dve.scalar_tensor_tensor(y[:, c], gate[:, c], 1.0, y[:, c], ALU.add, ALU.mult)\
                       .then_inc(s["ya_made"], 1)

            mean, var, gstd, grstd = (gn[:, n] for n in range(4))

            def center_heads(n):
                mine.round(n)
                mine.settle()
                dve.wait_ge(s["cb_made"], n)
                dve.wait_ge(s["yt_out"], 2 * n + 2)
                mine.add(dve.reduce_sum(mean, yt, AX))
                mine.settle()
                mine.add(dve.tensor_scalar(mean, mean, 1.0 / K, None, ALU.mult))
                mine.settle()
                mine.add(dve.tensor_tensor(yt, yt, mean.rearrange(each, o=1).broadcast_to([P, NH, K]), ALU.subtract))

            def square_heads(n):
                mine.settle()
                dve.wait_ge(s["wo_ps"], TT * n)
                mine.add(dve.tensor_tensor(ysq, yt, yt, ALU.mult))
                mine.settle()
                dve.reduce_sum(var, ysq, AX).then_inc(s["gn_var"], 1)

            def scale_heads(n):
                dve.wait_ge(s["gn_std"], n + 1)
                mine.add(dve.reciprocal(grstd, gstd))
                mine.settle()
                dve.tensor_tensor(yt, yt, grstd.rearrange(each, o=1).broadcast_to([P, NH, K]), ALU.mult)\
                   .then_inc(s["yn_made"], 1)

            def residual(n):
                dve.wait_ge(s["x_in"], 16 * n + 16)
                dve.wait_ge(s["acc_made"], n)
                for h in range(2):
                    dve.wait_ge(s["wo_ps"], TT * n + 2 * h + 2)
                    dve.tensor_tensor(x1[:, 2 * h:2 * h + 2], bank[6 + h][:].rearrange("p (t n) -> p t n", n=D),
                                      x_tok[:, 2 * h:2 * h + 2], ALU.add).then_inc(s["x1_made"], 1)
                dve.wait_ge(s["x1_made"], 2 * n + 2)
                for t in range(TT):
                    mine.add(dve.bn_stats(stats[:, t], x1[:, t]))
                mine.settle()
                mine.add(dve.memset(holds_wait[:, 0:1], 0.0))
                for t in range(TT):
                    ins = dve.bn_aggr(mv[:, t], stats[:, t])
                    if t < TT - 1:
                        mine.add(ins)
                ins.then_inc(s["ln_var"], 1)

            def norm(n):
                dve.wait_ge(s["ln_std"], n + 1)
                dve.wait_ge(s["xb_made"], 2 * n)
                for t in range(TT):
                    dve.tensor_scalar(xn[:, t], x1[:, t], mv[:, t, 0:1], rstd[:, 1, t:t + 1],
                                      ALU.subtract, ALU.mult).then_inc(s["xn_made"], 1)

            def rank_in(dst, scores, n, table, op_rows):
                oth = scores.rearrange("p m (o e) -> p m o e", o=1).broadcast_to([P, op_rows, n, n])
                its = scores.rearrange("p m (e o) -> p m e o", o=1).broadcast_to([P, op_rows, n, n])
                size = op_rows * n * n
                gt, eq = g1[:, 0:size], g2[:, 0:size]
                four = dict(m=op_rows, e=n, j=n)
                mine.add(dve.tensor_tensor(gt.rearrange("p (m e j) -> p m e j", **four), oth, its, ALU.is_gt))
                mine.add(dve.tensor_tensor(eq.rearrange("p (m e j) -> p m e j", **four), oth, its, ALU.is_equal))
                mine.settle()
                rows = eq.rearrange("p (m n) -> p m n", n=n * n)
                mine.add(dve.tensor_tensor(rows, rows, table.rearrange("p (o n) -> p o n", o=1)
                                          .broadcast_to([P, op_rows, n * n]), ALU.mult))
                mine.settle()
                mine.add(dve.tensor_tensor(gt, gt, eq, ALU.add))
                mine.settle()
                mine.add(dve.reduce_sum(dst, gt.rearrange("p (n j) -> p n j", j=n), AX))
                mine.settle()

            NGR, EG = TT * G4, E1 // G4
            in_groups = sbias.rearrange("p (m e) -> p m e", e=EG)
            gsum, grank, gmask, gless = (small[:, n, 0:NGR] for n in range(4))
            wide = "p (m o) -> p m o"

            def group_sums(n, settle=True):
                if settle:
                    own.settle()
                dve.wait_ge(s["sc_out"], n + 1)
                dve.wait_ge(s["cbT_ps"], n)
                dve.wait_ge(s["ynT_ps"], 2 * n + 2)
                mine.add(dve.tensor_scalar(sc[:], sc[:], 0.5, 0.5, ALU.mult, ALU.add))
                mine.settle()
                mine.add(dve.tensor_tensor(sbias.rearrange("p (t e) -> p t e", e=E1), sc[:], bias_r[:].rearrange("p (o e) -> p o e", o=1)
                                          .broadcast_to([P, TT, E1]), ALU.add))
                mine.settle()
                rank_in(rk[:, 0, :], in_groups, EG, before4[:], NGR)
                mine.add(dve.scalar_tensor_tensor(rk[:, 1, :], rk[:, 0, :], 2.0, sbias, ALU.is_lt, ALU.mult))
                mine.settle()
                mine.add(dve.reduce_sum(gsum, rk[:, 1, :].rearrange("p (m e) -> p m e", e=EG), AX))

            def masked_scores():
                mine.settle()
                rank_in(grank, gsum.rearrange("p (t m) -> p t m", m=G4), G4, before4[:], TT)
                mine.add(dve.tensor_scalar(gmask, grank, 2.0, None, ALU.is_lt))
                mine.settle()
                mine.add(dve.tensor_scalar(gless, gmask, 1e30, -1e30, ALU.mult, ALU.add))
                inside = rk[:, 2, :].rearrange("p (m e) -> p m e", e=EG)
                mine.add(dve.tensor_tensor(inside, in_groups,
                                          gmask.rearrange(wide, o=1).broadcast_to([P, NGR, EG]), ALU.mult))
                mine.settle()
                mine.add(dve.tensor_tensor(rk[:, 3, :].rearrange("p (m e) -> p m e", e=EG), inside,
                                          gless.rearrange(wide, o=1).broadcast_to([P, NGR, EG]), ALU.add))

            def routing_weights():
                mine.settle()
                rank_in(rk[:, 0, :], rk[:, 3, :].rearrange("p (t e) -> p t e", e=E1), E1, before16[:], TT)
                mine.add(dve.scalar_tensor_tensor(rk[:, 1, :], rk[:, 0, :], 4.0,
                                                 sc[:].rearrange("p t e -> p (t e)"), ALU.is_lt, ALU.mult))
                mine.settle()
                total = small[:, 4, 0:TT]
                mine.add(dve.reduce_sum(total, rk[:, 1, :].rearrange("p (t e) -> p t e", e=E1), AX))
                mine.settle()
                mine.add(dve.tensor_scalar(total, total, 1e-20, None, ALU.add))
                mine.settle()
                mine.add(dve.reciprocal(small[:, 4, TT:2 * TT], total))
                mine.settle()
                weight = rk[:, 2, :].rearrange("p (t e) -> p t e", e=E1)
                mine.add(dve.tensor_tensor(weight, rk[:, 1, :].rearrange("p (t e) -> p t e", e=E1),
                                          small[:, 4, TT:2 * TT].rearrange("p (t o) -> p t o", o=1)
                                          .broadcast_to([P, TT, E1]), ALU.mult))
                mine.settle()
                mine.add(dve.tensor_copy(cbp[:, :, 0, :], weight))
                mine.settle()
                mine.add(dve.tensor_tensor(crest, weight, cbp[:, :, 0, :], ALU.subtract))
                mine.settle()
                mine.add(dve.tensor_copy(cbp[:, :, 1, :], crest))
                mine.settle()
                dve.tensor_tensor(cbp[:, :, 2, :], crest, cbp[:, :, 1, :], ALU.subtract).then_inc(s["cb_made"], 1)

            def product(b, n):
                pair = 4 + 2 * (n % 2)
                dve.wait_ge(s["tanh_made"], b * MT1 + n + 1)
                dve.wait_ge(s["hid_l_made"], at(b, MT1, n - 1))
                dve.scalar_tensor_tensor(prod[:, n % 2], th[:, n % 2], 1.0, bank[pair][:], ALU.add, ALU.mult)\
                   .then_inc(s["gated"], 1)
                dve.wait_ge(s["gated"], b * MT1 + n + 1)
                dve.tensor_tensor(prod[:, n % 2], prod[:, n % 2], bank[pair + 1][:], ALU.mult)\
                   .then_inc(s["prod_made"], 1)

            def weigh(b, n):
                dve.wait_ge(s["cb_ps"], b * RT1 + ORDER[n] + 1)
                dve.wait_ge(s["prod_made"], b * MT1 + n + 1)
                dve.tensor_tensor(prod[:, n % 2], prod[:, n % 2], bank[4 + 2 * (n % 2)][:], ALU.mult)\
                   .then_inc(s["hid_made"], 1)

            def experts_out(b):
                for h in range(2):
                    for t in range(2 * h, 2 * h + 2):
                        dve.wait_ge(s["fy_ps"], TT * b + 2 * h + 2)
                        dve.wait_ge(s["acc_made"], b + 1)
                        ins = dve.scalar_tensor_tensor(acc[:, t], bank[4 + t // 2][:, t % 2 * D:t % 2 * D + D], 0.5,
                                                       acc[:, t],
                                                       ALU.mult, ALU.add)
                        if t % 2 == 0:
                            own.add(ins)
                    ins.then_inc(s["fy_used"], 1)

            a_all = w1[:].rearrange("p (t n) -> p t n", n=QK)
            b_all = w2[:].rearrange("p (t n) -> p t n", n=QK)
            heads16 = "p (n d) -> p n d"

            def rotate(b, layer, t):
                if t == 0:
                    own.settle()
                    dve.wait_ge(s["onT_ps"], 4 * b + 2 * layer)
                    dve.wait_ge(s["cb_made"], b + 1)
                dve.wait_ge(s["qkv_out"], 8 * b + 4 * layer + t + 1)
                cos, sin = (rope[:, layer, n, t].rearrange("p (o d) -> p o d", o=1).broadcast_to([P, NQ, K])
                            for n in range(2))
                own.add(dve.tensor_tensor(a_all[:, t].rearrange(heads16, d=K),
                                          qkv[:, t, 0:QK].rearrange(heads16, d=K), cos, ALU.mult))
                pairs = "p (n m two) -> p n m two"
                sin4 = rope[:, layer, 1, t].rearrange("p (o m two) -> p o m two", o=1, two=2)\
                    .broadcast_to([P, NQ, K // 2, 2])
                for e in range(2):
                    own.add(dve.tensor_tensor(
                        b_all[:, t].rearrange(pairs, m=K // 2, two=2)[:, :, :, e],
                        qkv[:, t, 0:QK].rearrange(pairs, m=K // 2, two=2)[:, :, :, 1 - e],
                        sin4[:, :, :, e], ALU.mult))

            def rotated(b, layer):
                own.settle()
                own.add(dve.tensor_tensor(w1[:], w1[:], w2[:], ALU.add))
                own.settle()

            def square_sums(b, layer):
                dve.wait_ge(s["squared"], 8 * b + 4 * layer + 4)
                dve.reduce_sum(qn[:, 0], squares.rearrange(heads16, d=K), AX).then_inc(s["qn_sum"], 1)

            def norm_qk(b, layer):
                L2 = 2 * b + layer
                dve.wait_ge(s["qn_std"], L2 + 1)
                dve.wait_ge(s["qkT_ps"], 5 * L2)
                own.add(dve.reciprocal(qn[:, 2], qn[:, 1]))
                own.settle()
                for t in range(TT):
                    mine_t = a_all[:, t].rearrange(heads16, d=K)
                    own.add(dve.tensor_tensor(
                        mine_t, mine_t,
                        qn[:, 2, NQ * t:NQ * t + NQ].rearrange(each, o=1).broadcast_to([P, NQ, K]), ALU.mult))
                own.settle()
                whole = w1[:].rearrange("p (t n d) -> p t n d", t=TT, d=K)
                dve.tensor_copy(parts[:, :, :, 0], whole).then_inc(s["hi_made"], 1)
                dve.wait_ge(s["hi_made"], L2 + 1)
                for heads, part in ((slice(0, H), 1), (slice(H, NQ), 2)):
                    dve.tensor_tensor(parts[:, :, heads, part], whole[:, :, heads], parts[:, :, heads, 0],
                                      ALU.subtract).then_inc(s["qk_made"], 1)

            def mask_k(b, layer):
                dve.wait_ge(s["qkT_ps"], 10 * b + 5 * layer + 1)
                dve.wait_ge(s["wl_made"], 2)
                dve.wait_ge(s["score_ps"], b * NG + (groups_until(0, 4, 4) if layer else 0))
                both = bank[TURNED[0]][0:R6].bitcast(F16).rearrange("p (m t) -> p m t", t=T)
                for n in range(KVH):
                    dve.tensor_scalar(kz[0:R6, n], both[:, n // 2], slot_of[0:R6, n % 2:n % 2 + 1], None, ALU.mult)\
                       .then_inc(s["kz_made"], 1)

            def over_sums(b, layer, j):
                dve.wait_ge(s["ot_ps"], 8 * b + 4 * layer + j + 1)
                ps = bank[3][:].rearrange("p (n d) -> p n d", d=32)
                own.add(dve.reciprocal(den[:, j], ps[:, :, K]))
                own.settle()
                for t in range(TT):
                    ins = dve.tensor_tensor(
                        o_tok[:, t, 64 * j:64 * j + 64].rearrange("p (g d) -> p g d", d=K),
                        ps[:, 4 * t:4 * t + 4, 0:K],
                        den[:, j, 4 * t:4 * t + 4].rearrange(each, o=1).broadcast_to([P, 4, K]), ALU.mult)
                    if t < TT - 1:
                        own.add(ins)
                ins.then_inc(s["o_made"], 1)

            def attention_out(b, layer, more):
                for h in range(2):
                    dve.wait_ge(s["ao_ps"], 8 * b + 4 * layer + 2 * h + 2)
                    ps = bank[2 + h][:].rearrange("p (t n) -> p t n", n=D)
                    part = slice(2 * h, 2 * h + 2)
                    if layer == 0:
                        dve.wait_ge(s["acc_made"], b)
                        dve.wait_ge(s["yT_ps"], TT * b + (2 * TT if more else TT))
                        dve.tensor_tensor(xb[:, part], ps, xn[:, part], ALU.add).then_inc(s["xb_made"], 1)
                    else:
                        dve.wait_ge(s["fy_used"], 2 * b + 2)
                        own.settle()
                        dve.tensor_tensor(acc[:, part], ps, acc[:, part], ALU.add).then_inc(s["fin_made"], 1)

            def body(b, more):
                own.round(b)
                for t in range(TT):
                    rotate(b, 0, t)
                square_sums(b, 0)
                rotated(b, 0)
                product(b, 0)
                product(b, 1)
                norm_qk(b, 0)
                product(b, 2)
                mask_k(b, 0)
                product(b, 3)
                if more:
                    gate_y(b + 1)
                product(b, 4)
                product(b, 5)
                weigh(b, 4)
                for j in range(4):
                    if j:
                        weigh(b, MIDDLE[j] - 1)
                        product(b, MIDDLE[j])
                        over_sums(b, 0, j - 1)
                    if more and j == 2:
                        square_heads(b + 1)
                    if more and j == 3:
                        scale_heads(b + 1)
                    if j < 3:
                        weigh(b, LAST[j] - 1)
                        product(b, LAST[j])
                    if more and j == 1:
                        center_heads(b + 1)
                weigh(b, MT1 - 1)
                over_sums(b, 0, 3)
                attention_out(b, 0, more)
                for t in range(TT):
                    rotate(b, 1, t)
                square_sums(b, 1)
                rotated(b, 1)
                if more:
                    residual(b + 1)
                norm_qk(b, 1)
                if more:
                    norm(b + 1)
                experts_out(b)
                mask_k(b, 1)
                over_sums(b, 1, 0)
                over_sums(b, 1, 1)
                if more:
                    group_sums(b + 1)
                over_sums(b, 1, 2)
                if more:
                    masked_scores()
                over_sums(b, 1, 3)
                if more:
                    routing_weights()
                    mine.end()
                attention_out(b, 1, more)
                own.end()

            gate_y(0)
            center_heads(0)
            square_heads(0)
            scale_heads(0)
            residual(0)
            norm(0)
            dve.wait_ge(s["weights_in"], LOADED)
            for c in range(C2):
                for w, layer in ((wq[0], 0), (wd, 0), (wq[1], 1)):
                    dve.tensor_scalar(w[:, c], w[:, c], norm_w[:, layer, c:c + 1], None, ALU.mult)\
                       .then_inc(s["setup"], 1)
            group_sums(0, settle=False)
            masked_scores()
            routing_weights()
            mine.end()
            with dve.Fori(0, NB - 1) as b:
                body(b, True)
            body(NB - 1, False)

        @block.scalar
        def _(act):
            for dst, name in first_loads:
                act.dma_start(dst, a[name]).then_inc(s["first_in"], 16)
            act.dma_start(up_raw, a["ffn1_up"]).then_inc(s["raw_in"], 16)
            for dst, name in loads:
                act.dma_start(dst, a[name]).then_inc(s["weights_in"], 16)
            act.dma_start(down_raw, a["ffn1_down"]).then_inc(s["raw_in"], 16)

            def half_y(n):
                for h in range(2):
                    act.wait_ge(s["yT_ps"], TT * n + 2 * h + 2)
                    act.wait_ge(s["ynT_ps"], 2 * n)
                    act.wait_ge(s["cb_made"], n)
                    act.activation(g1[:, 512 * h:512 * h + 512], bank[4 + h][:], ACT.Copy, scale=0.5)\
                       .then_inc(s["yt_out"], 1)

            def head_std(n):
                act.wait_ge(s["gn_var"], n + 1)
                act.wait_ge(s["yn_made"], n)
                act.activation(gn[:, 2], gn[:, 1], ACT.Sqrt, bias=eps[:, 0:1], scale=1.0 / K)\
                   .then_inc(s["gn_std"], 1)

            def affine(n):
                for c in range(C2):
                    act.wait_ge(s["ynT_ps"], 2 * n + c + 1)
                    act.wait_ge(s["wo_ps"], TT * n)
                    act.activation(yl[:, c], bank[4 + c][:], ACT.Identity, bias=ln_wb[:, 1, c:c + 1],
                                   scale=ln_wb[:, 0, c:c + 1]).then_inc(s["yl_made"], 1)

            def square_mean(layer, n, src, ready, count, tiles=range(TT)):
                for t in tiles:
                    act.wait_ge(ready, count)
                    act.wait_ge(s["ss_made"], 2 * TT * n + TT * layer + t)
                    act.activation(sq, src[:, t], ACT.Square, scale=1.0 / 16.0,
                                   accum_out=ss[:, layer, t:t + 1]).then_inc(s["ss_made"], 1)

            assert D == 16 * 16

            def copy_xT(n, halves=range(C2)):
                for c in halves:
                    act.wait_ge(s["xT_ps"], 2 * n + c + 1)
                    act.wait_ge(s["qkv_ps"], 8 * n)
                    act.wait_ge(s["up_ps"], MT1 * n)
                    act.wait_ge(s["xl_made"], 2 * n)
                    act.activation(xh[:, c], bank[6 + c][:], ACT.Copy).then_inc(s["xT_out"], 1)
                    act.activation(xT[:, c], bank[6 + c][:], ACT.Copy).then_inc(s["xT_out"], 1)

            def sc_tanh(n):
                act.wait_ge(s["route_ps"], n + 1)
                act.wait_ge(s["cb_made"], n)
                act.activation(sc[:], bank[7][:, 0:TT * E1].rearrange("p (t e) -> p t e", e=E1), ACT.Tanh, scale=0.5)\
                   .then_inc(s["sc_out"], 1)

            def gate_tanh(b, n):
                act.wait_ge(s["up_ps"], b * MT1 + n + 1)
                act.wait_ge(s["gated"], at(b, MT1, n - 1))
                act.activation(th[:, n % 2], bank[4 + 2 * (n % 2)][:], ACT.Tanh, scale=0.5)\
                   .then_inc(s["tanh_made"], 1)

            def high_hidden(b, n):
                if n < NSH:
                    act.wait_ge(s["prod_made"], b * MT1 + n + 1)
                else:
                    act.wait_ge(s["hid_made"], b * RT1 + ORDER[n] + 1)
                act.wait_ge(s["fy_ps"], TT * b)
                act.activation(hid_h[:, ORDER[n]], prod[:, n % 2], ACT.Copy).then_inc(s["hid_h_made"], 1)

            def copy_qkv(b, layer):
                L2 = 2 * b + layer
                if layer == 0:
                    act.wait_ge(s["lat_ps"], b + 1)
                    act.wait_ge(s["hid_l_made"], MT1 * b)
                    act.activation(lat, bank[4][0:LAT, :], ACT.Copy).then_inc(s["lat_out"], 1)
                act.wait_ge(s["rs_made"], L2 + 1)
                act.wait_ge(s["v_made"], L2)
                for t in range(TT):
                    act.wait_ge(s["qkv_ps"], 4 * L2 + t + 1)
                    act.activation(qkv[:, t], bank[t][:, 0:QKV], ACT.Copy, scale=rs[:, layer, 1, t:t + 1])\
                       .then_inc(s["qkv_out"], 1)
                    act.wait_ge(s["qkT_ps"], 5 * L2)
                    act.activation(squares[:, t * QK:(t + 1) * QK], bank[t][:, 0:QK], ACT.Square,
                                   scale=rs[:, layer, 1, t:t + 1]).then_inc(s["squared"], 1)

            def qk_std(b, layer):
                act.wait_ge(s["qn_sum"], 2 * b + layer + 1)
                act.wait_ge(s["qk_made"], 2 * b + layer)
                act.activation(qn[:, 1], qn[:, 0], ACT.Sqrt, bias=eps[:, 2:3], scale=1.0 / K)\
                   .then_inc(s["qn_std"], 1)

            def copy_high(b, layer):
                L2 = 2 * b + layer
                act.wait_ge(s["hi_made"], L2 + 1)
                for heads, part in ((slice(0, H), 2), (slice(H, NQ), 1)):
                    act.activation(parts[:, :, heads, part], parts[:, :, heads, 0], ACT.Copy)\
                       .then_inc(s["hi_copied"], 1)

            def copy_qT(b, layer, n):
                L2 = 2 * b + layer
                act.wait_ge(s["qkT_ps"], 5 * L2 + n + 2)
                act.activation(qT[0:R6, 2 * n:2 * n + 2],
                               bank[TURNED[n + 1]][0:R6].bitcast(F16).rearrange("p (m t) -> p m t", t=T),
                               ACT.Copy).then_inc(s["qkT_out"], 1)

            def exponentials(b, layer, j, i):
                for n, heads, start, width in groups_of(layer, j, i):
                    act.wait_ge(s["score_ps"], b * NG + n + 1)
                    act.wait_ge(s["pv_ps"], at(b, 32, 16 * layer + 4 * j + i - 1))
                    src = bank[n % 2][:, 0:len(heads) * width].rearrange("p (h t) -> p h t", t=width)
                    act.activation(prob[i % 2][:, heads[0]:heads[0] + len(heads), 0:width], src, ACT.Exp,
                                   scale=0.25).then_inc(s["exp_out"], 1)

            def copy_oT(b, layer, j):
                act.wait_ge(s["pv_ps"], 32 * b + 16 * layer + 4 * j + 4)
                act.wait_ge(s["ot_ps"], 8 * b + 4 * layer + j)
                act.activation(oT[:], bank[2][:], ACT.Copy).then_inc(s["oT_out"], 1)

            def copy_onT(b, layer):
                for c in range(C2):
                    act.wait_ge(s["onT_ps"], 4 * b + 2 * layer + c + 1)
                    act.wait_ge(s["ao_ps"], 8 * b + 4 * layer)
                    act.activation(onT[:, c], bank[c][:], ACT.Copy).then_inc(s["onT_out"], 1)

            def body(b, more):
                copy_qkv(b, 0)
                qk_std(b, 0)
                act.wait_ge(s["cbT_ps"], b + 1)
                act.activation(cbT[:], bank[6][0:48, 0:T // 2].bitcast(BF16), ACT.Copy).then_inc(s["cbT_out"], 1)
                gate_tanh(b, 0)
                gate_tanh(b, 1)
                high_hidden(b, 0)
                copy_high(b, 0)
                gate_tanh(b, 2)
                high_hidden(b, 1)
                gate_tanh(b, 3)
                high_hidden(b, 2)
                for n in range(3):
                    copy_qT(b, 0, n)
                gate_tanh(b, 4)
                high_hidden(b, 3)
                gate_tanh(b, 5)
                for j in range(4):
                    exponentials(b, 0, j, 0)
                    high_hidden(b, NSH if j == 0 else LAST[j - 1] - 1)
                    if j:
                        copy_oT(b, 0, j - 1)
                        gate_tanh(b, MIDDLE[j])
                    exponentials(b, 0, j, 1)
                    if j == 0:
                        copy_qT(b, 0, 3)
                        if more:
                            half_y(b + 1)
                    exponentials(b, 0, j, 2)
                    if j:
                        high_hidden(b, MIDDLE[j] - 1)
                    exponentials(b, 0, j, 3)
                    if more and j == 2:
                        head_std(b + 1)
                    if j < 3:
                        gate_tanh(b, LAST[j])
                copy_oT(b, 0, 3)
                high_hidden(b, MT1 - 1)
                if more:
                    affine(b + 1)
                copy_onT(b, 0)
                square_mean(1, b, xb, s["xb_made"], 2 * b + 2)
                for c in range(C2):
                    act.wait_ge(s["xbT_ps"], 2 * b + c + 1)
                    act.activation(xT[:, c], bank[c][:], ACT.Copy).then_inc(s["xbT_out"], 1)
                copy_qkv(b, 1)
                qk_std(b, 1)
                copy_high(b, 1)
                for n in range(3):
                    copy_qT(b, 1, n)
                for j in range(4):
                    exponentials(b, 1, j, 0)
                    if j:
                        copy_oT(b, 1, j - 1)
                    for i in range(1, TT):
                        if more and j == 0 and i < 3:
                            square_mean(0, b + 1, xn, s["xn_made"], TT * (b + 1) + TT, (2 * i - 2, 2 * i - 1))
                        elif more and j == 0:
                            copy_xT(b + 1, [0])
                        exponentials(b, 1, j, i)
                        if j == 0 and i == 1:
                            copy_qT(b, 1, 3)
                    if more and j == 0:
                        copy_xT(b + 1, [1])
                    if more and j == 1:
                        sc_tanh(b + 1)
                copy_oT(b, 1, 3)
                copy_onT(b, 1)

            act.wait_ge(s["first_in"], FIRST_LOADED)
            half_y(0)
            head_std(0)
            affine(0)
            act.wait_ge(s["raw_in"], 32)
            act.activation(up_h[:].rearrange("p n c m -> p (n c m)"), up_raw.rearrange("p n c m -> p (n c m)"),
                           ACT.Copy).then_inc(s["wh_made"], 1)
            act.activation(down_h[:].rearrange("p m n -> p (m n)"), down_raw.rearrange("p m n -> p (m n)"),
                           ACT.Copy).then_inc(s["wh_made"], 1)
            square_mean(0, 0, xn, s["xn_made"], TT)
            copy_xT(0)
            sc_tanh(0)
            with act.Fori(0, NB - 1) as b:
                body(b, True)
            body(NB - 1, False)

        @block.tensor
        def _(pe):
            def turn_y(n):
                pe.wait_ge(s["ya_made"], 2 * n + 2)
                for t in range(TT):
                    for c in range(C2):
                        at_col = (t % 2) * D + c * P
                        ins = pe.transpose(bank[4 + t // 2][:, at_col:at_col + P], y[:, c, t * P:(t + 1) * P],
                                           ident[:])
                    ins.then_inc(s["yT_ps"], 1)

            def turn_yn(n):
                pe.wait_ge(s["yn_made"], n + 1)
                ytok = g1[:].rearrange("p (t n) -> p t n", n=D)
                for c in range(C2):
                    for t in range(TT):
                        ins = pe.transpose(bank[4 + c][:, t * P:(t + 1) * P], ytok[:, t, c * P:(c + 1) * P], ident[:])
                    ins.then_inc(s["ynT_ps"], 1)

            def rwkv_out(n):
                pe.wait_ge(s["ag_made"], 2 * n + 2)
                for t in range(TT):
                    for c in range(C2):
                        ins = pe.matmul(bank[6 + t // 2][:, (t % 2) * D:(t % 2) * D + D],
                                        yl[:, c, t * P:(t + 1) * P], wo0[:, c], start=c == 0, stop=c == C2 - 1)
                    ins.then_inc(s["wo_ps"], 1)

            def turn_x(n):
                for c in range(C2):
                    for t in range(TT):
                        if c == 0:
                            pe.wait_ge(s["xn_made"], TT * n + t + 1)
                        ins = pe.transpose(bank[6 + c][:, t * P:(t + 1) * P], xn[:, t, c * P:(c + 1) * P], ident[:])
                    ins.then_inc(s["xT_ps"], 1)

            def three(ps, wh, wl, vh, vl, first, last):
                for n, (w, v) in enumerate(((wh, vh), (wh, vl), (wl, vh))):
                    ins = pe.matmul(ps, w, v, start=first and n == 0, stop=last and n == 2)
                return ins

            def scores_of_experts(b):
                pe.wait_ge(s["xT_out"], 4 * b + 4)
                for t in range(TT):
                    for c in range(C2):
                        ins = pe.matmul(bank[7][:, t * E1:(t + 1) * E1], xT[:, c, t * P:(t + 1) * P],
                                        route_w[:, c, :], start=c == 0, stop=c == C2 - 1)
                ins.then_inc(s["route_ps"], 1)

            def up(b, n, halves=(0, 1)):
                m = ORDER[n]
                pair = 4 + 2 * (n % 2)
                if n >= 2 + NSH:
                    pe.wait_ge(s["hid_made"], b * RT1 + n - 2 - NSH + 1)
                else:
                    pe.wait_ge(s["prod_made"], at(b, MT1, n - 1))
                if n == 0:
                    pe.wait_ge(s["wl_made"], 1)
                    pe.wait_ge(s["xl_made"], 2 * b + 2)
                    pe.wait_ge(s["lat_out"], b + 1)
                if n == 1:
                    pe.wait_ge(s["sc_out"], b + 1)
                    pe.wait_ge(s["cbT_out"], b + 1)
                for half in halves:
                    for c in range(C2):
                        cols = slice(m * P, (m + 1) * P)
                        ins = three(bank[pair + half][:], up_h[:, half, c, cols], up_l[:, half, c, cols],
                                    xh[:, c], xl[:, c], c == 0, c == C2 - 1)
                if halves[-1] == 1:
                    ins.then_inc(s["up_ps"], 1)

            def turn_weights(b):
                for t in range(TT):
                    ins = pe.transpose(bank[6][0:48, 64 * t:64 * t + 64].bitcast(BF16),
                                       cbp[:, t].rearrange("p s e -> p (s e)"), identb[:])
                ins.then_inc(s["cbT_ps"], 1)

            def spread_weights(b, n):
                pe.wait_ge(s["cbT_out"], b + 1)
                pe.wait_ge(s["gated"], b * MT1 + n + 1)
                pe.matmul(bank[4 + 2 * (n % 2)][:], sel[:, ORDER[n]], cbT[:], start=True, stop=True)\
                  .then_inc(s["cb_ps"], 1)

            def down(b, t):
                pe.wait_ge(s["wl_made"], 2)
                pe.wait_ge(s["hid_l_made"], b * MT1 + MT1)
                cols = slice(t * P, (t + 1) * P)
                for m in range(MT1):
                    ins = three(bank[4 + t // 2][:, t % 2 * D:t % 2 * D + D], hid_h[:, m, cols], hid_l[:, m, cols], down_h[:, m],
                                down_l[:, m], m == 0, m == MT1 - 1)
                ins.then_inc(s["fy_ps"], 1)

            def project_qkv(b, layer):
                if layer == 0:
                    pe.wait_ge(s["xT_out"], 4 * b + 4)
                    pe.wait_ge(s["cb_made"], b + 1)
                    for c in range(C2):
                        ins = pe.matmul(bank[4][0:LAT, :], wd[:, c], xT[:, c], start=c == 0, stop=c == C2 - 1)
                    ins.then_inc(s["lat_ps"], 1)
                    pe.wait_ge(s["fin_made"], 2 * b)
                else:
                    pe.wait_ge(s["xbT_out"], 2 * b + 2)
                for t in range(TT):
                    tok = slice(t * P, (t + 1) * P)
                    if layer == 0:
                        for c in range(C2):
                            pe.matmul(bank[t][:, 0:D], xT[:, c, tok], wq[0][:, c], start=c == 0, stop=c == C2 - 1)
                        if t == 0:
                            pe.wait_ge(s["lat_out"], b + 1)
                        ins = pe.matmul(bank[t][:, D:QKV], lat[:, tok], kv_up[:], start=True, stop=True)
                    else:
                        for c in range(C2):
                            ins = pe.matmul(bank[t][:, 0:QKV], xT[:, c, tok], wq[1][:, c],
                                            start=c == 0, stop=c == C2 - 1)
                    ins.then_inc(s["qkv_ps"], 1)

            def turn_qk(b, layer, banks):
                L2 = 2 * b + layer
                pe.wait_ge(s["qk_made"], 2 * L2 + 2)
                pe.wait_ge(s["hi_copied"], 2 * L2 + 2)
                for n in banks:
                    if n == 4:
                        pe.wait_ge(s["kz_made"], 4 * L2 + 4)
                    to = bank[TURNED[n]][0:R6].bitcast(F16)
                    first = QT if n == 0 else 2 * n - 2
                    for m in range(2):
                        heads = slice(2 * (first + m), 2 * (first + m) + 2)
                        for t in range(TT):
                            ins = pe.transpose(to[:, m * T + t * P:m * T + (t + 1) * P],
                                               parts[:, t, heads].rearrange("p n s d -> p (n s d)"), identh[:])
                    ins.then_inc(s["qkT_ps"], 1)

            def score(b, layer, j, i, some=slice(None)):
                for n, heads, start, width in groups_of(layer, j, i)[some]:
                    first = 0 if layer == 0 else groups_until(0, 4, 4)
                    pe.wait_ge(s["exp_out"], at(b, NG, n - 1 if n - first >= 2 else first))
                    for x, h in enumerate(heads):
                        ps = bank[n % 2][:, x * width:(x + 1) * width]
                        pe.matmul(ps, kz[0:R6, h, i * P:(i + 1) * P],
                                  qT[0:R6, 2 * j + h // 2, start:start + width], start=True, stop=False)
                        masked = min(width, P if layer == 0 else P + 64)
                        mask = causal if layer == 0 else window
                        ins = pe.matmul(ps[:, 0:masked], identb[:], mask[:, 0:masked], start=False, stop=True)
                    ins.then_inc(s["score_ps"], 1)

            def attend(b, layer, j, i):
                pe.wait_ge(s["exp_out"], b * NG + groups_until(layer, j, i))
                if i == 0:
                    pe.wait_ge(s["oT_out"], 8 * b + 4 * layer + j)
                start = P * i
                end = T if layer == 0 else min(T, P * i + P + 64)
                parts = [(start, end)] if i == 0 or layer == 0 else [(start, start + 64), (start + 64, end)]
                for lo, hi in parts:
                    for h in range(KVH):
                        ins = pe.matmul(bank[2][32 * h:32 * h + 32, lo:hi], v1[:, i, h],
                                        prob[i % 2][:, h, lo - start:hi - start],
                                        start=i == 0, stop=hi == T and i == TT - 1)
                ins.then_inc(s["pv_ps"], 1)

            def turn_o(b, layer, j):
                pe.wait_ge(s["qkT_out"], 8 * b + 4 * layer + 4)
                pe.wait_ge(s["oT_out"], 8 * b + 4 * layer + j + 1)
                pe.wait_ge(s["o_made"], 8 * b + 4 * layer + j)
                for t in range(TT):
                    ins = pe.transpose(bank[3][:, t * P:(t + 1) * P], oT[:, t * P:(t + 1) * P], ident[:])
                ins.then_inc(s["ot_ps"], 1)

            def turn_heads(b, layer):
                pe.wait_ge(s["o_made"], 8 * b + 4 * layer + 4)
                for c in range(C2):
                    for t in range(TT):
                        ins = pe.transpose(bank[c][:, t * P:(t + 1) * P], o_tok[:, t, c * P:(c + 1) * P], ident[:])
                    ins.then_inc(s["onT_ps"], 1)

            def project_out(b, layer):
                pe.wait_ge(s["onT_out"], 4 * b + 2 * layer + 2)
                for t in range(TT):
                    for c in range(C2):
                        ins = pe.matmul(bank[2 + t // 2][:, (t % 2) * D:(t % 2) * D + D],
                                        onT[:, c, t * P:(t + 1) * P], wo[layer][:, c], start=c == 0, stop=c == C2 - 1)
                    ins.then_inc(s["ao_ps"], 1)

            def turn_xb(b):
                for c in range(C2):
                    for t in range(TT):
                        pe.wait_ge(s["xb_made"], 2 * b + t // 2 + 1)
                        ins = pe.transpose(bank[c][:, t * P:(t + 1) * P], xb[:, t, c * P:(c + 1) * P], ident[:])
                    ins.then_inc(s["xbT_ps"], 1)

            def body(b, more):
                project_qkv(b, 0)
                turn_weights(b)
                for n in range(4):
                    up(b, n)
                turn_qk(b, 0, range(4))
                up(b, 4)
                turn_qk(b, 0, [4])
                up(b, 5)
                spread_weights(b, 4)
                pe.wait_ge(s["qkT_out"], 8 * b + 3)
                pe.wait_ge(s["v_made"], 2 * b + 1)
                for j in range(4):
                    score(b, 0, j, 0, slice(0, 2))
                    if j:
                        spread_weights(b, MIDDLE[j] - 1)
                        up(b, MIDDLE[j], (0,))
                        attend(b, 0, j - 1, 3)
                    elif more:
                        pe.wait_ge(s["hid_made"], b * RT1 + 1)
                        turn_y(b + 1)
                    score(b, 0, j, 0, slice(2, 4))
                    if j:
                        up(b, MIDDLE[j], (1,))
                    score(b, 0, j, 1, slice(0, 2))
                    attend(b, 0, j, 0)
                    score(b, 0, j, 1, slice(2, 4))
                    if j:
                        turn_o(b, 0, j - 1)
                    score(b, 0, j, 2)
                    attend(b, 0, j, 1)
                    score(b, 0, j, 3)
                    attend(b, 0, j, 2)
                    if j < 3:
                        if more and j == 0:
                            pe.wait_ge(s["yt_out"], 2 * b + 4)
                        spread_weights(b, LAST[j] - 1)
                        up(b, LAST[j])
                spread_weights(b, MT1 - 1)
                attend(b, 0, 3, 3)
                turn_o(b, 0, 3)
                if more:
                    pe.wait_ge(s["hid_made"], b * RT1 + RT1 - 1)
                    turn_yn(b + 1)
                turn_heads(b, 0)
                project_out(b, 0)
                turn_xb(b)
                if more:
                    pe.wait_ge(s["hid_made"], b * RT1 + RT1)
                    rwkv_out(b + 1)
                project_qkv(b, 1)
                for t in range(TT):
                    down(b, t)
                turn_qk(b, 1, range(5))
                if more:
                    turn_x(b + 1)
                pe.wait_ge(s["qkT_out"], 8 * b + 7)
                pe.wait_ge(s["v_made"], 2 * b + 2)
                for j in range(4):
                    score(b, 1, j, 0)
                    if j:
                        attend(b, 1, j - 1, 3)
                    score(b, 1, j, 1)
                    attend(b, 1, j, 0)
                    if j:
                        turn_o(b, 1, j - 1)
                    if more and j == 1:
                        scores_of_experts(b + 1)
                    score(b, 1, j, 2)
                    attend(b, 1, j, 1)
                    score(b, 1, j, 3)
                    attend(b, 1, j, 2)
                attend(b, 1, 3, 3)
                turn_o(b, 1, 3)
                turn_heads(b, 1)
                project_out(b, 1)

            turn_y(0)
            turn_yn(0)
            pe.wait_ge(s["first_in"], FIRST_LOADED)
            rwkv_out(0)
            turn_x(0)
            pe.wait_ge(s["weights_in"], LOADED)
            pe.wait_ge(s["setup"], SETUP)
            scores_of_experts(0)
            with pe.Fori(0, NB - 1) as b:
                body(b, True)
            body(NB - 1, False)


def _constants(np):
    bf16 = np.dtype("bfloat16")
    eye = np.eye(P, dtype=np.float32)
    before = lambda n: np.tile((np.arange(n)[None, :] < np.arange(n)[:, None]).astype(np.float32).reshape(1, n * n),
                               (P, 1))
    s, t = np.arange(P)[:, None], np.arange(P + 64)[None, :]
    causal = np.where(t[:, :P] < s, np.float32(-1e30), np.float32(0))
    window = np.where((t < s) | (t - s >= 64), np.float32(-1e30), np.float32(0))
    rope = np.zeros((P, 2, 2, TT, K // 2, 2), np.float32)
    for layer, base in enumerate((1000000.0, 10000.0)):
        inv = (1.0 / np.float32(base) ** (np.arange(0, K, 2, dtype=np.float32) / np.float32(K))).astype(np.float32)
        ang = np.arange(T, dtype=np.float32)[:, None] * inv[None, :]
        cos = np.cos(ang).astype(np.float32).reshape(TT, P, 8).transpose(1, 0, 2)
        sin = np.sin(ang).astype(np.float32).reshape(TT, P, 8).transpose(1, 0, 2)
        rope[:, layer, 0] = cos[:, :, :, None]
        rope[:, layer, 1, :, :, 0] = -sin
        rope[:, layer, 1, :, :, 1] = sin
    slot = (np.arange(P)[:, None] // (3 * K) == np.arange(2)[None, :]).astype(np.float32)
    sel = np.zeros((48, RT1, P), np.float32)
    for m in range(RT1):
        for p in range(P):
            sel[[2 * m + p // H1, E1 + 2 * m + p // H1, 2 * E1 + 2 * m + p // H1], m, p] = 1.0
    return {
        "c_ident": eye, "c_before8": before(E0), "c_identb": eye.astype(bf16),
        "c_identh": eye.astype(np.float16),
        "c_causal": causal.astype(bf16), "c_window": window.astype(bf16),
        "c_rope": rope.reshape(P, 2, 2, TT, K), "c_slot": slot,
        "c_eps": np.tile(np.array([[1e-5 * 64.0, 1e-5, 1e-6, 0.0] + [1e-5] * 4 + [1e-6] * 4 + [-0.5] * 4], np.float32),
                         (P, 1)),
        "c_sel": sel.astype(bf16), "c_before16": before(E1), "c_before4": before(G4),
    }


def _layouts(np, i):
    def rows(w):
        w = np.asarray(w)
        return np.ascontiguousarray(w.reshape(C2, P, -1).transpose(1, 0, 2))

    def vec(v):
        return np.ascontiguousarray(np.asarray(v).reshape(C2, P).T)

    n = {k: np.asarray(v) for k, v in i.items()}
    l0, f0, l1, f1 = "L0_attn_", "L0_ffn_", "L1_attn_", "L1_ffn_"
    conv = n[l0 + "conv_w"]
    heads = np.array([4 * g + j for j in range(4) for g in range(KVH)])
    cols = (heads[:, None] * K + np.arange(K)[None, :]).reshape(-1)
    token = lambda x: np.ascontiguousarray(x.reshape(NB, TT, P, D).transpose(0, 2, 1, 3))
    full = P * (HT0 - 1)
    w1, w2 = n[f0 + "W1"], n[f0 + "W2"]
    up0 = np.concatenate([w1[:, :full], w1[:, full:], w2[:, full:], w2[:, :full]], 1)
    down0 = np.concatenate([n[f0 + "W3"].transpose(0, 2, 1), np.zeros((E0, HT0 * P - H0, D), np.float32)], 1)
    up1 = np.stack([np.concatenate([n[f1 + "gate_w"].transpose(1, 0, 2).reshape(D, E1 * H1),
                                    n[f1 + "shared_gate_w"].T], 1),
                    np.concatenate([n[f1 + "up_w"].transpose(1, 0, 2).reshape(D, E1 * H1),
                                    n[f1 + "shared_up_w"].T], 1)], 0)
    down1 = np.concatenate([n[f1 + "down_w"].reshape(E1 * H1, D), n[f1 + "shared_down_w"].T], 0)
    c = np.ascontiguousarray
    return {
        "x": token(n[l0 + "x"]),
        "c_vecs": c(np.stack([vec(v) for v in (conv[:, 0, 0], conv[:, 0, 1], conv[:, 0, 2], n[l0 + "maa_x"],
                                               n[l0 + "maa_w"], n[l0 + "maa_k"], n[l0 + "maa_v"], n[l0 + "maa_r"],
                                               n[l0 + "maa_g"], n[l0 + "gate_b"])], 1)),
        "time_decay": vec(n[l0 + "time_decay"]),
        "maa_w1": rows(n[l0 + "maa_w1"]), "maa_w2": c(n[l0 + "maa_w2"]),
        "gate_w": rows(n[l0 + "gate_w"]), "Wk": rows(n[l0 + "Wk"]), "Wv": rows(n[l0 + "Wv"]),
        "Wr": rows(n[l0 + "Wr"]), "Wg": rows(n[l0 + "Wg"]), "Wo": rows(n[l0 + "Wo"]),
        "decay_w1": rows(n[l0 + "decay_w1"]), "decay_w2": c(n[l0 + "decay_w2"]),
        "ffn_Wg": rows(n[f0 + "Wg"].T),
        "ffn_up": c(up0.reshape(E0, 2 * H0, C2, P).transpose(0, 3, 2, 1)),
        "ffn_down": c(down0.reshape(E0, HT0, P, D).transpose(0, 2, 1, 3)),
        "ln_wb": c(np.stack([vec(n[l0 + "ln_w"]), vec(n[l0 + "ln_b"])], 1)),
        "norm_w": c(np.stack([vec(n[l1 + "norm1_w"]), vec(n[l1 + "norm2_w"])], 1)),
        "g_wq": rows(n[l1 + "g_wq"][:, cols]), "g_kv_down": rows(n[l1 + "g_kv_down"]),
        "g_kv_up": c(np.concatenate([n[l1 + "g_k_up"], n[l1 + "g_v_up"]], 1)),
        "l_wqkv": rows(np.concatenate([n[l1 + "l_wq"][:, cols], n[l1 + "l_wk"], n[l1 + "l_wv"]], 1)),
        "g_wo": rows(n[l1 + "g_wo"][cols]), "l_wo": rows(n[l1 + "l_wo"][cols]),
        "router_w": rows(n[f1 + "router_w"].T), "bias_r": c(np.tile(n[f1 + "correction_bias"][None, :], (P, 1))),
        "ffn1_up": c(up1.reshape(2, C2, P, MT1 * P).transpose(2, 0, 1, 3)),
        "ffn1_down": c(down1.reshape(MT1, P, D).transpose(1, 0, 2)),
    }


def kernel(**inputs):
    import concourse.bacc as bacc
    import numpy as np
    from concourse.bass_utils import run_bass_kernel_spmd

    arrays = {**_layouts(np, inputs), **_constants(np)}
    nc = bacc.Bacc("TRN2", target_bir_lowering=False, num_devices=1)
    a = {k: nc.dram_tensor("in_" + k, v.shape, mybir.dt.from_np(v.dtype), kind="ExternalInput").ap()
         for k, v in arrays.items()}
    out = nc.dram_tensor("out", (NB, P, TT, D), F32, kind="ExternalOutput").ap()
    build(nc, a, out)
    r = run_bass_kernel_spmd(nc, [{"in_" + k: v for k, v in arrays.items()}], core_ids=[0])
    got = r.results[0]["out"]
    return np.ascontiguousarray(got.transpose(0, 2, 1, 3)).reshape(NB, T, D)
```
